# Optimizing a Trainium2 kernel written in Bass

```python
import numpy as np
import jax
import jax.numpy as jnp

def _softmax(x, axis=-1):
    return jax.nn.softmax(x, axis=axis)

def _gelu(x):
    return jax.nn.gelu(x, approximate=True)

def _silu(x):
    return jax.nn.silu(x)

def _sigmoid(x):
    return jax.nn.sigmoid(x)

def _layernorm(x, axis=-1, eps=1e-05):
    m = jnp.mean(x, axis=axis, keepdims=True)
    v = jnp.var(x, axis=axis, keepdims=True)
    return (x - m) / jnp.sqrt(v + eps)

def _scatter_add(tgt, idx, src, axis=0):
    return tgt.at[idx].add(src)

def _segment_sum(src, seg, n):
    return jax.ops.segment_sum(src, seg, n)
kernel_name = 'mk_adaln_ffn_d2_seqx_r8_e99af2'

def setup_inputs(seed: int=0):
    np.random.seed(seed)
    _w = jnp.asarray

    def _rec_inputs():
        import jax
        import jax.numpy as jnp
        _rk = jax.random.key(seed)
        x = -7.109e-05 + 0.9999 * jax.random.normal(jax.random.fold_in(_rk, 1), (64, 32, 512), jnp.float32)
        _lenS = 32 - jax.random.randint(jax.random.fold_in(_rk, 7), (64,), 0, max(1, 32 // 4) + 1, jnp.int32)
        _lenS2 = 32 - jax.random.randint(jax.random.fold_in(_rk, 8), (64,), 0, max(1, 32 // 4) + 1, jnp.int32)
        itok_B_4_50 = jax.random.randint(jax.random.fold_in(_rk, 11), (64,), 4, 51, jnp.int32)
        itok_Bx16_0_63 = jax.random.randint(jax.random.fold_in(_rk, 12), (64, 16), 0, 64, jnp.int32)
        itok_B_207_1644 = jax.random.randint(jax.random.fold_in(_rk, 13), (64,), 207, 1645, jnp.int32)
        return (x, itok_B_4_50, itok_Bx16_0_63, itok_B_207_1644)
    x, itok_B_4_50, itok_Bx16_0_63, itok_B_207_1644 = _rec_inputs()

    def _L0_cond_setup():
        import jax, jax.numpy as jnp
        import numpy as np
        RANK = 16
        ALPHA = 16.0
        SCALING = ALPHA / RANK
        key = jax.random.key(seed)
        k1, k2, k3, k4 = jax.random.split(key, 4)
        batch, n_tok, d_in, d_out, n_adapters, rank = (8, 256, 512, 512, 64, RANK)
        x = jax.random.normal(k1, (batch, n_tok, d_in), dtype=jnp.float32)
        A = jax.random.normal(k2, (n_adapters, d_out, rank), dtype=jnp.float32) * 0.02
        B = jax.random.normal(k3, (n_adapters, rank, d_in), dtype=jnp.float32)
        adapter_ids = jax.random.randint(k4, (batch,), 0, n_adapters, dtype=jnp.int32)
        return {'x': x, 'A': A, 'B': B, 'adapter_ids': adapter_ids}
    _L0_cond_all = _L0_cond_setup()
    _L0_cond_in = {k: v for k, v in _L0_cond_all.items() if k in ('A', 'B')}
    del _L0_cond_all

    def _L0_ffn_setup():
        import jax, jax.numpy as jnp
        import numpy as np
        BLK = 16
        FP8_MAX = 448.0
        GSCALE_DIV = 448.0 * 6.0
        SELECT = 128

        def _ste(x, q):
            return x + jax.lax.stop_gradient(q - x)

        def _fp8_block_qdq(v):
            lead, C = (v.shape[:-1], v.shape[-1])
            vb = v.reshape(*lead, C // BLK, BLK)
            s = jnp.maximum(jnp.max(jnp.abs(vb), axis=-1, keepdims=True) / FP8_MAX, 1e-08)
            q = (vb / s).astype(jnp.float8_e4m3fn).astype(jnp.float32) * s
            return _ste(vb, q).reshape(*lead, C)

        def _int4_block_qdq(w):
            out, C = w.shape
            wb = w.reshape(out, C // BLK, BLK)
            s = jnp.maximum(jnp.max(jnp.abs(wb), axis=-1, keepdims=True) / 7.0, 1e-08)
            q = jnp.round(jnp.clip(wb / s, -8.0, 7.0)) * s
            return _ste(wb, q).reshape(out, C)

        def _quant_act(x2d, reorder_index, select_num):
            g = jnp.maximum(jnp.max(jnp.abs(x2d)) / GSCALE_DIV, 1e-08)
            xr = (x2d / g)[:, reorder_index]
            n = xr.shape[1] - select_num
            normal = _fp8_block_qdq(xr[:, :n])
            outl = xr[:, n:]
            q1 = _fp8_block_qdq(outl)
            q2 = _fp8_block_qdq(outl - q1)
            A = jnp.concatenate([normal, q1, q2], axis=1)
            return (A, g)

        def _quant_w(w, reorder_index, select_num):
            wr = w[:, reorder_index]
            n = wr.shape[1] - select_num
            wq = jnp.concatenate([wr[:, :n], wr[:, n:], wr[:, n:]], axis=1)
            return _int4_block_qdq(wq)
        key = jax.random.key(seed)
        k0, k1, k2, k3 = jax.random.split(key, 4)
        B, L, H, I = (2, 256, 512, 1376)
        return {'x': jax.random.normal(k0, (B, L, H), dtype=jnp.float32), 'w_gate': jax.random.normal(k1, (I, H), dtype=jnp.float32) * 0.02, 'w_up': jax.random.normal(k2, (I, H), dtype=jnp.float32) * 0.02, 'w_down': jax.random.normal(k3, (H, I), dtype=jnp.float32) * 0.02, 'ri_in': jnp.arange(H, dtype=jnp.int32), 'ri_mid': jnp.arange(I, dtype=jnp.int32)}
    _L0_ffn_all = _L0_ffn_setup()
    _L0_ffn_in = {k: v for k, v in _L0_ffn_all.items() if k in ('w_gate', 'w_up', 'w_down', 'ri_in', 'ri_mid')}
    del _L0_ffn_all

    def _L1_cond_setup():
        import jax, jax.numpy as jnp
        import numpy as np
        B, S, HID = (4, 128, 512)
        D, HQ, HK = (128, 32, 8)
        PAGES, PSIZE, NPP = (64, 32, 16)
        THETA = 10000.0
        EPS = 1e-06
        SCALE = 1.0 / float(np.sqrt(D))

        def _rmsnorm(t, w):
            var = jnp.mean(t * t, axis=-1, keepdims=True)
            return t * jax.lax.rsqrt(var + EPS) * w

        def _rope(t, pos):
            inv_freq = 1.0 / THETA ** (jnp.arange(0, D, 2, dtype=jnp.float32) / D)
            freqs = pos[..., None].astype(jnp.float32) * inv_freq
            cos = jnp.cos(freqs)[:, :, None, :]
            sin = jnp.sin(freqs)[:, :, None, :]
            t1, t2 = (t[..., :D // 2], t[..., D // 2:])
            return jnp.concatenate([t1 * cos - t2 * sin, t2 * cos + t1 * sin], axis=-1)
        key = jax.random.key(seed)
        ks = jax.random.split(key, 10)
        x = jax.random.normal(ks[0], (B, S, HID), jnp.float32)
        Wq = jax.random.normal(ks[1], (HQ * D, HID), jnp.float32) * 0.02
        Wk = jax.random.normal(ks[2], (HK * D, HID), jnp.float32) * 0.02
        Wv = jax.random.normal(ks[3], (HK * D, HID), jnp.float32) * 0.02
        Wo = jax.random.normal(ks[4], (HID, HQ * D), jnp.float32) * 0.02
        q_norm_w = jax.random.uniform(ks[5], (D,), jnp.float32)
        k_norm_w = jax.random.uniform(ks[6], (D,), jnp.float32)
        k_cache = jax.random.normal(ks[7], (PAGES, PSIZE, HK, D), jnp.float32)
        v_cache = jax.random.normal(ks[8], (PAGES, PSIZE, HK, D), jnp.float32)
        block_table = jnp.arange(B * NPP, dtype=jnp.int32).reshape(B, NPP)
        cache_seqlens = jax.random.randint(ks[9], (B,), 0, 475).astype(jnp.int32)
        return dict(x=x, Wq=Wq, Wk=Wk, Wv=Wv, Wo=Wo, q_norm_w=q_norm_w, k_norm_w=k_norm_w, k_cache=k_cache, v_cache=v_cache, block_table=block_table, cache_seqlens=cache_seqlens)
    _L1_cond_all = _L1_cond_setup()
    _L1_cond_in = {k: v for k, v in _L1_cond_all.items() if k in ('Wq', 'Wk', 'Wv', 'Wo', 'q_norm_w', 'k_norm_w', 'k_cache', 'v_cache')}
    del _L1_cond_all

    def _L1_ffn_setup():
        import jax, jax.numpy as jnp
        import numpy as np
        RANKS = (8, 16, 32, 64)
        TOPK = 1
        SCALING = 1.0 / 4
        key = jax.random.key(seed)
        ks = jax.random.split(key, 7)
        D_IN, D_OUT, MAX_R, N_RANKS = (512, 512, 64, len(RANKS))
        B_, S_ = (4, 256)
        return {'hidden_states': jax.random.normal(ks[0], (B_, S_, D_IN), jnp.float32), 'W': jax.random.normal(ks[1], (D_OUT, D_IN), jnp.float32) * 0.02, 'b': jax.random.normal(ks[2], (D_OUT,), jnp.float32) * 0.02, 'A': jax.random.normal(ks[3], (MAX_R, D_IN), jnp.float32) * 0.02, 'B': jnp.zeros((D_OUT, MAX_R), jnp.float32) + jax.random.normal(ks[4], (D_OUT, MAX_R), jnp.float32) * 0.02, 'gate_w': jax.random.normal(ks[5], (N_RANKS, D_IN), jnp.float32) * 0.02, 'gate_b': jax.random.normal(ks[6], (N_RANKS,), jnp.float32) * 0.02}
    _L1_ffn_all = _L1_ffn_setup()
    _L1_ffn_in = {k: v for k, v in _L1_ffn_all.items() if k in ('W', 'b', 'A', 'B', 'gate_w', 'gate_b')}
    del _L1_ffn_all
    return {'x': x, 'itok_B_4_50': itok_B_4_50, 'itok_Bx16_0_63': itok_Bx16_0_63, 'itok_B_207_1644': itok_B_207_1644, 'L0_cond_A': _L0_cond_in['A'], 'L0_cond_B': _L0_cond_in['B'], 'L0_ffn_w_gate': _L0_ffn_in['w_gate'], 'L0_ffn_w_up': _L0_ffn_in['w_up'], 'L0_ffn_w_down': _L0_ffn_in['w_down'], 'L0_ffn_ri_in': _L0_ffn_in['ri_in'], 'L0_ffn_ri_mid': _L0_ffn_in['ri_mid'], 'L1_cond_Wq': _L1_cond_in['Wq'], 'L1_cond_Wk': _L1_cond_in['Wk'], 'L1_cond_Wv': _L1_cond_in['Wv'], 'L1_cond_Wo': _L1_cond_in['Wo'], 'L1_cond_q_norm_w': _L1_cond_in['q_norm_w'], 'L1_cond_k_norm_w': _L1_cond_in['k_norm_w'], 'L1_cond_k_cache': _L1_cond_in['k_cache'], 'L1_cond_v_cache': _L1_cond_in['v_cache'], 'L1_ffn_W': _L1_ffn_in['W'], 'L1_ffn_b': _L1_ffn_in['b'], 'L1_ffn_A': _L1_ffn_in['A'], 'L1_ffn_B': _L1_ffn_in['B'], 'L1_ffn_gate_w': _L1_ffn_in['gate_w'], 'L1_ffn_gate_b': _L1_ffn_in['gate_b']}

def reference(x, itok_B_4_50, itok_Bx16_0_63, itok_B_207_1644, L0_cond_A, L0_cond_B, L0_ffn_w_gate, L0_ffn_w_up, L0_ffn_w_down, L0_ffn_ri_in, L0_ffn_ri_mid, L1_cond_Wq, L1_cond_Wk, L1_cond_Wv, L1_cond_Wo, L1_cond_q_norm_w, L1_cond_k_norm_w, L1_cond_k_cache, L1_cond_v_cache, L1_ffn_W, L1_ffn_b, L1_ffn_A, L1_ffn_B, L1_ffn_gate_w, L1_ffn_gate_b):
    import jax
    import jax.numpy as jnp

    def _L0_cond_ref(x, A, B, adapter_ids):
        import jax, jax.numpy as jnp
        import numpy as np
        RANK = 16
        ALPHA = 16.0
        SCALING = ALPHA / RANK
        B_req = B[adapter_ids]
        A_req = A[adapter_ids]
        Bx = jnp.einsum('bni,bri->bnr', x, B_req)
        out = jnp.einsum('bnr,bor->bno', Bx, A_req)
        return out * SCALING

    def _L0_ffn_ref(x, w_gate, w_up, w_down, ri_in, ri_mid):
        import jax, jax.numpy as jnp
        import numpy as np
        BLK = 16
        FP8_MAX = 448.0
        GSCALE_DIV = 448.0 * 6.0
        SELECT = 128

        def _ste(x, q):
            return x + jax.lax.stop_gradient(q - x)

        def _fp8_block_qdq(v):
            lead, C = (v.shape[:-1], v.shape[-1])
            vb = v.reshape(*lead, C // BLK, BLK)
            s = jnp.maximum(jnp.max(jnp.abs(vb), axis=-1, keepdims=True) / FP8_MAX, 1e-08)
            q = (vb / s).astype(jnp.float8_e4m3fn).astype(jnp.float32) * s
            return _ste(vb, q).reshape(*lead, C)

        def _int4_block_qdq(w):
            out, C = w.shape
            wb = w.reshape(out, C // BLK, BLK)
            s = jnp.maximum(jnp.max(jnp.abs(wb), axis=-1, keepdims=True) / 7.0, 1e-08)
            q = jnp.round(jnp.clip(wb / s, -8.0, 7.0)) * s
            return _ste(wb, q).reshape(out, C)

        def _quant_act(x2d, reorder_index, select_num):
            g = jnp.maximum(jnp.max(jnp.abs(x2d)) / GSCALE_DIV, 1e-08)
            xr = (x2d / g)[:, reorder_index]
            n = xr.shape[1] - select_num
            normal = _fp8_block_qdq(xr[:, :n])
            outl = xr[:, n:]
            q1 = _fp8_block_qdq(outl)
            q2 = _fp8_block_qdq(outl - q1)
            A = jnp.concatenate([normal, q1, q2], axis=1)
            return (A, g)

        def _quant_w(w, reorder_index, select_num):
            wr = w[:, reorder_index]
            n = wr.shape[1] - select_num
            wq = jnp.concatenate([wr[:, :n], wr[:, n:], wr[:, n:]], axis=1)
            return _int4_block_qdq(wq)
        B, L, H = x.shape
        x2 = x.reshape(B * L, H)
        A, g = _quant_act(x2, ri_in, SELECT)
        Wg = _quant_w(w_gate, ri_in, SELECT)
        Wu = _quant_w(w_up, ri_in, SELECT)
        gate = A @ Wg.T * g
        up = A @ Wu.T * g
        h = jax.nn.silu(gate) * up
        Am, gm = _quant_act(h, ri_mid, SELECT)
        Wd = _quant_w(w_down, ri_mid, SELECT)
        y = Am @ Wd.T * gm
        return y.reshape(B, L, -1)

    def _L1_cond_ref(x, Wq, Wk, Wv, Wo, q_norm_w, k_norm_w, k_cache, v_cache, block_table, cache_seqlens):
        import jax, jax.numpy as jnp
        import numpy as np
        B, S, HID = (4, 128, 512)
        D, HQ, HK = (128, 32, 8)
        PAGES, PSIZE, NPP = (64, 32, 16)
        THETA = 10000.0
        EPS = 1e-06
        SCALE = 1.0 / float(np.sqrt(D))

        def _rmsnorm(t, w):
            var = jnp.mean(t * t, axis=-1, keepdims=True)
            return t * jax.lax.rsqrt(var + EPS) * w

        def _rope(t, pos):
            inv_freq = 1.0 / THETA ** (jnp.arange(0, D, 2, dtype=jnp.float32) / D)
            freqs = pos[..., None].astype(jnp.float32) * inv_freq
            cos = jnp.cos(freqs)[:, :, None, :]
            sin = jnp.sin(freqs)[:, :, None, :]
            t1, t2 = (t[..., :D // 2], t[..., D // 2:])
            return jnp.concatenate([t1 * cos - t2 * sin, t2 * cos + t1 * sin], axis=-1)
        bsz, seqlen, _ = x.shape
        q = jnp.einsum('bsd,ed->bse', x, Wq).reshape(bsz, seqlen, HQ, D)
        k = jnp.einsum('bsd,ed->bse', x, Wk).reshape(bsz, seqlen, HK, D)
        v = jnp.einsum('bsd,ed->bse', x, Wv).reshape(bsz, seqlen, HK, D)
        q = _rmsnorm(q, q_norm_w)
        k = _rmsnorm(k, k_norm_w)
        pos = cache_seqlens[:, None] + jnp.arange(seqlen)[None, :]
        q = _rope(q, pos)
        k = _rope(k, pos)
        L = NPP * PSIZE
        kc = k_cache[block_table].reshape(bsz, L, HK, D)
        vc = v_cache[block_table].reshape(bsz, L, HK, D)
        k_all = jnp.concatenate([kc, k], axis=1)
        v_all = jnp.concatenate([vc, v], axis=1)
        valid_c = jnp.arange(L)[None, :] < cache_seqlens[:, None]
        valid = jnp.concatenate([valid_c, jnp.ones((bsz, seqlen), dtype=bool)], axis=1)
        rep = HQ // HK
        k_all = jnp.repeat(k_all, rep, axis=2)
        v_all = jnp.repeat(v_all, rep, axis=2)
        scores = jnp.einsum('bqhd,bkhd->bhqk', q, k_all) * SCALE
        scores = jnp.where(valid[:, None, None, :], scores, -1e+30)
        probs = jax.nn.softmax(scores, axis=-1)
        o = jnp.einsum('bhqk,bkhd->bqhd', probs, v_all)
        o = o.reshape(bsz, seqlen, HQ * D)
        return jnp.einsum('bse,de->bsd', o, Wo)

    def _L1_ffn_ref(hidden_states, W, b, A, B, gate_w, gate_b):
        import jax, jax.numpy as jnp
        import numpy as np
        RANKS = (8, 16, 32, 64)
        TOPK = 1
        SCALING = 1.0 / 4
        bsz, seq, d_in = hidden_states.shape
        out = jnp.einsum('bsd,od->bso', hidden_states, W) + b
        x = hidden_states.reshape(-1, d_in)
        scores = x @ gate_w.T + gate_b
        probs = jax.nn.softmax(scores, axis=-1)
        routing_weights, selected = jax.lax.top_k(probs, TOPK)
        routing_weights = routing_weights / jnp.sum(routing_weights, axis=-1, keepdims=True)
        lora_outputs = jnp.stack([x @ A[:r, :].T @ B[:, :r].T for r in RANKS], axis=1)
        sel = jnp.take_along_axis(lora_outputs, selected[:, :, None], axis=1)
        final = jnp.sum(sel * routing_weights[:, :, None], axis=1)
        return out + final.reshape(bsz, seq, -1)
    x = x + _L0_ffn_ref(_L0_cond_ref(x, L0_cond_A, L0_cond_B, itok_B_4_50), L0_ffn_w_gate, L0_ffn_w_up, L0_ffn_w_down, L0_ffn_ri_in, L0_ffn_ri_mid)
    x = x + _L1_ffn_ref(_L1_cond_ref(x, L1_cond_Wq, L1_cond_Wk, L1_cond_Wv, L1_cond_Wo, L1_cond_q_norm_w, L1_cond_k_norm_w, L1_cond_k_cache, L1_cond_v_cache, itok_Bx16_0_63, itok_B_207_1644), L1_ffn_W, L1_ffn_b, L1_ffn_A, L1_ffn_B, L1_ffn_gate_w, L1_ffn_gate_b)
    return x

_drawn_inputs = setup_inputs


def setup_inputs(seed=0):
    import zlib

    import numpy as np

    out = dict(_drawn_inputs(seed))
    spreads = {}
    factors = {'L1_cond_Wq': 3.275,
     'L1_cond_Wk': 8.0,
     'L1_cond_Wv': 8.0,
     'L1_cond_q_norm_w': 5.667,
     'L1_cond_k_norm_w': 8.0,
     'L1_cond_k_cache': 3.279,
     'L1_ffn_b': 23.848,
     'L1_ffn_A': 8.0,
     'L1_ffn_B': 8.0,
     'L1_ffn_gate_w': 8.0,
     'L1_ffn_gate_b': 8.0}
    for name, (base, spread) in spreads.items():
        noise = np.random.default_rng([zlib.crc32(name.encode()), seed]).standard_normal(out[name].shape)
        drawn = base * np.exp(spread * noise) if base else spread * noise
        out[name] = jnp.asarray(drawn.astype(out[name].dtype))
    for name, factor in factors.items():
        out[name] = (out[name] * factor).astype(out[name].dtype)
    return out
```

```python
from contextlib import ExitStack

import concourse.bass as bass
from concourse import mybir

F32 = mybir.dt.float32
I32 = mybir.dt.int32
U32 = mybir.dt.uint32
ALU = mybir.AluOpType
ACT = mybir.ActivationFunctionType
AX_X = mybir.AxisListType.X
RMAX = bass.bass_isa.ReduceOp.max

P = 128
B, S, H = 64, 32, 512
TOK = B * S
NT = TOK // P
BT = P // S
RANK = 16
IDS = 64
I_DIM = 1376
KH = H // P
CHUNKS_OF_X = (2, 3, 0, 1)
KI = (I_DIM + P - 1) // P
BLK = 16
SELECT = 128
HQ, HK, D = 32, 8, 128
REP = HQ // HK
PAGES, PSIZE, NPP = 64, 32, 16
LC = NPP * PSIZE
KC = LC // P
NKEY = LC + S
EPS = 1e-6
SCALE = D ** -0.5
FP8_MAX = 448.0
GDIV = 448.0 * 6.0
MAGIC_INT = 1.5 * 2.0 ** 23
FP8_TO_C = 1.5 * 2.0 ** 20
FP8_MIN_NORMAL = 2.0 ** -6
EXPONENT = 0x7F800000
LMAX = 64
NROUTE = 4
RANKS = (8, 16, 32, 64)
PIECES = [(0, 352), (352, 352), (704, 352), (1056, 320)]


def width(k):
    return min(P, I_DIM - k * P)


class Link:

    def __init__(self, eng, sem, base=0):
        self.eng, self.sem, self.base, self.n = eng, sem, base, 0

    def __call__(self, ins):
        self.n += 1
        ins.then_inc(self.sem, 1)
        self.eng.wait_ge(self.sem, self.base + self.n)


def hold(eng, passed):
    eng.sem_inc(passed, 1)


def blocks(ap):
    return ap.rearrange("p (b e) -> p b e", e=BLK)


def per_block(ap, nb):
    return ap.unsqueeze(2).to_broadcast([P, nb, BLK])


def seventh(nc, link, out, a, q, t):
    link(nc.vector.tensor_scalar(q, a, 1.0 / 7.0, None, ALU.mult))
    link(nc.vector.scalar_tensor_tensor(t, q, -8.0, a, ALU.mult, ALU.add))
    link(nc.vector.tensor_tensor(t, t, q, ALU.add))
    link(nc.vector.scalar_tensor_tensor(out, t, 1.0 / 7.0, q, ALU.mult, ALU.add))


def fp8_scales(nc, link, s, rs, t):
    seventh(nc, link, s, s, rs, t)
    link(nc.vector.tensor_scalar(s, s, 7.0 / FP8_MAX, 1e-8, ALU.mult, ALU.max))
    link(nc.vector.reciprocal(rs, s))


def fp8_round(nc, link, v, c):
    link(nc.vector.tensor_scalar(c.bitcast(I32), v.bitcast(I32), EXPONENT, None, ALU.bitwise_and))
    link(nc.vector.tensor_scalar(c, c, FP8_MIN_NORMAL, FP8_TO_C, ALU.max, ALU.mult))
    link(nc.vector.tensor_tensor(v, v, c, ALU.add))
    link(nc.vector.tensor_tensor(v, v, c, ALU.subtract))


def fp8_quantise(nc, link, x, rg, s, rs, out, v, c, s2, rs2, t2, r, n, out_gate):
    nb, no = n // BLK, SELECT // BLK
    link(nc.vector.scalar_tensor_tensor(blocks(v), blocks(x), rg, per_block(rs, nb), ALU.mult, ALU.mult))
    fp8_round(nc, link, v, c)
    if out_gate is not None:
        out_gate()
    link(nc.vector.tensor_tensor(blocks(out), blocks(v), per_block(s, nb), ALU.mult))
    tail, v, c = out[:, n - SELECT:n], v[:, 0:SELECT], c[:, 0:SELECT]
    link(nc.vector.scalar_tensor_tensor(r, x[:, n - SELECT:n], rg, tail, ALU.mult, ALU.subtract))
    link(nc.vector.tensor_reduce(s2, blocks(r), AX_X, ALU.max, apply_absolute_value=True))
    fp8_scales(nc, link, s2, rs2, t2)
    link(nc.vector.tensor_tensor(blocks(v), blocks(r), per_block(rs2, no), ALU.mult))
    fp8_round(nc, link, v, c)
    link(nc.vector.tensor_tensor(blocks(r), blocks(v), per_block(s2, no), ALU.mult))
    return nc.vector.tensor_tensor(tail, tail, r, ALU.add)


FP8_LINKS = (1 + 4 + 1) + (2 + 6) + (1 + 4 + 1)


def int4_quantise(nc, link, w, v, am, s, rs, out, nb):
    link(nc.vector.tensor_reduce(am, blocks(w), AX_X, ALU.max, apply_absolute_value=True))
    seventh(nc, link, am, am, rs, s)
    link(nc.vector.tensor_scalar(s, am, 1e-8, None, ALU.max))
    link(nc.vector.reciprocal(rs, s))
    m = w.shape[0]
    wide = lambda a: a.unsqueeze(2).to_broadcast([m, nb, BLK])
    link(nc.vector.tensor_tensor(blocks(v), blocks(w), wide(rs), ALU.mult))
    link(nc.vector.tensor_scalar(v, v, MAGIC_INT, MAGIC_INT, ALU.add, ALU.subtract))
    return nc.vector.tensor_tensor(blocks(out), blocks(v), wide(s), ALU.mult)


def condition(nc, K, I, sem):
    GB = 8
    NG = B // GB
    with ExitStack() as ctx:
        sb = lambda n, s, d=F32: ctx.enter_context(nc.sbuf_tensor(n, s, d))
        ps = lambda n, s: ctx.enter_context(nc.psum_tensor(n, s, F32))
        xT = sb("xT", [P, KH, TOK])
        a_gath = sb("a_gath", [P, KH, IDS * RANK])
        a_rows = sb("a_rows", [P, 2, H])
        ids = sb("ids", [P, NG, GB], I32)
        idf = sb("idf", [P, NG, GB])
        rowf = sb("rowf", [P, NG])
        row = sb("row", [P, NG], U32)
        ri = sb("ri", [P, KH], I32)
        tmp = sb("c_tmp", [P, NT * H // BLK])
        a_sel = sb("a_sel", [P, 2, H])
        b_sel = sb("b_sel", [P, 2, H])
        bT = sb("bT", [P, 2, KH * P])
        bx = sb("bx", [P, 2, 2 * P])
        mine = sb("mine", [P, 2 * P])
        rank_of = sb("rank_of", [P, 1])
        eight = sb("eight", [P, GB])
        t_ps = ps("t_ps", [P, 2, H])
        bT_ps = ps("bT_ps", [P, 2, H])
        bx_ps = ps("bx_ps", [P, 2, H])
        x2_ps = ps("x2_ps", [P, 2, H])

        def amax(dve, g):
            for n in (2 * g, 2 * g + 1):
                dve.wait_ge(sem("c_x2s"), n + 1)
                nc.vector.tensor_reduce(K["xmax"][:, n, :], blocks(K["x2"][:, n, :]), AX_X, ALU.max,
                                    apply_absolute_value=True).then_inc(sem("c_amax"), 1)

        with nc.Block() as block:
            @block.sync
            def _(sp):
                sp.dma_start(K["ident"][:, :], I["ident"]).then_inc(sem("c_const"), 16)
                sp.dma_start(mine[:, :], I["mine"]).then_inc(sem("c_const"), 16)
                sp.dma_start(rank_of[:, :], I["rank_of"]).then_inc(sem("c_const"), 16)
                sp.dma_start(eight[:, :], I["eight"]).then_inc(sem("c_const"), 16)
                sp.dma_start(ids[:, :, :], I["ids"].partition_broadcast(P).rearrange(
                    "p (g b) -> p g b", b=GB)).then_inc(sem("c_const"), 16)
                sp.dma_start(ri[:, :], I["ri_in"]).then_inc(sem("c_ri"), 16)
                sp.dma_start(xT[:, :, :], I["xT"].rearrange("(c p) t -> p c t", p=P)).then_inc(sem("c_x"), 16)
                for j in range(8):
                    sp.wait_ge(sem("c_arow"), j + 1)
                    sp.dma_start(I["a_scratch"][j * P:(j + 1) * P, :], a_rows[:, j % 2, :]).then_inc(
                        sem(f"c_astore{j % 2}"), 16)

            @block.gpsimd
            def _(pool):
                pool.wait_ge(sem("c_ri"), 16)
                for c in range(KH):
                    nc.gpsimd.indirect_dma_start(
                        a_gath[:, c, :], None, I["A_o"],
                        bass.IndirectOffsetOnAxis(ap=ri[:, c:c + 1], axis=0)).then_inc(sem("c_agath"), 16)
                pool.wait_ge(sem("c_row"), 1)
                pool.wait_ge(sem("c_astore0"), 64)
                pool.wait_ge(sem("c_astore1"), 64)
                for g in range(NG):
                    if g >= 2:
                        pool.wait_ge(sem("c_bT"), g - 1)
                        pool.wait_ge(sem("c_x2"), 2 * (g - 1))
                    off = bass.IndirectOffsetOnAxis(ap=row[:, g:g + 1], axis=0)
                    nc.gpsimd.indirect_dma_start(b_sel[:, g % 2, :], None, I["B_r"], off).then_inc(
                        sem(f"c_bsel{g % 2}"), 16)
                    nc.gpsimd.indirect_dma_start(a_sel[:, g % 2, :], None, I["a_scratch"], off).then_inc(
                        sem(f"c_asel{g % 2}"), 16)
                pool.wait_ge(sem("c_gmax"), 1)
                nc.gpsimd.partition_all_reduce(K["gall"][:, :], K["gpart"][:, :], P, RMAX).then_inc(
                    sem("c_gall"), 1)

            @block.tensor
            def _(pe):
                pe.wait_ge(sem("c_const"), 80)
                pe.wait_ge(sem("c_agath"), 64)
                for j in range(8):
                    if j >= 2:
                        pe.wait_ge(sem("c_arow"), j - 1)
                    for c in range(KH):
                        last = nc.tensor.transpose(t_ps[:, j % 2, c * P:(c + 1) * P],
                                                   a_gath[:, c, j * P:(j + 1) * P], K["ident"][:, :])
                    last.then_inc(sem("c_aT"), 1)
                pe.wait_ge(sem("c_x"), 16)
                for g in range(NG):
                    pe.wait_ge(sem(f"c_bsel{g % 2}"), 16 * (g // 2 + 1))
                    if g >= 2:
                        pe.wait_ge(sem("c_bTs"), g - 1)
                    for c in range(KH):
                        last = nc.tensor.transpose(bT_ps[:, g % 2, c * P:(c + 1) * P],
                                                   b_sel[:, g % 2, c * P:(c + 1) * P], K["ident"][:, :])
                    last.then_inc(sem("c_bT"), 1)
                    pe.wait_ge(sem("c_bTs"), g + 1)
                    for c in CHUNKS_OF_X:
                        last = nc.tensor.matmul(bx_ps[:, g % 2, 0:2 * P], bT[:, g % 2, c * P:(c + 1) * P],
                                                xT[:, c, g * 2 * P:(g + 1) * 2 * P],
                                                start=(c == CHUNKS_OF_X[0]), stop=(c == CHUNKS_OF_X[-1]))
                    last.then_inc(sem("c_bx"), 1)
                    pe.wait_ge(sem("c_bxs"), g + 1)
                    pe.wait_ge(sem(f"c_asel{g % 2}"), 16 * (g // 2 + 1))
                    for h in range(2):
                        n = 2 * g + h
                        if n >= 2:
                            pe.wait_ge(sem("c_x2s"), n - 1)
                        nc.tensor.matmul(x2_ps[:, h, :], bx[:, g % 2, h * P:(h + 1) * P],
                                         a_sel[:, g % 2, :], start=True, stop=True).then_inc(sem("c_x2"), 1)

            @block.scalar
            def _(act):
                for j in range(8):
                    act.wait_ge(sem("c_aT"), j + 1)
                    if j >= 2:
                        act.wait_ge(sem(f"c_astore{j % 2}"), 16 * (j // 2))
                    nc.scalar.copy(a_rows[:, j % 2, :], t_ps[:, j % 2, :]).then_inc(sem("c_arow"), 1)
                for g in range(NG):
                    act.wait_ge(sem("c_bT"), g + 1)
                    if g >= 2:
                        act.wait_ge(sem("c_bx"), g - 1)
                    nc.scalar.copy(bT[:, g % 2, :], bT_ps[:, g % 2, :]).then_inc(sem("c_bTs"), 1)
                    for h in range(2):
                        n = 2 * g + h
                        act.wait_ge(sem("c_x2"), n + 1)
                        nc.scalar.copy(K["x2"][:, n, :], x2_ps[:, h, :]).then_inc(sem("c_x2s"), 1)

            @block.vector
            def _(dve):
                link = Link(dve, sem("c_link"))
                dve.wait_ge(sem("c_const"), 80)
                link(nc.vector.tensor_copy(idf[:, :, :], ids[:, :, :]))
                link(nc.vector.tensor_tensor(idf[:, :, :], idf[:, :, :],
                                             eight[:, :].unsqueeze(1).to_broadcast([P, NG, GB]), ALU.mult))
                link(nc.vector.tensor_reduce(rowf[:, :], idf[:, :, :], AX_X, ALU.add))
                link(nc.vector.tensor_scalar(rowf[:, :], rowf[:, :], float(RANK), rank_of[:, 0:1],
                                             ALU.mult, ALU.add))
                nc.vector.tensor_copy(row[:, :], rowf[:, :]).then_inc(sem("c_row"), 1)
                for g in range(NG):
                    dve.wait_ge(sem("c_bx"), g + 1)
                    if g >= 2:
                        dve.wait_ge(sem("c_x2"), 2 * (g - 1))
                    nc.vector.tensor_tensor(bx[:, g % 2, :], bx_ps[:, g % 2, 0:2 * P], mine[:, :],
                                            ALU.mult).then_inc(sem("c_bxs"), 1)
                    if g:
                        amax(dve, g - 1)
                amax(dve, NG - 1)
                dve.wait_ge(sem("c_amax"), NT)
                link(nc.vector.tensor_reduce(K["gpart"][:, :],
                                             K["xmax"][:, :, :].rearrange("p t b -> p (t b)"), AX_X, ALU.max))
                nc.vector.tensor_copy(K["gall"][:, :], K["gpart"][:, :]).then_inc(sem("c_gmax"), 1)
                dve.wait_ge(sem("c_gall"), 1)
                global_scale(nc, link, K["gall"][:, :], K["xg"][:, :], K["xrg"][:, 0:1],
                             K["xmax"][:, :, :].rearrange("p t b -> p (t b)"),
                             K["xrs"][:, :, :].rearrange("p t b -> p (t b)"), tmp[:, :])
                link(nc.vector.tensor_scalar(K["half_g"][:, :], K["xg"][:, :], 0.5, None, ALU.mult))
                link(nc.vector.tensor_tensor(K["half_gg"][:, :], K["half_g"][:, :], K["xg"][:, :], ALU.mult))



def global_scale(nc, link, gall, g, rg, amax, rs, t):
    link(nc.vector.tensor_scalar(g, gall, 1.0 / GDIV, 1e-8, ALU.mult, ALU.max))
    link(nc.vector.reciprocal(rg, g))
    link(nc.vector.tensor_scalar(amax, amax, rg, None, ALU.mult))
    fp8_scales(nc, link, amax, rs, t)


def weights(nc, K, I, sem):
    with ExitStack() as ctx:
        sb = lambda n, s, d=F32: ctx.enter_context(nc.sbuf_tensor(n, s, d))
        ps = lambda n, s: ctx.enter_context(nc.psum_tensor(n, s, F32))
        taken = [0]

        def spare(*shape):
            n, a = 1, taken[0]
            for d in shape:
                n *= d
            taken[0] += n
            flat = K["h"][:, :, :].rearrange("p t n -> p (t n)")[:, a:a + n]
            names = "abc"[:len(shape)]
            sizes = dict(zip(names[1:], shape[1:]))
            return flat.rearrange(f"p ({' '.join(names)}) -> p {' '.join(names)}", **sizes)

        guT = spare(2, KH, I_DIM)
        dT = spare(KI, H)
        ri = sb("w_ri", [P, KH], I32)
        rm = sb("w_rm", [P, KI], I32)
        nat = spare(2, H)
        wi = spare(2, H)
        wq = spare(2, H)
        v = spare(1, I_DIM)[:, 0, :]
        am = sb("w_am", [P, I_DIM // BLK])
        s_ = sb("w_s", [P, I_DIM // BLK])
        rs = sb("w_rs", [P, I_DIM // BLK])
        dn = sb("dn", [P, I_DIM])
        dq = sb("dq", [P, I_DIM])
        a_ps = ps("a_ps", [P, 2, H])
        b_ps = ps("b_ps", [P, 2, H])
        d_ps = ps("d_ps", [P, 3 * H])
        tiles = [(m, k) for m in range(2) for k in range(KI)]
        NW = len(tiles)

        with nc.Block() as block:
            @block.sync
            def _(sp):
                sp.dma_start(ri[:, :], I["ri_in"]).then_inc(sem("w_idx"), 16)
                sp.dma_start(rm[:, 0:KI - 1], I["ri_mid"]).then_inc(sem("w_idx"), 16)
                sp.dma_start(rm[0:width(KI - 1), KI - 1:KI],
                             I["ri_tail"]).then_inc(sem("w_idx"), 16)
                for j, (m, k) in enumerate(tiles):
                    w = width(k)
                    sp.wait_ge(sem("w_nat"), j + 1)
                    sp.dma_start(I["w_scratch"][m * I_DIM + k * P:m * I_DIM + k * P + w, :],
                                 nat[0:w, j % 2, :]).then_inc(sem(f"w_store{j % 2}"), 16)

            @block.gpsimd
            def _(pool):
                pool.wait_ge(sem("w_idx"), 48)
                for m, name in enumerate(("wgT", "wuT")):
                    for c in range(KH):
                        nc.gpsimd.indirect_dma_start(
                            guT[:, m, c, :], None, I[name],
                            bass.IndirectOffsetOnAxis(ap=ri[:, c:c + 1], axis=0)).then_inc(sem("w_gu"), 16)
                for k in range(KI):
                    w = width(k)
                    nc.gpsimd.indirect_dma_start(
                        dT[0:w, k, :], None, I["wdT"],
                        bass.IndirectOffsetOnAxis(ap=rm[0:w, k:k + 1], axis=0)).then_inc(sem("w_d"), 16)
                pool.wait_ge(sem("w_store0"), 16 * KI)
                pool.wait_ge(sem("w_store1"), 16 * KI)
                for j, (m, k) in enumerate(tiles):
                    w = width(k)
                    if j >= 2:
                        pool.wait_ge(sem("w_q"), j - 1)
                    nc.gpsimd.indirect_dma_start(
                        wi[0:w, j % 2, :], None, I["w_scratch"],
                        bass.IndirectOffsetOnAxis(ap=rm[0:w, k:k + 1], axis=0),
                        element_offset=m * I_DIM * H).then_inc(sem(f"w_wi{j % 2}"), 16)

            @block.tensor
            def _(pe):
                ident = K["ident"]
                pe.wait_ge(sem("w_gu"), 16 * 2 * KH)
                for j, (m, k) in enumerate(tiles):
                    w = width(k)
                    if j >= 2:
                        pe.wait_ge(sem("w_nat"), j - 1)
                    for c in range(KH):
                        last = nc.tensor.transpose(a_ps[0:w, j % 2, c * P:(c + 1) * P],
                                                   guT[:, m, c, k * P:k * P + w], ident[:, :])
                    last.then_inc(sem("w_aps"), 1)
                pe.wait_ge(sem("w_d"), 16 * KI)
                for n in range(KH):
                    if n:
                        pe.wait_ge(sem("w_dn"), n)
                    for k in range(KI):
                        w = width(k)
                        last = nc.tensor.transpose(d_ps[:, k * P:k * P + w],
                                                   dT[0:w, k, n * P:(n + 1) * P], ident[0:w, 0:w])
                    last.then_inc(sem("w_dps"), 1)
                    pe.wait_ge(sem("w_dq"), n + 1)
                    pe.wait_ge(sem("w_dn"), n + 1)
                    for k in range(KI):
                        w = width(k)
                        last = nc.tensor.transpose(d_ps[0:w, k * P:(k + 1) * P],
                                                   dq[:, k * P:k * P + w], ident[:, :])
                    last.then_inc(sem("w_dtp"), 1)
                    pe.wait_ge(sem("w_dts"), n + 1)
                for j, (m, k) in enumerate(tiles):
                    w = width(k)
                    pe.wait_ge(sem("w_q"), j + 1)
                    if j >= 2:
                        pe.wait_ge(sem("w_bs"), j - 1)
                    for c in range(KH):
                        last = nc.tensor.transpose(b_ps[:, j % 2, c * P:c * P + w],
                                                   wq[0:w, j % 2, c * P:(c + 1) * P], ident[0:w, 0:w])
                    last.then_inc(sem("w_bps"), 1)

            @block.scalar
            def _(act):
                for j, (m, k) in enumerate(tiles):
                    w = width(k)
                    act.wait_ge(sem("w_aps"), j + 1)
                    if j >= 2:
                        act.wait_ge(sem(f"w_store{j % 2}"), 16 * (j // 2))
                    nc.scalar.copy(nat[0:w, j % 2, :], a_ps[0:w, j % 2, :]).then_inc(sem("w_nat"), 1)
                for n in range(KH):
                    act.wait_ge(sem("w_dps"), n + 1)
                    if n:
                        act.wait_ge(sem("w_dq"), n)
                    nc.scalar.copy(dn[:, :], d_ps[:, 0:I_DIM]).then_inc(sem("w_dn"), 1)
                    act.wait_ge(sem("w_dtp"), n + 1)
                    nc.scalar.copy(K["wdT"][:, 0:KI - 1, n * P:(n + 1) * P],
                                   d_ps[:, 0:(KI - 1) * P].rearrange("p (k o) -> p k o", o=P))
                    w = width(KI - 1)
                    nc.scalar.copy(K["wdT"][0:w, KI - 1, n * P:(n + 1) * P],
                                   d_ps[0:w, (KI - 1) * P:KI * P]).then_inc(sem("w_dts"), 1)
                for j, (m, k) in enumerate(tiles):
                    w = width(k)
                    act.wait_ge(sem("w_bps"), j + 1)
                    nc.scalar.copy(K["wguT"][:, m, :, k * P:k * P + w],
                                   b_ps[:, j % 2, :].rearrange("p (c i) -> p c i", i=P)[:, :, 0:w]
                                   ).then_inc(sem("w_bs"), 1)

            @block.vector
            def _(dve):
                link = Link(dve, sem("w_link"))
                for n in range(KH):
                    dve.wait_ge(sem("w_dn"), n + 1)
                    if n:
                        dve.wait_ge(sem("w_dtp"), n)
                    nb = I_DIM // BLK
                    int4_quantise(nc, link, dn[:, :], v[:, :], am[:, :], s_[:, :], rs[:, :], dq[:, :],
                                  nb).then_inc(sem("w_dq"), 1)
                for j, (m, k) in enumerate(tiles):
                    w = width(k)
                    nb = H // BLK
                    dve.wait_ge(sem(f"w_wi{j % 2}"), 16 * (j // 2 + 1))
                    if j >= 2:
                        dve.wait_ge(sem("w_bps"), j - 1)
                    int4_quantise(nc, link, wi[0:w, j % 2, :], v[0:w, 0:H], am[0:w, 0:nb], s_[0:w, 0:nb],
                                  rs[0:w, 0:nb], wq[0:w, j % 2, :], nb).then_inc(sem("w_q"), 1)


def gate_up(nc, K, I, sem):
    NP_ = len(PIECES)
    with ExitStack() as ctx:
        sb = lambda n, s, d=F32: ctx.enter_context(nc.sbuf_tensor(n, s, d))
        ps = lambda n, s: ctx.enter_context(nc.psum_tensor(n, s, F32))
        v, c = sb("g_v", [P, H]), sb("g_c", [P, H])
        aq = sb("g_aq", [P, H])
        aT = sb("g_aT", [P, 2, H])
        s2, rs2, am2 = sb("g_s2", [P, 8]), sb("g_rs2", [P, 8]), sb("g_am2", [P, 8])
        r = sb("g_r", [P, SELECT])
        sg = sb("g_sg", [P, 2, 352])
        gate_ps, up_ps = ps("gate_ps", [P, 2, H]), ps("up_ps", [P, 2, H])
        aT_ps = ps("aT_ps", [P, H])

        def guarded(eng, name, value, first):
            if not first or value > 0:
                eng.wait_ge(sem(name), value)

        def pe_transpose(pe, i):
            pe.wait_ge(sem("g_aq"), i + 1)
            for k in range(KH):
                last = nc.tensor.transpose(aT_ps[:, k * P:(k + 1) * P], aq[:, k * P:(k + 1) * P],
                                           K["ident"][:, :])
            last.then_inc(sem("g_aT"), 1)

        def pe_tile(pe, i, slot, first=False, last_tile=False):
            for p, (o, w) in enumerate(PIECES):
                if p == NP_ - 1 and not last_tile:
                    pe_transpose(pe, i + 1)
                if p == 0:
                    pe.wait_ge(sem("g_aTs"), i + 1)
                guarded(pe, "g_h", NP_ * i + p - 1, first)
                for m, dst in enumerate((gate_ps, up_ps)):
                    for k in range(KH):
                        last = nc.tensor.matmul(dst[:, p % 2, 0:w], aT[:, slot, k * P:(k + 1) * P],
                                                K["wguT"][:, m, k, o:o + w],
                                                start=(k == 0), stop=(k == KH - 1))
                last.then_inc(sem("g_mm"), 1)

        def act_evac(act, i, slot, first=False):
            act.wait_ge(sem("g_aT"), i + 1)
            if not first:
                act.wait_ge(sem("g_mm"), NP_ * (i - 1))
            nc.scalar.copy(aT[:, slot, :], aT_ps[:, :]).then_inc(sem("g_aTs"), 1)

        def act_tile(act, i, slot, first=False, last_tile=False):
            for p, (o, w) in enumerate(PIECES):
                if p == NP_ - 1 and not last_tile:
                    act_evac(act, i + 1, 1 - slot, first)
                act.wait_ge(sem("g_mm"), NP_ * i + p + 1)
                guarded(act, "g_h", NP_ * i + p - 1, first)
                nc.scalar.activation(sg[:, p % 2, 0:w], gate_ps[:, p % 2, 0:w], ACT.Tanh,
                                     scale=K["half_g"][:, 0:1]).then_inc(
                    sem("g_tanh"), 1)

        def dve_quantise(dve, i, first=False):
            link = Link(dve, sem("g_link"), i * (FP8_LINKS))
            gate = None if first else (lambda: dve.wait_ge(sem("g_aT"), i))
            x = K["x2"][:, bass.ds(i, 1), :].squeeze(1)
            fp8_quantise(nc, link, x, K["xrg"][:, 0:1], K["xmax"][:, bass.ds(i, 1), :].squeeze(1),
                         K["xrs"][:, bass.ds(i, 1), :].squeeze(1), aq[:, :], v[:, :], c[:, :],
                         s2[:, :], rs2[:, :], am2[:, :], r[:, :], H, gate).then_inc(sem("g_aq"), 1)
            assert link.n == FP8_LINKS

        def dve_tile(dve, i, last_tile=False):
            if not last_tile:
                dve_quantise(dve, i + 1)
            for p, (o, w) in enumerate(PIECES):
                dve.wait_ge(sem("g_tanh"), NP_ * i + p + 1)
                h = K["h"][:, bass.ds(i, 1), o:o + w].squeeze(1)
                nc.vector.scalar_tensor_tensor(h, sg[:, p % 2, 0:w], 1.0, gate_ps[:, p % 2, 0:w],
                                               ALU.add, ALU.mult).then_inc(sem("g_silu"), 1)
                dve.wait_ge(sem("g_silu"), NP_ * i + p + 1)
                nc.vector.scalar_tensor_tensor(h, h, K["half_gg"][:, 0:1], up_ps[:, p % 2, 0:w], ALU.mult,
                                               ALU.mult).then_inc(sem("g_h"), 1)
                dve.wait_ge(sem("g_h"), NP_ * i + p + 1)
                nc.vector.tensor_reduce(
                    K["hmax"][:, bass.ds(i, 1), o // BLK:(o + w) // BLK].squeeze(1), blocks(h), AX_X,
                    ALU.max, apply_absolute_value=True).then_inc(sem("g_hmax"), 1)

        with nc.Block() as block:
            @block.tensor
            def _(pe):
                pe_transpose(pe, 0)
                pe_tile(pe, 0, 0, first=True)
                with pe.Fori(0, NT // 2 - 1) as j:
                    pe_tile(pe, 2 * j + 1, 1)
                    pe_tile(pe, 2 * j + 2, 0)
                pe_tile(pe, NT - 1, 1, last_tile=True)

            @block.scalar
            def _(act):
                act_evac(act, 0, 0, first=True)
                act_tile(act, 0, 0, first=True)
                with act.Fori(0, NT // 2 - 1) as j:
                    act_tile(act, 2 * j + 1, 1)
                    act_tile(act, 2 * j + 2, 0)
                act_tile(act, NT - 1, 1, last_tile=True)

            @block.vector
            def _(dve):
                dve_quantise(dve, 0, first=True)
                with dve.Fori(0, NT - 1) as i:
                    dve_tile(dve, i)
                dve_tile(dve, NT - 1, last_tile=True)
                link = Link(dve, sem("g_link2"))
                dve.wait_ge(sem("g_hmax"), NT * NP_)
                link(nc.vector.tensor_reduce(K["gpart"][:, :],
                                             K["hmax"][:, :, :].rearrange("p t b -> p (t b)"), AX_X, ALU.max))
                nc.vector.tensor_copy(K["gall"][:, :], K["gpart"][:, :]).then_inc(sem("g_gmax"), 1)
                dve.wait_ge(sem("g_gall"), 1)

            @block.gpsimd
            def _(pool):
                pool.wait_ge(sem("g_gmax"), 1)
                nc.gpsimd.partition_all_reduce(K["gall"][:, :], K["gpart"][:, :], P, RMAX).then_inc(
                    sem("g_gall"), 1)


def down(nc, K, I, sem):
    with ExitStack() as ctx:
        sb = lambda n, s, d=F32: ctx.enter_context(nc.sbuf_tensor(n, s, d))
        ps = lambda n, s: ctx.enter_context(nc.psum_tensor(n, s, F32))
        v, c, hq = sb("d_v", [P, I_DIM]), sb("d_c", [P, I_DIM]), sb("d_hq", [P, I_DIM])
        hT = sb("d_hT", [P, KI * P])
        NB = I_DIM // BLK
        hrs, tmp = sb("d_hrs", [P, NT, NB]), sb("d_tmp", [P, NT * NB])
        s2, rs2, am2 = sb("d_s2", [P, 8]), sb("d_rs2", [P, 8]), sb("d_am2", [P, 8])
        r = sb("d_r", [P, SELECT])
        x1s = sb("x1s", [P, H])
        xt = sb("d_xt", [P, H])
        hT_ps = ps("hT_ps", [P, 3 * H])
        y_ps = ps("y_ps", [P, H])
        xT_ps = ps("xT_ps", [P, H])
        WL = width(KI - 1)

        def pe_down(pe, i):
            pe.wait_ge(sem("d_hq"), i + 1)
            for k in range(KI):
                w = width(k)
                last = nc.tensor.transpose(hT_ps[0:w, k * P:(k + 1) * P], hq[:, k * P:k * P + w],
                                           K["ident"][:, :])
            last.then_inc(sem("d_hT"), 1)
            pe.wait_ge(sem("d_hTs"), 2 * (i + 1))
            for k in range(KI):
                w = width(k)
                last = nc.tensor.matmul(y_ps[:, :], hT[0:w, k * P:(k + 1) * P], K["wdT"][0:w, k, :],
                                        start=(k == 0), stop=(k == KI - 1))
            last.then_inc(sem("d_y"), 1)

        def pe_x1(pe, i, first=False):
            pe.wait_ge(sem("d_x1"), i + 1)
            if not first:
                pe.wait_ge(sem("d_xTs"), i)
            for k in range(KH):
                last = nc.tensor.transpose(xT_ps[:, k * P:(k + 1) * P], x1s[:, k * P:(k + 1) * P],
                                           K["ident"][:, :])
            last.then_inc(sem("d_xT"), 1)

        def act_down(act, i):
            act.wait_ge(sem("d_hT"), i + 1)
            nc.scalar.copy(hT[:, 0:(KI - 1) * P], hT_ps[:, 0:(KI - 1) * P]).then_inc(sem("d_hTs"), 1)
            nc.scalar.copy(hT[0:WL, (KI - 1) * P:KI * P], hT_ps[0:WL, (KI - 1) * P:KI * P]).then_inc(
                sem("d_hTs"), 1)

        def act_x1(act, i):
            act.wait_ge(sem("d_xT"), i + 1)
            nc.scalar.copy(K["x1T"][:, :, bass.ds(i * P, P)],
                           xT_ps[:, :].rearrange("p (c t) -> p c t", t=P)).then_inc(sem("d_xTs"), 1)

        def dve_quantise(dve, i, first=False):
            link = Link(dve, sem("d_link"), i * FP8_LINKS)
            gate = None if first else (lambda: dve.wait_ge(sem("d_hT"), i))
            fp8_quantise(nc, link, K["h"][:, bass.ds(i, 1), :].squeeze(1), K["hrg"][:, 0:1],
                         K["hmax"][:, bass.ds(i, 1), :].squeeze(1), hrs[:, bass.ds(i, 1), :].squeeze(1),
                         hq[:, :], v[:, :], c[:, :], s2[:, :], rs2[:, :], am2[:, :], r[:, :],
                         I_DIM, gate).then_inc(sem("d_hq"), 1)

        def dve_x1(dve, i, first=False):
            dve.wait_ge(sem("d_y"), i + 1)
            if not first:
                dve.wait_ge(sem("d_xT"), i)
                dve.wait_ge(sem("d_store"), 16 * i)
            dve.wait_ge(sem("d_x"), 16 * (i + 1))
            nc.vector.scalar_tensor_tensor(x1s[:, :], y_ps[:, :], K["hg"][:, 0:1], xt[:, :], ALU.mult,
                                           ALU.add).then_inc(sem("d_x1"), 1)

        with nc.Block() as block:
            @block.sync
            def _(sp):
                with sp.Fori(0, NT) as i:
                    sp.dma_start(xt[:, :], I["x"][bass.ds(i * P, P), :]).then_inc(sem("d_x"), 16)
                    sp.wait_ge(sem("d_x1"), i + 1)
                    sp.dma_start(I["x1_scratch"][bass.ds(i * P, P), :], x1s[:, :]).then_inc(
                        sem("d_store"), 16)
                sp.wait_ge(sem("d_store"), 16 * NT)

            @block.tensor
            def _(pe):
                pe_down(pe, 0)
                pe_x1(pe, 0, first=True)
                pe_down(pe, 1)
                with pe.Fori(2, NT) as i:
                    pe_x1(pe, i - 1)
                    pe_down(pe, i)
                pe_x1(pe, NT - 1)

            @block.scalar
            def _(act):
                act_down(act, 0)
                with act.Fori(1, NT) as i:
                    act_x1(act, i - 1)
                    act_down(act, i)
                act_x1(act, NT - 1)

            @block.vector
            def _(dve):
                global_scale(nc, Link(dve, sem("d_scale")), K["gall"][:, :], K["hg"][:, :],
                             K["hrg"][:, 0:1], K["hmax"][:, :, :].rearrange("p t b -> p (t b)"),
                             hrs[:, :, :].rearrange("p t b -> p (t b)"), tmp[:, :])
                dve_quantise(dve, 0, first=True)
                dve_quantise(dve, 1)
                dve_x1(dve, 0, first=True)
                with dve.Fori(2, NT) as i:
                    dve_quantise(dve, i)
                    dve_x1(dve, i - 1)
                dve_x1(dve, NT - 1)


TWO_PI = 6.283185307179586
C1 = 6.28125
C2 = 0.0019350051879882812
C3 = TWO_PI - C1 - C2


def project(nc, K, I, sem):
    NQ = HQ * D // H
    NK = HK * D // H
    NGR = NQ + 2 * NK
    HEADS = HQ + HK
    HPG = H // D
    with ExitStack() as ctx:
        sb = lambda n, s, d=F32: ctx.enter_context(nc.sbuf_tensor(n, s, d))
        ps = lambda n, s: ctx.enter_context(nc.psum_tensor(n, s, F32))
        w = sb("p_w", [P, KH, NGR * H])
        raw = sb("p_raw", [P, 2, HEADS * D])
        val = sb("p_val", [P, HK * D])
        sq = sb("p_sq", [P, 2, H])
        xs = sb("p_xs", [P, 2, H])
        rot = sb("p_rot", [P, 16 * D])
        cos, sin = sb("p_cos", [P, NT, D // 2]), sb("p_sin", [P, NT, D // 2])
        tab = sb("p_tab", [P, 4, D])
        nw = sb("p_nw", [P, 2, D])
        nws = sb("p_nws", [P, 2, D])
        ss, sd, y, t = (sb("p_" + n, [P, HEADS]) for n in ("ss", "sd", "y", "t"))
        pos = sb("p_pos", [P, NT])
        in_req = sb("p_in_req", [P, 1])
        invf = sb("p_invf", [P, D // 2])
        g_ps = ps("p_ps", [P, 4, H])

        def pe_tile(pe, i, slot, first=False):
            pe.wait_ge(sem("p_xs"), i + 1)
            for n in range(NGR):
                if not (first and n < 4):
                    pe.wait_ge(sem("p_read"), NGR * i + n - 3)
                for k in range(KH):
                    last = nc.tensor.matmul(g_ps[:, n % 4, :], xs[:, slot, k * P:(k + 1) * P],
                                            w[:, k, n * H:(n + 1) * H], start=(k == 0), stop=(k == KH - 1))
                last.then_inc(sem("p_mm"), 1)

        def act_tile(act, i, slot, turn):
            static = isinstance(turn, int)
            for n in range(NGR):
                act.wait_ge(sem("p_mm"), NGR * i + n + 1)
                src = g_ps[:, n % 4, :]
                if n < NQ + NK:
                    if not (static and i == 0 and n < 2):
                        act.wait_ge(sem("p_ss"), (NQ + NK) * i + n - 1)
                    nc.scalar.activation(sq[:, n % 2, :], src, ACT.Square).then_inc(sem("p_sq"), 1)
                    if n == 0 and not static:
                        act.wait_ge(sem(f"p_store{slot}"), 32 * turn)
                    nc.scalar.copy(raw[:, slot, n * H:(n + 1) * H], src).then_inc(sem("p_read"), 1)
                else:
                    if n == NQ + NK and not (static and i == 0):
                        act.wait_ge(sem("p_vstore"), 16 * i)
                    j = n - NQ - NK
                    nc.scalar.copy(val[:, j * H:(j + 1) * H], src).then_inc(sem("p_read"), 1)
            act.wait_ge(sem("p_ms"), i + 1)
            nc.scalar.activation(sd[:, :], ss[:, :], ACT.Sqrt).then_inc(sem("p_sd"), 1)

        def dve_tile(dve, i, slot, links):
            link = Link(dve, sem("p_link"), links * i)
            for q in range(2):
                for a, (base, wt) in enumerate(((cos, nw), (sin, nws))):
                    link(nc.vector.tensor_tensor(
                        tab[:, 2 * q + a, :].rearrange("p (h f) -> p h f", h=2),
                        wt[:, q, :].rearrange("p (h f) -> p h f", h=2),
                        base[:, bass.ds(i, 1), :].to_broadcast([P, 2, D // 2]), ALU.mult))
            for n in range(NQ + NK):
                dve.wait_ge(sem("p_sq"), (NQ + NK) * i + n + 1)
                nc.vector.tensor_reduce(ss[:, n * HPG:(n + 1) * HPG],
                                        sq[:, n % 2, :].rearrange("p (h d) -> p h d", d=D), AX_X,
                                        ALU.add).then_inc(sem("p_ss"), 1)
            dve.wait_ge(sem("p_ss"), (NQ + NK) * (i + 1))
            nc.vector.tensor_scalar(ss[:, :], ss[:, :], 1.0 / D, EPS, ALU.mult, ALU.add).then_inc(
                sem("p_ms"), 1)
            dve.wait_ge(sem("p_sd"), i + 1)
            link(nc.vector.reciprocal(y[:, :], sd[:, :]))
            link(nc.vector.tensor_tensor(t[:, :], y[:, :], y[:, :], ALU.mult))
            link(nc.vector.tensor_tensor(t[:, :], t[:, :], ss[:, :], ALU.mult))
            link(nc.vector.tensor_scalar(t[:, :], t[:, :], -0.5, 1.5, ALU.mult, ALU.add))
            link(nc.vector.tensor_tensor(y[:, :], y[:, :], t[:, :], ALU.mult))
            link(nc.vector.tensor_scalar(y[:, 0:HQ], y[:, 0:HQ], -SCALE, None, ALU.mult))
            dve.wait_ge(sem("p_read"), NGR * i + NQ + NK)
            for h0, nh, q in ((0, 16, 0), (16, 16, 0), (HQ, HK, 1)):
                x = raw[:, slot, h0 * D:(h0 + nh) * D].rearrange("p (h d) -> p h d", d=D)
                o = rot[:, 0:nh * D].rearrange("p (h d) -> p h d", d=D)
                over = lambda a, n: a.unsqueeze(1).to_broadcast([P, nh, n])
                half = D // 2
                c_, s_ = tab[:, 2 * q, :], tab[:, 2 * q + 1, :]
                nc.vector.tensor_tensor(o[:, :, 0:half], x[:, :, half:D], over(s_[:, 0:half], half), ALU.mult
                                        ).then_inc(sem("p_link"), 1)
                link.n += 1
                link(nc.vector.tensor_tensor(o[:, :, half:D], x[:, :, 0:half], over(s_[:, half:D], half),
                                             ALU.mult))
                link(nc.vector.tensor_tensor(x, x, over(c_, D), ALU.mult))
                link(nc.vector.tensor_tensor(x, x, o, ALU.add))
                last = nc.vector.tensor_tensor(
                    x, x, y[:, h0:h0 + nh].unsqueeze(2).to_broadcast([P, nh, D]), ALU.mult)
                last.then_inc(sem("p_out"), 1)
            return link.n

        PROJ_LINKS = 4 + 6 + 3 * 4

        with nc.Block() as block:
            @block.sync
            def _(sp):
                sp.dma_start(w[:, :, :], I["wqkvT"].rearrange("(c p) n -> p c n", p=P)).then_inc(
                    sem("p_w"), 16)
                for n, (dst, src) in enumerate((
                        (K["lens_i"][:, :], I["lens"].partition_broadcast(P)),
                        (in_req[:, :], I["in_req"]),
                        (invf[:, :], I["invf"].partition_broadcast(P)),
                        (nw[:, 0, :], I["qw"].partition_broadcast(P)),
                        (nw[:, 1, :], I["kw"].partition_broadcast(P)))):
                    sp.dma_start(dst, src).then_inc(sem("p_const"), 16)
                with sp.Fori(0, NT // 2) as j:
                    for slot in range(2):
                        i = 2 * j + slot
                        rows = bass.ds(i * P, P)
                        sp.wait_ge(sem("p_read"), NGR * (i + 1))
                        sp.dma_start(I["v_scratch"][rows, :], val[:, :]).then_inc(sem("p_vstore"), 16)
                        sp.wait_ge(sem("p_out"), 3 * (i + 1))
                        sp.dma_start(I["q_scratch"][rows, :], raw[:, slot, 0:HQ * D]).then_inc(
                            sem(f"p_store{slot}"), 16)
                        sp.dma_start(I["k_scratch"][rows, :], raw[:, slot, HQ * D:]).then_inc(
                            sem(f"p_store{slot}"), 16)
                sp.wait_ge(sem("p_vstore"), 16 * NT)
                sp.wait_ge(sem("p_store0"), 16 * NT)
                sp.wait_ge(sem("p_store1"), 16 * NT)

            @block.tensor
            def _(pe):
                pe.wait_ge(sem("p_w"), 16)
                pe_tile(pe, 0, 0, first=True)
                pe_tile(pe, 1, 1)
                with pe.Fori(1, NT // 2) as j:
                    pe_tile(pe, 2 * j, 0)
                    pe_tile(pe, 2 * j + 1, 1)

            @block.scalar
            def _(act):
                act.wait_ge(sem("p_angle"), 1)
                nc.scalar.activation(sin[:, :, :], sin[:, :, :], ACT.Sin).then_inc(sem("p_trig"), 1)
                nc.scalar.activation(cos[:, :, :], cos[:, :, :], ACT.Sin).then_inc(sem("p_trig"), 1)
                act_tile(act, 0, 0, 0)
                act_tile(act, 1, 1, 0)
                with act.Fori(1, NT // 2) as j:
                    for slot in range(2):
                        act_tile(act, 2 * j + slot, slot, j)

            @block.vector
            def _(dve):
                link = Link(dve, sem("p_link0"))
                lens = K["lens"]
                dve.wait_ge(sem("p_const"), 80)
                link(nc.vector.tensor_copy(lens[:, :], K["lens_i"][:, :]))
                for q in range(BT):
                    rows = slice(q * S, (q + 1) * S)
                    nc.vector.tensor_copy(
                        pos[rows, :], lens[rows, :].rearrange("p (t q) -> p t q", q=BT)[:, :, q]
                    ).then_inc(sem("p_pos"), 1)
                dve.wait_ge(sem("p_pos"), BT)
                link(nc.vector.tensor_scalar(pos[:, :], pos[:, :], in_req[:, 0:1], None, ALU.add))
                for q in range(2):
                    link(nc.vector.tensor_scalar(nws[:, q, 0:D // 2], nw[:, q, D // 2:D], -1.0, None,
                                                 ALU.mult))
                    link(nc.vector.tensor_copy(nws[:, q, D // 2:D], nw[:, q, 0:D // 2]))
                f = raw[:, 0, 0:NT * D // 2].rearrange("p (t f) -> p t f", f=D // 2)
                k_ = raw[:, 0, NT * D // 2:NT * D].rearrange("p (t f) -> p t f", f=D // 2)
                link(nc.vector.tensor_tensor(
                    f, pos[:, :].unsqueeze(2).to_broadcast([P, NT, D // 2]),
                    invf[:, :].unsqueeze(1).to_broadcast([P, NT, D // 2]), ALU.mult))
                link(nc.vector.tensor_scalar(k_, f, 1.0 / TWO_PI, MAGIC_INT, ALU.mult, ALU.add))
                link(nc.vector.tensor_scalar(k_, k_, MAGIC_INT, None, ALU.subtract))
                for part in (C1, C2, C3):
                    link(nc.vector.scalar_tensor_tensor(f, k_, -part, f, ALU.mult, ALU.add))
                link(nc.vector.tensor_scalar(sin[:, :, :], f, 3.1415925, -3.1415925, ALU.min, ALU.max))
                link(nc.vector.tensor_scalar(cos[:, :, :].bitcast(I32), sin[:, :, :].bitcast(I32), 0x7FFFFFFF,
                                             None, ALU.bitwise_and))
                nc.vector.tensor_scalar(cos[:, :, :], cos[:, :, :], -1.0, TWO_PI / 4, ALU.mult, ALU.add
                                        ).then_inc(sem("p_angle"), 1)
                dve.wait_ge(sem("p_trig"), 2)
                def stage_x(i, slot):
                    nc.vector.tensor_copy(xs[:, slot, :].rearrange("p (c t) -> p c t", t=P),
                                          K["x1T"][:, :, bass.ds(i * P, P)]).then_inc(sem("p_xs"), 1)

                def tile(i, slot, first=False, more=True):
                    if more:
                        if not first:
                            dve.wait_ge(sem("p_mm"), NGR * i)
                        stage_x(i + 1, 1 - slot)
                    n = dve_tile(dve, i, slot, PROJ_LINKS)
                    assert n == PROJ_LINKS, n

                stage_x(0, 0)
                tile(0, 0, first=True)
                tile(1, 1)
                with dve.Fori(1, NT // 2 - 1) as j:
                    tile(2 * j, 0)
                    tile(2 * j + 1, 1)
                tile(NT - 2, 0)
                tile(NT - 1, 1, more=False)


def attention(nc, K, I, sem):
    PAIRS = BT * HK
    UH = 2
    UG = HK // UH
    UNITS = BT * UH
    UW = UG * D
    with ExitStack() as ctx:
        sb = lambda n, s, d=F32: ctx.enter_context(nc.sbuf_tensor(n, s, d))
        ps = lambda n, s: ctx.enter_context(nc.psum_tensor(n, s, F32))
        kc = [sb(f"kc{n}", [P, KC, UW]) for n in range(2)]
        vc = [sb(f"vc{n}", [P, KC, UW]) for n in range(2)]
        kn = [sb(f"kn{n}", [S, UW]) for n in range(2)]
        vn = [sb(f"vn{n}", [S, UW]) for n in range(2)]
        qu = [sb(f"qu{n}", [P, UW]) for n in range(2)]
        woT = sb("woT", [P, HQ, H])
        oT = sb("oT", [P, HQ, P])
        kT = sb("kT", [P, 2, LC])
        qT = sb("qT", [P, 2, P + S])
        sc = sb("sc", [P, 2, NKEY])
        pr = sb("pr", [P, 2, NKEY])
        pT = sb("pT", [P, 2, (KC + 1) * P])
        mask = sb("mask", [P, NKEY])
        key = sb("key", [P, LC])
        mneg, rsum, rinv = sb("mneg", [P, 2]), sb("rsum", [P, 2]), sb("rinv", [P, 2])
        idx = sb("idx", [P, UH, BT * KC], U32)
        bt_i = sb("bt_i", [P, B * NPP], I32)
        rows_f = sb("rows_f", [P, B * KC])
        rows = sb("rows", [P, UH, B * KC], U32)
        in_page = sb("in_page", [P, 1])
        lin = sb("lin", [P, KH, H])
        ag = sb("ag", [P, KH, LMAX + NROUTE])
        bl = sb("bl", [LMAX, H])
        bias = sb("bias", [P, H])
        gb = sb("gb", [P, LMAX + NROUTE])
        yt, yT, x1t, res = sb("yt", [P, H]), sb("yT", [P, H]), sb("x1t", [P, H]), sb("res", [P, H])
        u, um, uT = sb("u", [P, LMAX + NROUTE]), sb("um", [P, LMAX]), sb("uT", [LMAX, P])
        rmax, low = sb("rmax", [P, 1]), sb("low", [P, NROUTE])
        s_ps = [ps(f"s_ps{n}", [P, 2 * H]) for n in range(2)]
        kT_ps = ps("kT_ps", [P, H])
        q_ps = ps("q_ps", [P, H])
        pT_ps = ps("pT_ps", [P, H])
        pn_ps = ps("pn_ps", [P, H])
        o_ps = q_ps[:, 256:256 + P]
        wo_ps = s_ps[0][:, H:2 * H]
        z_ps, u_ps = s_ps[1][:, 0:H], s_ps[1][:, H:2 * H]
        ident = K["ident"]

        def steps():
            for k in range(PAIRS + 4):
                yield k, [k - d if 0 <= k - d < PAIRS else None for d in range(5)]

        def base(i, first):
            def wait(eng, name, value, per=1):
                if first and value <= 0:
                    return
                eng.wait_ge(sem(name), i * (PAIRS * per) + value * per)
            return wait

        def pe_tile(pe, i, first=False):
            wait = base(i, first)
            for k, (t, s, _, pt, pv) in steps():
                if t is not None:
                    un, g, sl = t // UG, t % UG, (t // UG) % 2
                    cols = slice(g * D, (g + 1) * D)
                    if g == 0:
                        n = i * (UNITS // 2) + un // 2 + 1
                        pe.wait_ge(sem(f"a_k{sl}"), n * 16 * KC)
                        pe.wait_ge(sem(f"a_q{sl}"), n * 16 * (REP + 1))
                    wait(pe, "a_kTs", t)
                    for c in range(KC):
                        last = nc.tensor.transpose(kT_ps[:, c * P:(c + 1) * P], kc[sl][:, c, cols],
                                                   ident[:, :])
                    last.then_inc(sem("a_kT"), 1)
                if pt is not None:
                    wait(pe, "a_pr", pt + 1)
                    wait(pe, "a_pTs", pt)
                    wait(pe, "a_pns", pt)
                    for c in range(KC):
                        nc.tensor.transpose(pT_ps[:, c * P:(c + 1) * P],
                                            pr[:, pt % 2, c * P:(c + 1) * P], ident[:, :])
                    nc.tensor.transpose(pn_ps[0:S, 0:P], pr[:, pt % 2, LC:NKEY], ident[:, :]).then_inc(
                        sem("a_pT"), 1)
                if t is not None:
                    wait(pe, "a_qTs", t)
                    wait(pe, "a_oTs", max(t - 4, 0))
                    if t == 0 and not first:
                        pe.wait_ge(sem("a_uTs"), i)
                    nc.tensor.transpose(q_ps[:, 0:P], qu[sl][:, cols], ident[:, :])
                    nc.tensor.transpose(q_ps[:, P:P + S], kn[sl][:, cols], ident[0:S, 0:S]).then_inc(
                        sem("a_qT"), 1)
                if s is not None:
                    wait(pe, "a_kTs", s + 1)
                    wait(pe, "a_qTs", s + 1)
                    wait(pe, "a_max", s - 1)
                    if s == 1 and not first:
                        pe.wait_ge(sem("a_res"), 2 * i)
                    dst = s_ps[s % 2]
                    nc.tensor.matmul(dst[:, 0:LC], qT[:, s % 2, 0:P], kT[:, s % 2, :], start=True, stop=True)
                    nc.tensor.matmul(dst[:, LC:NKEY], qT[:, s % 2, 0:P], qT[:, s % 2, P:P + S],
                                     start=True, stop=True).then_inc(sem("a_s"), 1)
                if pv is not None:
                    un, g, sl = pv // UG, pv % UG, (pv // UG) % 2
                    cols = slice(g * D, (g + 1) * D)
                    if g == 0:
                        n = i * (UNITS // 2) + un // 2 + 1
                        pe.wait_ge(sem(f"a_v{sl}"), n * 16 * KC)
                        pe.wait_ge(sem(f"a_vn{sl}"), n * 16)
                    wait(pe, "a_pTs", pv + 1)
                    wait(pe, "a_pns", pv + 1)
                    wait(pe, "a_oTs", pv)
                    wait(pe, "a_qTs", min(pv + 5, PAIRS))
                    for c in range(KC):
                        nc.tensor.matmul(o_ps, vc[sl][:, c, cols], pT[:, pv % 2, c * P:(c + 1) * P],
                                         start=(c == 0), stop=False)
                    nc.tensor.matmul(o_ps, vn[sl][:, cols], pT[0:S, pv % 2, KC * P:(KC + 1) * P],
                                     start=False, stop=True).then_inc(sem("a_o"), 1)
                if k >= PAIRS:
                    pe_project(pe, i, k - PAIRS, wait)
            for g in range(4, HK):
                pe_project(pe, i, g, wait)
            pe_linear(pe, i)

        def pe_project(pe, i, g, wait):
            wait(pe, "a_oTs", PAIRS - HK + g + 1)
            if g == 0:
                wait(pe, "a_max", PAIRS - 1)
            for r in range(REP):
                h = REP * g + r
                last = nc.tensor.matmul(wo_ps, oT[:, h, :], woT[:, h, :], start=(h == 0), stop=(h == HQ - 1))
            if g == HK - 1:
                last.then_inc(sem("a_wo"), 1)

        def pe_linear(pe, i):
            pe.wait_ge(sem("a_y"), i + 1)
            for c in range(KH):
                last = nc.tensor.transpose(kT_ps[:, c * P:(c + 1) * P], yt[:, c * P:(c + 1) * P], ident[:, :])
            last.then_inc(sem("a_yT"), 1)
            pe.wait_ge(sem("a_yTs"), i + 1)
            pe.wait_ge(sem("a_max"), (i + 1) * PAIRS)
            for c in range(KH):
                last = nc.tensor.matmul(u_ps[:, 0:LMAX + NROUTE], yT[:, c * P:(c + 1) * P], ag[:, c, :],
                                        start=(c == 0), stop=(c == KH - 1))
            last.then_inc(sem("a_u"), 1)
            for c in range(KH):
                nc.tensor.matmul(z_ps, yT[:, c * P:(c + 1) * P], lin[:, c, :], start=(c == 0), stop=False)
            pe.wait_ge(sem("a_um"), i + 1)
            hold(pe, sem("a_passed"))
            nc.tensor.transpose(q_ps[0:LMAX, 0:P], um[:, :], ident[:, :]).then_inc(sem("a_uT"), 1)
            pe.wait_ge(sem("a_uTs"), i + 1)
            nc.tensor.matmul(z_ps, uT[:, :], bl[:, :], start=False, stop=True).then_inc(sem("a_z"), 1)

        def act_tile(act, i, first=False):
            wait = base(i, first)
            for k, (t, s, _, pt, pv) in steps():
                if t is not None:
                    wait(act, "a_kT", t + 1)
                    wait(act, "a_s", t - 1)
                    nc.scalar.copy(kT[:, t % 2, :], kT_ps[:, :]).then_inc(sem("a_kTs"), 1)
                if pt is not None:
                    wait(act, "a_pT", pt + 1)
                    wait(act, "a_o", pt - 1)
                    nc.scalar.copy(pT[0:S, pt % 2, KC * P:(KC + 1) * P], pn_ps[0:S, 0:P]).then_inc(
                        sem("a_pns"), 1)
                if t is not None:
                    wait(act, "a_qT", t + 1)
                    nc.scalar.copy(qT[:, t % 2, :], q_ps[:, 0:P + S]).then_inc(sem("a_qTs"), 1)
                if pv is not None:
                    b, g = pv // HK, pv % HK
                    wait(act, "a_o", pv + 1)
                    if pv == 0 and not first:
                        act.wait_ge(sem("a_wo"), i)
                    nc.scalar.copy(oT[:, REP * g:REP * (g + 1), b * S:(b + 1) * S],
                                   o_ps.rearrange("p (r t) -> p r t", t=S)).then_inc(sem("a_oTs"), 1)
                if s is not None:
                    wait(act, "a_max", s + 1)
                    wait(act, "a_pT", s - 1)
                    nc.scalar.activation(pr[:, s % 2, :], sc[:, s % 2, :], ACT.Exp, scale=-1.0,
                                         bias=mneg[:, s % 2:s % 2 + 1],
                                         accum_out=rsum[:, s % 2:s % 2 + 1]).then_inc(sem("a_exp"), 1)
            act.wait_ge(sem("a_wo"), i + 1)
            nc.scalar.copy(yt[:, :], wo_ps).then_inc(sem("a_y"), 1)
            act.wait_ge(sem("a_yT"), i + 1)
            nc.scalar.copy(yT[:, :], kT_ps[:, :]).then_inc(sem("a_yTs"), 1)
            act.wait_ge(sem("a_uT"), i + 1)
            nc.scalar.copy(uT[:, :], q_ps[0:LMAX, 0:P]).then_inc(sem("a_uTs"), 1)

        MASK_LINKS = BT
        ROUTE_LINKS = 8

        def dve_tile(dve, i, first=False):
            wait = base(i, first)
            link = Link(dve, sem("a_link"), i * (MASK_LINKS + PAIRS + ROUTE_LINKS))
            for k, (t, s, e, pt, pv) in steps():
                if pt is not None:
                    wait(dve, "a_pT", pt + 1)
                    wait(dve, "a_o", pt - 1)
                    nc.vector.tensor_copy(pT[:, pt % 2, 0:KC * P], pT_ps[:, :]).then_inc(sem("a_pTs"), 1)
                if e is not None:
                    wait(dve, "a_exp", e + 1)
                    link(nc.vector.reciprocal(rinv[:, e % 2:e % 2 + 1], rsum[:, e % 2:e % 2 + 1]))
                    nc.vector.tensor_scalar(pr[:, e % 2, :], pr[:, e % 2, :], rinv[:, e % 2:e % 2 + 1], None,
                                            ALU.mult).then_inc(sem("a_pr"), 1)
                if s is not None:
                    if s % HK == 0:
                        link(nc.vector.tensor_scalar(mask[:, 0:LC], key[:, :],
                                                     K["lens"][:, bass.ds(BT * i + s // HK, 1)], 1e30,
                                                     ALU.is_ge, ALU.mult))
                    wait(dve, "a_s", s + 1)
                    wait(dve, "a_exp", s - 1)
                    hold(dve, sem("a_passed"))
                    nc.vector.tensor_tensor_reduce(
                        out=sc[:, s % 2, :], in0=s_ps[s % 2][:, 0:NKEY], in1=mask[:, :], scale=1.0,
                        scalar=3e38, op0=ALU.add, op1=ALU.min,
                        accum_out=mneg[:, s % 2:s % 2 + 1]).then_inc(sem("a_max"), 1)
            dve.wait_ge(sem("a_u"), i + 1)
            link(nc.vector.tensor_tensor(u[:, :], u_ps[:, 0:LMAX + NROUTE], gb[:, :], ALU.add))
            link(nc.vector.tensor_reduce(rmax[:, :], u[:, LMAX:], AX_X, ALU.max))
            link(nc.vector.tensor_scalar(low[:, :], u[:, LMAX:], rmax[:, 0:1], None, ALU.is_lt))
            for r in range(1, NROUTE - 1):
                link(nc.vector.tensor_tensor(low[:, r:r + 1], low[:, r:r + 1], low[:, r - 1:r], ALU.mult))
            link(nc.vector.tensor_copy(um[:, 0:RANKS[0]], u[:, 0:RANKS[0]]))
            for r in range(NROUTE - 1):
                last = nc.vector.tensor_scalar(um[:, RANKS[r]:RANKS[r + 1]], u[:, RANKS[r]:RANKS[r + 1]],
                                               low[:, r:r + 1], None, ALU.mult)
                if r < NROUTE - 2:
                    link(last)
            last.then_inc(sem("a_um"), 1)
            dve.wait_ge(sem("a_x1"), 16 * (i + 1))
            if not first:
                dve.wait_ge(sem("a_out"), 16 * i)
            nc.vector.tensor_tensor(res[:, :], x1t[:, :], bias[:, :], ALU.add).then_inc(sem("a_res"), 1)
            dve.wait_ge(sem("a_res"), 2 * i + 1)
            dve.wait_ge(sem("a_z"), i + 1)
            nc.vector.tensor_tensor(res[:, :], res[:, :], z_ps, ALU.add).then_inc(sem("a_res"), 1)
            return link.n

        def freed(eng, name, i, un, first):
            if first and un < 2:
                return
            eng.wait_ge(sem(name), i * PAIRS + (un - 1) * UG)

        def pool_tile(pool, i, first=False):
            if not first:
                for sl in range(2):
                    pool.wait_ge(sem(f"a_k{sl}"), i * (UNITS // 2) * 16 * KC)
                    pool.wait_ge(sem(f"a_v{sl}"), i * (UNITS // 2) * 16 * KC)
            nc.gpsimd.tensor_copy(idx[:, :, :], rows[:, :, bass.ds(i * BT * KC, BT * KC)]).then_inc(
                sem("a_idx"), 1)
            pool.wait_ge(sem("a_idx"), i + 1)
            for un in range(UNITS):
                b, half, sl = un // UH, un % UH, un % 2
                for name, free, cache, dst in (("a_k", "a_qT", "kcache", kc), ("a_v", "a_o", "vcache", vc)):
                    freed(pool, free, i, un, first)
                    hold(pool, sem("a_passed"))
                    for c in range(KC):
                        nc.gpsimd.indirect_dma_start(
                            dst[sl][:, c, :], None, I[cache],
                            bass.IndirectOffsetOnAxis(ap=idx[:, half, b * KC + c:b * KC + c + 1], axis=0)
                        ).then_inc(sem(f"{name}{sl}"), 16)

        def sync_tile(sp, i, first=False):
            for un in range(UNITS):
                b, half, sl = un // UH, un % UH, un % 2
                tok = bass.ds(i * P + b * S, S)
                freed(sp, "a_qT", i, un, first)
                for r in range(REP):
                    src = I["q_scratch"][tok, :].rearrange("t (g r d) -> t g r d", r=REP, d=D)[
                        :, half * UG:(half + 1) * UG, r, :]
                    sp.dma_start(qu[sl][r * S:(r + 1) * S, :].rearrange("t (g d) -> t g d", d=D), src
                                 ).then_inc(sem(f"a_q{sl}"), 16)
                sp.dma_start(kn[sl][:, :], I["k_scratch"][tok, half * UW:(half + 1) * UW]).then_inc(
                    sem(f"a_q{sl}"), 16)
                freed(sp, "a_o", i, un, first)
                sp.dma_start(vn[sl][:, :], I["v_scratch"][tok, half * UW:(half + 1) * UW]).then_inc(
                    sem(f"a_vn{sl}"), 16)
            rows_ = bass.ds(i * P, P)
            if not first:
                sp.wait_ge(sem("a_res"), 2 * i)
            sp.dma_start(x1t[:, :], I["x1_scratch"][rows_, :]).then_inc(sem("a_x1"), 16)
            sp.wait_ge(sem("a_res"), 2 * (i + 1))
            sp.dma_start(I["out"][rows_, :], res[:, :]).then_inc(sem("a_out"), 16)

        with nc.Block() as block:
            @block.sync
            def _(sp):
                for dst, src in ((bt_i[:, :], I["bt"].partition_broadcast(P)), (in_page[:, :], I["in_req"])):
                    sp.dma_start(dst, src).then_inc(sem("a_pages"), 16)
                for dst, src in ((key[:, :], I["key"].partition_broadcast(P)),
                                 (bias[:, :], I["lb"].partition_broadcast(P)),
                                 (gb[:, LMAX:], I["gate_b"].partition_broadcast(P)),
                                 (bl[:, :], I["BlT"])):
                    sp.dma_start(dst, src).then_inc(sem("a_const"), 16)
                for dst, src in ((lin[:, :, :], I["linT"].rearrange("(c p) n -> p c n", p=P)),
                                 (ag[:, :, 0:LMAX], I["AlT"].rearrange("(c p) n -> p c n", p=P)),
                                 (ag[:, :, LMAX:], I["gateT"].rearrange("(c p) n -> p c n", p=P))):
                    sp.dma_start(dst, src).then_inc(sem("a_const"), 16)
                sync_tile_first = True
                sp.dma_start(woT[:, :, :], I["woT"].rearrange("(h d) n -> d h n", d=P)).then_inc(
                    sem("a_const"), 16)
                sync_tile(sp, 0, first=sync_tile_first)
                with sp.Fori(1, NT) as i:
                    sync_tile(sp, i)
                sp.wait_ge(sem("a_out"), 16 * NT)

            @block.gpsimd
            def _(pool):
                pool.wait_ge(sem("a_rows"), 2)
                pool_tile(pool, 0, first=True)
                with pool.Fori(1, NT) as i:
                    pool_tile(pool, i)

            @block.tensor
            def _(pe):
                pe.wait_ge(sem("a_const"), 16 * 8)
                pe_tile(pe, 0, first=True)
                with pe.Fori(1, NT) as i:
                    pe_tile(pe, i)

            @block.scalar
            def _(act):
                act_tile(act, 0, first=True)
                with act.Fori(1, NT) as i:
                    act_tile(act, i)

            @block.vector
            def _(dve):
                link = Link(dve, sem("a_link0"))
                link(nc.vector.memset(mask[:, :], 0.0))
                link(nc.vector.memset(gb[:, 0:LMAX], 0.0))
                dve.wait_ge(sem("a_pages"), 32)
                for q in range(P // PSIZE):
                    part = slice(q * PSIZE, (q + 1) * PSIZE)
                    nc.vector.tensor_copy(
                        rows_f[part, :], bt_i[part, :].rearrange("p (n q) -> p n q", q=P // PSIZE)[:, :, q]
                    ).then_inc(sem("a_bt"), 1)
                dve.wait_ge(sem("a_bt"), P // PSIZE)
                link(nc.vector.tensor_scalar(rows_f[:, :], rows_f[:, :], float(PSIZE), in_page[:, 0:1],
                                             ALU.mult, ALU.add))
                for half in range(UH):
                    nc.vector.tensor_scalar(rows[:, half, :], rows_f[:, :], float(UH), float(half), ALU.mult,
                                            ALU.add).then_inc(sem("a_rows"), 1)
                dve.wait_ge(sem("a_const"), 16 * 8)
                n = dve_tile(dve, 0, first=True)
                assert n == MASK_LINKS + PAIRS + ROUTE_LINKS, n
                with dve.Fori(1, NT) as i:
                    dve_tile(dve, i)


def build(nc, I):
    sems = {}
    with ExitStack() as ctx:
        def sem(name):
            if name not in sems:
                sems[name] = ctx.enter_context(nc.semaphore(name))
            return sems[name]

        keep = lambda c, n, s, d=F32: c.enter_context(nc.sbuf_tensor(n, s, d))
        K = {
            "ident": keep(ctx, "ident", [P, P]),
            "lens_i": keep(ctx, "lens_i", [P, B], I32),
            "lens": keep(ctx, "lens", [P, B]),
            "xg": keep(ctx, "xg", [P, 1]),
            "xrg": keep(ctx, "xrg", [P, 1]),
            "half_g": keep(ctx, "half_g", [P, 1]),
            "half_gg": keep(ctx, "half_gg", [P, 1]),
            "hg": keep(ctx, "hg", [P, 1]),
            "hrg": keep(ctx, "hrg", [P, 1]),
            "gpart": keep(ctx, "gpart", [P, 1]),
            "gall": keep(ctx, "gall", [P, 1]),
        }
        with ExitStack() as middle:
            K["x2"] = keep(middle, "x2", [P, NT, H])
            K["x1T"] = K["x2"][:, :, :].rearrange("p t n -> p (t n)").rearrange("p (c t) -> p c t", t=TOK)
            with ExitStack() as layer0:
                K["xmax"] = keep(layer0, "xmax", [P, NT, H // BLK])
                K["xrs"] = keep(layer0, "xrs", [P, NT, H // BLK])
                condition(nc, K, I, sem)
                K["wdT"] = keep(layer0, "wdT", [P, KI, H])
                K["h"] = keep(layer0, "h", [P, NT, I_DIM])
                K["hmax"] = keep(layer0, "hmax", [P, NT, I_DIM // BLK])
                with ExitStack() as gu:
                    K["wguT"] = keep(gu, "wguT", [P, 2, KH, I_DIM])
                    weights(nc, K, I, sem)
                    gate_up(nc, K, I, sem)
                down(nc, K, I, sem)
            project(nc, K, I, sem)
        attention(nc, K, I, sem)


def layout(x, itok_B_4_50, itok_Bx16_0_63, itok_B_207_1644, L0_cond_A, L0_cond_B, L0_ffn_w_gate,
           L0_ffn_w_up, L0_ffn_w_down, L0_ffn_ri_in, L0_ffn_ri_mid, L1_cond_Wq, L1_cond_Wk, L1_cond_Wv,
           L1_cond_Wo, L1_cond_q_norm_w, L1_cond_k_norm_w, L1_cond_k_cache, L1_cond_v_cache, L1_ffn_W,
           L1_ffn_b, L1_ffn_A, L1_ffn_B, L1_ffn_gate_w, L1_ffn_gate_b):
    import numpy as np

    c = np.ascontiguousarray
    x = np.asarray(x).reshape(TOK, H)
    p = np.arange(P)
    return {
        "x": c(x), "xT": c(x.T),
        "ids": c(itok_B_4_50), "bt": c(itok_Bx16_0_63).reshape(-1), "lens": c(itok_B_207_1644),
        "A_o": c(np.asarray(L0_cond_A).transpose(1, 0, 2).reshape(H, IDS * RANK)),
        "B_r": c(L0_cond_B).reshape(IDS * RANK, H),
        "wgT": c(np.asarray(L0_ffn_w_gate).T), "wuT": c(np.asarray(L0_ffn_w_up).T),
        "wdT": c(np.asarray(L0_ffn_w_down).T),
        "ri_in": c(np.asarray(L0_ffn_ri_in).reshape(KH, P).T),
        "ri_mid": c(np.asarray(L0_ffn_ri_mid)[:I_DIM // P * P].reshape(-1, P).T),
        "ri_tail": c(np.asarray(L0_ffn_ri_mid)[I_DIM // P * P:].reshape(-1, 1)),
        "wqkvT": c(np.concatenate([np.asarray(L1_cond_Wq), np.asarray(L1_cond_Wk),
                                   np.asarray(L1_cond_Wv)]).T),
        "woT": c(np.asarray(L1_cond_Wo).T),
        "qw": c(L1_cond_q_norm_w), "kw": c(L1_cond_k_norm_w),
        "kcache": c(L1_cond_k_cache).reshape(2 * PAGES * PSIZE, HK * D // 2),
        "vcache": c(L1_cond_v_cache).reshape(2 * PAGES * PSIZE, HK * D // 2),
        "linT": c(np.asarray(L1_ffn_W).T), "lb": c(L1_ffn_b), "AlT": c(np.asarray(L1_ffn_A).T),
        "BlT": c(np.asarray(L1_ffn_B).T), "gateT": c(np.asarray(L1_ffn_gate_w).T),
        "gate_b": c(L1_ffn_gate_b),
        "ident": np.eye(P, dtype=np.float32),
        "mine": (p[:, None] // RANK == np.arange(2 * P)[None, :] // S).astype(np.float32),
        "eight": (p[:, None] // RANK == np.arange(8)[None, :]).astype(np.float32),
        "rank_of": (p[:, None] % RANK).astype(np.float32),
        "in_req": (p[:, None] % S).astype(np.float32),
        "key": np.arange(LC, dtype=np.float32),
        "invf": (1.0 / np.float32(10000.0) ** (np.arange(0, D, 2, dtype=np.float32) / np.float32(D))
                 ).astype(np.float32),
    }


def kernel(**inputs):
    import concourse.bacc as _bacc
    from concourse import mybir as _mybir
    from concourse.bass_utils import run_bass_kernel_spmd as _run

    nc = _bacc.Bacc("TRN2", target_bir_lowering=False, num_devices=1)
    arrays = layout(**inputs)
    I = {n: nc.dram_tensor(n + "_in", a.shape, _mybir.dt.from_np(a.dtype), kind="ExternalInput").ap()
         for n, a in arrays.items()}
    for n, shape in (("a_scratch", (IDS * RANK, H)), ("w_scratch", (2 * I_DIM, H)),
                     ("x1_scratch", (TOK, H)), ("q_scratch", (TOK, HQ * D)),
                     ("k_scratch", (TOK, HK * D)), ("v_scratch", (TOK, HK * D))):
        I[n] = nc.dram_tensor(n, shape, F32).ap()
    I["out"] = nc.dram_tensor("out", (TOK, H), F32, kind="ExternalOutput").ap()
    build(nc, I)
    r = _run(nc, [{n + "_in": a for n, a in arrays.items()}], core_ids=[0])
    return r.results[0]["out"].reshape(B, S, H)
```

```python
from contextlib import ExitStack

import concourse.bass as bass
from concourse import mybir

F32 = mybir.dt.float32
I32 = mybir.dt.int32
U32 = mybir.dt.uint32
ALU = mybir.AluOpType
ACT = mybir.ActivationFunctionType
AX_X = mybir.AxisListType.X
RMAX = bass.bass_isa.ReduceOp.max

P = 128
B, S, H = 64, 32, 512
TOK = B * S
NT = TOK // P
BT = P // S
RANK = 16
IDS = 64
I_DIM = 1376
KH = H // P
CHUNKS_OF_X = (2, 3, 0, 1)
KI = (I_DIM + P - 1) // P
BLK = 16
SELECT = 128
HQ, HK, D = 32, 8, 128
REP = HQ // HK
PAGES, PSIZE, NPP = 64, 32, 16
LC = NPP * PSIZE
KC = LC // P
NKEY = LC + S
EPS = 1e-6
SCALE = D ** -0.5
FP8_MAX = 448.0
GDIV = 448.0 * 6.0
MAGIC_INT = 1.5 * 2.0 ** 23
FP8_TO_C = 1.5 * 2.0 ** 20
FP8_MIN_NORMAL = 2.0 ** -6
EXPONENT = 0x7F800000
LMAX = 64
NROUTE = 4
RANKS = (8, 16, 32, 64)
PIECES = [(0, 352), (352, 352), (704, 352), (1056, 320)]


def width(k):
    return min(P, I_DIM - k * P)


class Link:

    def __init__(self, eng, sem, base=0):
        self.eng, self.sem, self.base, self.n = eng, sem, base, 0

    def __call__(self, ins):
        self.n += 1
        ins.then_inc(self.sem, 1)
        self.eng.wait_ge(self.sem, self.base + self.n)


def hold(eng, passed):
    eng.sem_inc(passed, 1)


def blocks(ap):
    return ap.rearrange("p (b e) -> p b e", e=BLK)


def per_block(ap, nb):
    return ap.unsqueeze(2).to_broadcast([P, nb, BLK])


def seventh(nc, link, out, a, q, t):
    link(nc.vector.tensor_scalar(q, a, 1.0 / 7.0, None, ALU.mult))
    link(nc.vector.scalar_tensor_tensor(t, q, -8.0, a, ALU.mult, ALU.add))
    link(nc.vector.tensor_tensor(t, t, q, ALU.add))
    link(nc.vector.scalar_tensor_tensor(out, t, 1.0 / 7.0, q, ALU.mult, ALU.add))


def fp8_scales(nc, link, s, rs, t):
    seventh(nc, link, s, s, rs, t)
    link(nc.vector.tensor_scalar(s, s, 7.0 / FP8_MAX, 1e-8, ALU.mult, ALU.max))
    link(nc.vector.reciprocal(rs, s))


def fp8_round(nc, link, v, c):
    link(nc.vector.tensor_scalar(c.bitcast(I32), v.bitcast(I32), EXPONENT, None, ALU.bitwise_and))
    link(nc.vector.tensor_scalar(c, c, FP8_MIN_NORMAL, FP8_TO_C, ALU.max, ALU.mult))
    link(nc.vector.tensor_tensor(v, v, c, ALU.add))
    link(nc.vector.tensor_tensor(v, v, c, ALU.subtract))


def fp8_quantise(nc, link, x, rg, s, rs, out, v, c, s2, rs2, t2, r, n, out_gate):
    nb, no = n // BLK, SELECT // BLK
    link(nc.vector.scalar_tensor_tensor(blocks(v), blocks(x), rg, per_block(rs, nb), ALU.mult, ALU.mult))
    fp8_round(nc, link, v, c)
    if out_gate is not None:
        out_gate()
    link(nc.vector.tensor_tensor(blocks(out), blocks(v), per_block(s, nb), ALU.mult))
    tail, v, c = out[:, n - SELECT:n], v[:, 0:SELECT], c[:, 0:SELECT]
    link(nc.vector.scalar_tensor_tensor(r, x[:, n - SELECT:n], rg, tail, ALU.mult, ALU.subtract))
    link(nc.vector.tensor_reduce(s2, blocks(r), AX_X, ALU.max, apply_absolute_value=True))
    fp8_scales(nc, link, s2, rs2, t2)
    link(nc.vector.tensor_tensor(blocks(v), blocks(r), per_block(rs2, no), ALU.mult))
    fp8_round(nc, link, v, c)
    link(nc.vector.tensor_tensor(blocks(r), blocks(v), per_block(s2, no), ALU.mult))
    return nc.vector.tensor_tensor(tail, tail, r, ALU.add)


FP8_LINKS = (1 + 4 + 1) + (2 + 6) + (1 + 4 + 1)


def int4_quantise(nc, link, w, v, am, s, rs, out, nb):
    link(nc.vector.tensor_reduce(am, blocks(w), AX_X, ALU.max, apply_absolute_value=True))
    seventh(nc, link, am, am, rs, s)
    link(nc.vector.tensor_scalar(s, am, 1e-8, None, ALU.max))
    link(nc.vector.reciprocal(rs, s))
    m = w.shape[0]
    wide = lambda a: a.unsqueeze(2).to_broadcast([m, nb, BLK])
    link(nc.vector.tensor_tensor(blocks(v), blocks(w), wide(rs), ALU.mult))
    link(nc.vector.tensor_scalar(v, v, MAGIC_INT, MAGIC_INT, ALU.add, ALU.subtract))
    return nc.vector.tensor_tensor(blocks(out), blocks(v), wide(s), ALU.mult)


def condition(nc, K, I, sem):
    GB = 8
    NG = B // GB
    with ExitStack() as ctx:
        sb = lambda n, s, d=F32: ctx.enter_context(nc.sbuf_tensor(n, s, d))
        ps = lambda n, s: ctx.enter_context(nc.psum_tensor(n, s, F32))
        xT = sb("xT", [P, KH, TOK])
        a_gath = sb("a_gath", [P, KH, IDS * RANK])
        a_rows = sb("a_rows", [P, 2, H])
        ids = sb("ids", [P, NG, GB], I32)
        idf = sb("idf", [P, NG, GB])
        rowf = sb("rowf", [P, NG])
        row = sb("row", [P, NG], U32)
        ri = sb("ri", [P, KH], I32)
        tmp = sb("c_tmp", [P, NT * H // BLK])
        a_sel = sb("a_sel", [P, 2, H])
        b_sel = sb("b_sel", [P, 2, H])
        bT = sb("bT", [P, 2, KH * P])
        bx = sb("bx", [P, 2, 2 * P])
        mine = sb("mine", [P, 2 * P])
        rank_of = sb("rank_of", [P, 1])
        eight = sb("eight", [P, GB])
        t_ps = ps("t_ps", [P, 2, H])
        bT_ps = ps("bT_ps", [P, 2, H])
        bx_ps = ps("bx_ps", [P, 2, H])
        x2_ps = ps("x2_ps", [P, 2, H])

        def amax(dve, g):
            for n in (2 * g, 2 * g + 1):
                dve.wait_ge(sem("c_x2s"), n + 1)
                nc.vector.tensor_reduce(K["xmax"][:, n, :], blocks(K["x2"][:, n, :]), AX_X, ALU.max,
                                    apply_absolute_value=True).then_inc(sem("c_amax"), 1)

        with nc.Block() as block:
            @block.sync
            def _(sp):
                sp.dma_start(K["ident"][:, :], I["ident"]).then_inc(sem("c_const"), 16)
                sp.dma_start(mine[:, :], I["mine"]).then_inc(sem("c_const"), 16)
                sp.dma_start(rank_of[:, :], I["rank_of"]).then_inc(sem("c_const"), 16)
                sp.dma_start(eight[:, :], I["eight"]).then_inc(sem("c_const"), 16)
                sp.dma_start(ids[:, :, :], I["ids"].partition_broadcast(P).rearrange(
                    "p (g b) -> p g b", b=GB)).then_inc(sem("c_const"), 16)
                sp.dma_start(ri[:, :], I["ri_in"]).then_inc(sem("c_ri"), 16)
                sp.dma_start(xT[:, :, :], I["xT"].rearrange("(c p) t -> p c t", p=P)).then_inc(sem("c_x"), 16)
                for j in range(8):
                    sp.wait_ge(sem("c_arow"), j + 1)
                    sp.dma_start(I["a_scratch"][j * P:(j + 1) * P, :], a_rows[:, j % 2, :]).then_inc(
                        sem(f"c_astore{j % 2}"), 16)

            @block.gpsimd
            def _(pool):
                pool.wait_ge(sem("c_ri"), 16)
                for c in range(KH):
                    nc.gpsimd.indirect_dma_start(
                        a_gath[:, c, :], None, I["A_o"],
                        bass.IndirectOffsetOnAxis(ap=ri[:, c:c + 1], axis=0)).then_inc(sem("c_agath"), 16)
                pool.wait_ge(sem("c_row"), 1)
                pool.wait_ge(sem("c_astore0"), 64)
                pool.wait_ge(sem("c_astore1"), 64)
                for g in range(NG):
                    if g >= 2:
                        pool.wait_ge(sem("c_bT"), g - 1)
                        pool.wait_ge(sem("c_x2"), 2 * (g - 1))
                    off = bass.IndirectOffsetOnAxis(ap=row[:, g:g + 1], axis=0)
                    nc.gpsimd.indirect_dma_start(b_sel[:, g % 2, :], None, I["B_r"], off).then_inc(
                        sem(f"c_bsel{g % 2}"), 16)
                    nc.gpsimd.indirect_dma_start(a_sel[:, g % 2, :], None, I["a_scratch"], off).then_inc(
                        sem(f"c_asel{g % 2}"), 16)
                pool.wait_ge(sem("c_gmax"), 1)
                nc.gpsimd.partition_all_reduce(K["gall"][:, :], K["gpart"][:, :], P, RMAX).then_inc(
                    sem("c_gall"), 1)

            @block.tensor
            def _(pe):
                pe.wait_ge(sem("c_const"), 80)
                pe.wait_ge(sem("c_agath"), 64)
                for j in range(8):
                    if j >= 2:
                        pe.wait_ge(sem("c_arow"), j - 1)
                    for c in range(KH):
                        last = nc.tensor.transpose(t_ps[:, j % 2, c * P:(c + 1) * P],
                                                   a_gath[:, c, j * P:(j + 1) * P], K["ident"][:, :])
                    last.then_inc(sem("c_aT"), 1)
                pe.wait_ge(sem("c_x"), 16)
                for g in range(NG):
                    pe.wait_ge(sem(f"c_bsel{g % 2}"), 16 * (g // 2 + 1))
                    if g >= 2:
                        pe.wait_ge(sem("c_bTs"), g - 1)
                    for c in range(KH):
                        last = nc.tensor.transpose(bT_ps[:, g % 2, c * P:(c + 1) * P],
                                                   b_sel[:, g % 2, c * P:(c + 1) * P], K["ident"][:, :])
                    last.then_inc(sem("c_bT"), 1)
                    pe.wait_ge(sem("c_bTs"), g + 1)
                    for c in CHUNKS_OF_X:
                        last = nc.tensor.matmul(bx_ps[:, g % 2, 0:2 * P], bT[:, g % 2, c * P:(c + 1) * P],
                                                xT[:, c, g * 2 * P:(g + 1) * 2 * P],
                                                start=(c == CHUNKS_OF_X[0]), stop=(c == CHUNKS_OF_X[-1]))
                    last.then_inc(sem("c_bx"), 1)
                    pe.wait_ge(sem("c_bxs"), g + 1)
                    pe.wait_ge(sem(f"c_asel{g % 2}"), 16 * (g // 2 + 1))
                    for h in range(2):
                        n = 2 * g + h
                        if n >= 2:
                            pe.wait_ge(sem("c_x2s"), n - 1)
                        nc.tensor.matmul(x2_ps[:, h, :], bx[:, g % 2, h * P:(h + 1) * P],
                                         a_sel[:, g % 2, :], start=True, stop=True).then_inc(sem("c_x2"), 1)

            @block.scalar
            def _(act):
                for j in range(8):
                    act.wait_ge(sem("c_aT"), j + 1)
                    if j >= 2:
                        act.wait_ge(sem(f"c_astore{j % 2}"), 16 * (j // 2))
                    nc.scalar.copy(a_rows[:, j % 2, :], t_ps[:, j % 2, :]).then_inc(sem("c_arow"), 1)
                for g in range(NG):
                    act.wait_ge(sem("c_bT"), g + 1)
                    if g >= 2:
                        act.wait_ge(sem("c_bx"), g - 1)
                    nc.scalar.copy(bT[:, g % 2, :], bT_ps[:, g % 2, :]).then_inc(sem("c_bTs"), 1)
                    for h in range(2):
                        n = 2 * g + h
                        act.wait_ge(sem("c_x2"), n + 1)
                        nc.scalar.copy(K["x2"][:, n, :], x2_ps[:, h, :]).then_inc(sem("c_x2s"), 1)

            @block.vector
            def _(dve):
                link = Link(dve, sem("c_link"))
                dve.wait_ge(sem("c_const"), 80)
                link(nc.vector.tensor_copy(idf[:, :, :], ids[:, :, :]))
                link(nc.vector.tensor_tensor(idf[:, :, :], idf[:, :, :],
                                             eight[:, :].unsqueeze(1).to_broadcast([P, NG, GB]), ALU.mult))
                link(nc.vector.tensor_reduce(rowf[:, :], idf[:, :, :], AX_X, ALU.add))
                link(nc.vector.tensor_scalar(rowf[:, :], rowf[:, :], float(RANK), rank_of[:, 0:1],
                                             ALU.mult, ALU.add))
                nc.vector.tensor_copy(row[:, :], rowf[:, :]).then_inc(sem("c_row"), 1)
                for g in range(NG):
                    dve.wait_ge(sem("c_bx"), g + 1)
                    if g >= 2:
                        dve.wait_ge(sem("c_x2"), 2 * (g - 1))
                    nc.vector.tensor_tensor(bx[:, g % 2, :], bx_ps[:, g % 2, 0:2 * P], mine[:, :],
                                            ALU.mult).then_inc(sem("c_bxs"), 1)
                    if g:
                        amax(dve, g - 1)
                amax(dve, NG - 1)
                dve.wait_ge(sem("c_amax"), NT)
                link(nc.vector.tensor_reduce(K["gpart"][:, :],
                                             K["xmax"][:, :, :].rearrange("p t b -> p (t b)"), AX_X, ALU.max))
                nc.vector.tensor_copy(K["gall"][:, :], K["gpart"][:, :]).then_inc(sem("c_gmax"), 1)
                dve.wait_ge(sem("c_gall"), 1)
                global_scale(nc, link, K["gall"][:, :], K["xg"][:, :], K["xrg"][:, 0:1],
                             K["xmax"][:, :, :].rearrange("p t b -> p (t b)"),
                             K["xrs"][:, :, :].rearrange("p t b -> p (t b)"), tmp[:, :])
                link(nc.vector.tensor_scalar(K["half_g"][:, :], K["xg"][:, :], 0.5, None, ALU.mult))
                link(nc.vector.tensor_tensor(K["half_gg"][:, :], K["half_g"][:, :], K["xg"][:, :], ALU.mult))



def global_scale(nc, link, gall, g, rg, amax, rs, t):
    link(nc.vector.tensor_scalar(g, gall, 1.0 / GDIV, 1e-8, ALU.mult, ALU.max))
    link(nc.vector.reciprocal(rg, g))
    link(nc.vector.tensor_scalar(amax, amax, rg, None, ALU.mult))
    fp8_scales(nc, link, amax, rs, t)


def weights(nc, K, I, sem):
    with ExitStack() as ctx:
        sb = lambda n, s, d=F32: ctx.enter_context(nc.sbuf_tensor(n, s, d))
        ps = lambda n, s: ctx.enter_context(nc.psum_tensor(n, s, F32))
        taken = [0]

        def spare(*shape):
            n, a = 1, taken[0]
            for d in shape:
                n *= d
            taken[0] += n
            flat = K["h"][:, :, :].rearrange("p t n -> p (t n)")[:, a:a + n]
            names = "abc"[:len(shape)]
            sizes = dict(zip(names[1:], shape[1:]))
            return flat.rearrange(f"p ({' '.join(names)}) -> p {' '.join(names)}", **sizes)

        guT = spare(2, KH, I_DIM)
        dT = spare(KI, H)
        ri = sb("w_ri", [P, KH], I32)
        rm = sb("w_rm", [P, KI], I32)
        nat = spare(2, H)
        wi = spare(2, H)
        wq = spare(2, H)
        v = spare(1, I_DIM)[:, 0, :]
        am = sb("w_am", [P, I_DIM // BLK])
        s_ = sb("w_s", [P, I_DIM // BLK])
        rs = sb("w_rs", [P, I_DIM // BLK])
        dn = sb("dn", [P, I_DIM])
        dq = sb("dq", [P, I_DIM])
        a_ps = ps("a_ps", [P, 2, H])
        b_ps = ps("b_ps", [P, 2, H])
        d_ps = ps("d_ps", [P, 3 * H])
        tiles = [(m, k) for m in range(2) for k in range(KI)]
        NW = len(tiles)

        with nc.Block() as block:
            @block.sync
            def _(sp):
                sp.dma_start(ri[:, :], I["ri_in"]).then_inc(sem("w_idx"), 16)
                sp.dma_start(rm[:, 0:KI - 1], I["ri_mid"]).then_inc(sem("w_idx"), 16)
                sp.dma_start(rm[0:width(KI - 1), KI - 1:KI],
                             I["ri_tail"]).then_inc(sem("w_idx"), 16)
                for j, (m, k) in enumerate(tiles):
                    w = width(k)
                    sp.wait_ge(sem("w_nat"), j + 1)
                    sp.dma_start(I["w_scratch"][m * I_DIM + k * P:m * I_DIM + k * P + w, :],
                                 nat[0:w, j % 2, :]).then_inc(sem(f"w_store{j % 2}"), 16)

            @block.gpsimd
            def _(pool):
                pool.wait_ge(sem("w_idx"), 48)
                for m, name in enumerate(("wgT", "wuT")):
                    for c in range(KH):
                        nc.gpsimd.indirect_dma_start(
                            guT[:, m, c, :], None, I[name],
                            bass.IndirectOffsetOnAxis(ap=ri[:, c:c + 1], axis=0)).then_inc(sem("w_gu"), 16)
                for k in range(KI):
                    w = width(k)
                    nc.gpsimd.indirect_dma_start(
                        dT[0:w, k, :], None, I["wdT"],
                        bass.IndirectOffsetOnAxis(ap=rm[0:w, k:k + 1], axis=0)).then_inc(sem("w_d"), 16)
                pool.wait_ge(sem("w_store0"), 16 * KI)
                pool.wait_ge(sem("w_store1"), 16 * KI)
                for j, (m, k) in enumerate(tiles):
                    w = width(k)
                    if j >= 2:
                        pool.wait_ge(sem("w_q"), j - 1)
                    nc.gpsimd.indirect_dma_start(
                        wi[0:w, j % 2, :], None, I["w_scratch"],
                        bass.IndirectOffsetOnAxis(ap=rm[0:w, k:k + 1], axis=0),
                        element_offset=m * I_DIM * H).then_inc(sem(f"w_wi{j % 2}"), 16)

            @block.tensor
            def _(pe):
                ident = K["ident"]
                pe.wait_ge(sem("w_gu"), 16 * 2 * KH)
                for j, (m, k) in enumerate(tiles):
                    w = width(k)
                    if j >= 2:
                        pe.wait_ge(sem("w_nat"), j - 1)
                    for c in range(KH):
                        last = nc.tensor.transpose(a_ps[0:w, j % 2, c * P:(c + 1) * P],
                                                   guT[:, m, c, k * P:k * P + w], ident[:, :])
                    last.then_inc(sem("w_aps"), 1)
                pe.wait_ge(sem("w_d"), 16 * KI)
                for n in range(KH):
                    if n:
                        pe.wait_ge(sem("w_dn"), n)
                    for k in range(KI):
                        w = width(k)
                        last = nc.tensor.transpose(d_ps[:, k * P:k * P + w],
                                                   dT[0:w, k, n * P:(n + 1) * P], ident[0:w, 0:w])
                    last.then_inc(sem("w_dps"), 1)
                    pe.wait_ge(sem("w_dq"), n + 1)
                    pe.wait_ge(sem("w_dn"), n + 1)
                    for k in range(KI):
                        w = width(k)
                        last = nc.tensor.transpose(d_ps[0:w, k * P:(k + 1) * P],
                                                   dq[:, k * P:k * P + w], ident[:, :])
                    last.then_inc(sem("w_dtp"), 1)
                    pe.wait_ge(sem("w_dts"), n + 1)
                for j, (m, k) in enumerate(tiles):
                    w = width(k)
                    pe.wait_ge(sem("w_q"), j + 1)
                    if j >= 2:
                        pe.wait_ge(sem("w_bs"), j - 1)
                    for c in range(KH):
                        last = nc.tensor.transpose(b_ps[:, j % 2, c * P:c * P + w],
                                                   wq[0:w, j % 2, c * P:(c + 1) * P], ident[0:w, 0:w])
                    last.then_inc(sem("w_bps"), 1)

            @block.scalar
            def _(act):
                for j, (m, k) in enumerate(tiles):
                    w = width(k)
                    act.wait_ge(sem("w_aps"), j + 1)
                    if j >= 2:
                        act.wait_ge(sem(f"w_store{j % 2}"), 16 * (j // 2))
                    nc.scalar.copy(nat[0:w, j % 2, :], a_ps[0:w, j % 2, :]).then_inc(sem("w_nat"), 1)
                for n in range(KH):
                    act.wait_ge(sem("w_dps"), n + 1)
                    if n:
                        act.wait_ge(sem("w_dq"), n)
                    nc.scalar.copy(dn[:, :], d_ps[:, 0:I_DIM]).then_inc(sem("w_dn"), 1)
                    act.wait_ge(sem("w_dtp"), n + 1)
                    nc.scalar.copy(K["wdT"][:, 0:KI - 1, n * P:(n + 1) * P],
                                   d_ps[:, 0:(KI - 1) * P].rearrange("p (k o) -> p k o", o=P))
                    w = width(KI - 1)
                    nc.scalar.copy(K["wdT"][0:w, KI - 1, n * P:(n + 1) * P],
                                   d_ps[0:w, (KI - 1) * P:KI * P]).then_inc(sem("w_dts"), 1)
                for j, (m, k) in enumerate(tiles):
                    w = width(k)
                    act.wait_ge(sem("w_bps"), j + 1)
                    nc.scalar.copy(K["wguT"][:, m, :, k * P:k * P + w],
                                   b_ps[:, j % 2, :].rearrange("p (c i) -> p c i", i=P)[:, :, 0:w]
                                   ).then_inc(sem("w_bs"), 1)

            @block.vector
            def _(dve):
                link = Link(dve, sem("w_link"))
                for n in range(KH):
                    dve.wait_ge(sem("w_dn"), n + 1)
                    if n:
                        dve.wait_ge(sem("w_dtp"), n)
                    nb = I_DIM // BLK
                    int4_quantise(nc, link, dn[:, :], v[:, :], am[:, :], s_[:, :], rs[:, :], dq[:, :],
                                  nb).then_inc(sem("w_dq"), 1)
                for j, (m, k) in enumerate(tiles):
                    w = width(k)
                    nb = H // BLK
                    dve.wait_ge(sem(f"w_wi{j % 2}"), 16 * (j // 2 + 1))
                    if j >= 2:
                        dve.wait_ge(sem("w_bps"), j - 1)
                    int4_quantise(nc, link, wi[0:w, j % 2, :], v[0:w, 0:H], am[0:w, 0:nb], s_[0:w, 0:nb],
                                  rs[0:w, 0:nb], wq[0:w, j % 2, :], nb).then_inc(sem("w_q"), 1)


def gate_up(nc, K, I, sem):
    NP_ = len(PIECES)
    with ExitStack() as ctx:
        sb = lambda n, s, d=F32: ctx.enter_context(nc.sbuf_tensor(n, s, d))
        ps = lambda n, s: ctx.enter_context(nc.psum_tensor(n, s, F32))
        v, c = sb("g_v", [P, H]), sb("g_c", [P, H])
        aq = sb("g_aq", [P, H])
        aT = sb("g_aT", [P, 2, H])
        s2, rs2, am2 = sb("g_s2", [P, 8]), sb("g_rs2", [P, 8]), sb("g_am2", [P, 8])
        r = sb("g_r", [P, SELECT])
        sg = sb("g_sg", [P, 2, 352])
        gate_ps, up_ps = ps("gate_ps", [P, 2, H]), ps("up_ps", [P, 2, H])
        aT_ps = ps("aT_ps", [P, H])

        def guarded(eng, name, value, first):
            if not first or value > 0:
                eng.wait_ge(sem(name), value)

        def pe_transpose(pe, i):
            pe.wait_ge(sem("g_aq"), i + 1)
            for k in range(KH):
                last = nc.tensor.transpose(aT_ps[:, k * P:(k + 1) * P], aq[:, k * P:(k + 1) * P],
                                           K["ident"][:, :])
            last.then_inc(sem("g_aT"), 1)

        def pe_tile(pe, i, slot, first=False, last_tile=False):
            for p, (o, w) in enumerate(PIECES):
                if p == NP_ - 1 and not last_tile:
                    pe_transpose(pe, i + 1)
                if p == 0:
                    pe.wait_ge(sem("g_aTs"), i + 1)
                guarded(pe, "g_h", NP_ * i + p - 1, first)
                for m, dst in enumerate((gate_ps, up_ps)):
                    for k in range(KH):
                        last = nc.tensor.matmul(dst[:, p % 2, 0:w], aT[:, slot, k * P:(k + 1) * P],
                                                K["wguT"][:, m, k, o:o + w],
                                                start=(k == 0), stop=(k == KH - 1))
                last.then_inc(sem("g_mm"), 1)

        def act_evac(act, i, slot, first=False):
            act.wait_ge(sem("g_aT"), i + 1)
            if not first:
                act.wait_ge(sem("g_mm"), NP_ * (i - 1))
            nc.scalar.copy(aT[:, slot, :], aT_ps[:, :]).then_inc(sem("g_aTs"), 1)

        def act_tile(act, i, slot, first=False, last_tile=False):
            for p, (o, w) in enumerate(PIECES):
                if p == NP_ - 1 and not last_tile:
                    act_evac(act, i + 1, 1 - slot, first)
                act.wait_ge(sem("g_mm"), NP_ * i + p + 1)
                guarded(act, "g_h", NP_ * i + p - 1, first)
                nc.scalar.activation(sg[:, p % 2, 0:w], gate_ps[:, p % 2, 0:w], ACT.Tanh,
                                     scale=K["half_g"][:, 0:1]).then_inc(
                    sem("g_tanh"), 1)

        def dve_quantise(dve, i, first=False):
            link = Link(dve, sem("g_link"), i * (FP8_LINKS))
            gate = None if first else (lambda: dve.wait_ge(sem("g_aT"), i))
            x = K["x2"][:, bass.ds(i, 1), :].squeeze(1)
            fp8_quantise(nc, link, x, K["xrg"][:, 0:1], K["xmax"][:, bass.ds(i, 1), :].squeeze(1),
                         K["xrs"][:, bass.ds(i, 1), :].squeeze(1), aq[:, :], v[:, :], c[:, :],
                         s2[:, :], rs2[:, :], am2[:, :], r[:, :], H, gate).then_inc(sem("g_aq"), 1)
            assert link.n == FP8_LINKS

        def dve_tile(dve, i, last_tile=False):
            if not last_tile:
                dve_quantise(dve, i + 1)
            for p, (o, w) in enumerate(PIECES):
                dve.wait_ge(sem("g_tanh"), NP_ * i + p + 1)
                h = K["h"][:, bass.ds(i, 1), o:o + w].squeeze(1)
                nc.vector.scalar_tensor_tensor(h, sg[:, p % 2, 0:w], 1.0, gate_ps[:, p % 2, 0:w],
                                               ALU.add, ALU.mult).then_inc(sem("g_silu"), 1)
                dve.wait_ge(sem("g_silu"), NP_ * i + p + 1)
                nc.vector.scalar_tensor_tensor(h, h, K["half_gg"][:, 0:1], up_ps[:, p % 2, 0:w], ALU.mult,
                                               ALU.mult).then_inc(sem("g_h"), 1)
                dve.wait_ge(sem("g_h"), NP_ * i + p + 1)
                nc.vector.tensor_reduce(
                    K["hmax"][:, bass.ds(i, 1), o // BLK:(o + w) // BLK].squeeze(1), blocks(h), AX_X,
                    ALU.max, apply_absolute_value=True).then_inc(sem("g_hmax"), 1)

        with nc.Block() as block:
            @block.tensor
            def _(pe):
                pe_transpose(pe, 0)
                pe_tile(pe, 0, 0, first=True)
                with pe.Fori(0, NT // 2 - 1) as j:
                    pe_tile(pe, 2 * j + 1, 1)
                    pe_tile(pe, 2 * j + 2, 0)
                pe_tile(pe, NT - 1, 1, last_tile=True)

            @block.scalar
            def _(act):
                act_evac(act, 0, 0, first=True)
                act_tile(act, 0, 0, first=True)
                with act.Fori(0, NT // 2 - 1) as j:
                    act_tile(act, 2 * j + 1, 1)
                    act_tile(act, 2 * j + 2, 0)
                act_tile(act, NT - 1, 1, last_tile=True)

            @block.vector
            def _(dve):
                dve_quantise(dve, 0, first=True)
                with dve.Fori(0, NT - 1) as i:
                    dve_tile(dve, i)
                dve_tile(dve, NT - 1, last_tile=True)
                link = Link(dve, sem("g_link2"))
                dve.wait_ge(sem("g_hmax"), NT * NP_)
                link(nc.vector.tensor_reduce(K["gpart"][:, :],
                                             K["hmax"][:, :, :].rearrange("p t b -> p (t b)"), AX_X, ALU.max))
                nc.vector.tensor_copy(K["gall"][:, :], K["gpart"][:, :]).then_inc(sem("g_gmax"), 1)
                dve.wait_ge(sem("g_gall"), 1)

            @block.gpsimd
            def _(pool):
                pool.wait_ge(sem("g_gmax"), 1)
                nc.gpsimd.partition_all_reduce(K["gall"][:, :], K["gpart"][:, :], P, RMAX).then_inc(
                    sem("g_gall"), 1)


def down(nc, K, I, sem):
    with ExitStack() as ctx:
        sb = lambda n, s, d=F32: ctx.enter_context(nc.sbuf_tensor(n, s, d))
        ps = lambda n, s: ctx.enter_context(nc.psum_tensor(n, s, F32))
        v, c, hq = sb("d_v", [P, I_DIM]), sb("d_c", [P, I_DIM]), sb("d_hq", [P, I_DIM])
        hT = sb("d_hT", [P, KI * P])
        NB = I_DIM // BLK
        hrs, tmp = sb("d_hrs", [P, NT, NB]), sb("d_tmp", [P, NT * NB])
        s2, rs2, am2 = sb("d_s2", [P, 8]), sb("d_rs2", [P, 8]), sb("d_am2", [P, 8])
        r = sb("d_r", [P, SELECT])
        x1s = sb("x1s", [P, H])
        xt = sb("d_xt", [P, H])
        hT_ps = ps("hT_ps", [P, 3 * H])
        y_ps = ps("y_ps", [P, H])
        xT_ps = ps("xT_ps", [P, H])
        WL = width(KI - 1)

        def pe_down(pe, i):
            pe.wait_ge(sem("d_hq"), i + 1)
            for k in range(KI):
                w = width(k)
                last = nc.tensor.transpose(hT_ps[0:w, k * P:(k + 1) * P], hq[:, k * P:k * P + w],
                                           K["ident"][:, :])
            last.then_inc(sem("d_hT"), 1)
            pe.wait_ge(sem("d_hTs"), 2 * (i + 1))
            for k in range(KI):
                w = width(k)
                last = nc.tensor.matmul(y_ps[:, :], hT[0:w, k * P:(k + 1) * P], K["wdT"][0:w, k, :],
                                        start=(k == 0), stop=(k == KI - 1))
            last.then_inc(sem("d_y"), 1)

        def pe_x1(pe, i, first=False):
            pe.wait_ge(sem("d_x1"), i + 1)
            if not first:
                pe.wait_ge(sem("d_xTs"), i)
            for k in range(KH):
                last = nc.tensor.transpose(xT_ps[:, k * P:(k + 1) * P], x1s[:, k * P:(k + 1) * P],
                                           K["ident"][:, :])
            last.then_inc(sem("d_xT"), 1)

        def act_down(act, i):
            act.wait_ge(sem("d_hT"), i + 1)
            nc.scalar.copy(hT[:, 0:(KI - 1) * P], hT_ps[:, 0:(KI - 1) * P]).then_inc(sem("d_hTs"), 1)
            nc.scalar.copy(hT[0:WL, (KI - 1) * P:KI * P], hT_ps[0:WL, (KI - 1) * P:KI * P]).then_inc(
                sem("d_hTs"), 1)

        def act_x1(act, i):
            act.wait_ge(sem("d_xT"), i + 1)
            nc.scalar.copy(K["x1T"][:, :, bass.ds(i * P, P)],
                           xT_ps[:, :].rearrange("p (c t) -> p c t", t=P)).then_inc(sem("d_xTs"), 1)

        def dve_quantise(dve, i, first=False):
            link = Link(dve, sem("d_link"), i * FP8_LINKS)
            gate = None if first else (lambda: dve.wait_ge(sem("d_hT"), i))
            fp8_quantise(nc, link, K["h"][:, bass.ds(i, 1), :].squeeze(1), K["hrg"][:, 0:1],
                         K["hmax"][:, bass.ds(i, 1), :].squeeze(1), hrs[:, bass.ds(i, 1), :].squeeze(1),
                         hq[:, :], v[:, :], c[:, :], s2[:, :], rs2[:, :], am2[:, :], r[:, :],
                         I_DIM, gate).then_inc(sem("d_hq"), 1)

        def dve_x1(dve, i, first=False):
            dve.wait_ge(sem("d_y"), i + 1)
            if not first:
                dve.wait_ge(sem("d_xT"), i)
                dve.wait_ge(sem("d_store"), 16 * i)
            dve.wait_ge(sem("d_x"), 16 * (i + 1))
            nc.vector.scalar_tensor_tensor(x1s[:, :], y_ps[:, :], K["hg"][:, 0:1], xt[:, :], ALU.mult,
                                           ALU.add).then_inc(sem("d_x1"), 1)

        with nc.Block() as block:
            @block.sync
            def _(sp):
                with sp.Fori(0, NT) as i:
                    sp.dma_start(xt[:, :], I["x"][bass.ds(i * P, P), :]).then_inc(sem("d_x"), 16)
                    sp.wait_ge(sem("d_x1"), i + 1)
                    sp.dma_start(I["x1_scratch"][bass.ds(i * P, P), :], x1s[:, :]).then_inc(
                        sem("d_store"), 16)
                sp.wait_ge(sem("d_store"), 16 * NT)

            @block.tensor
            def _(pe):
                pe_down(pe, 0)
                pe_x1(pe, 0, first=True)
                pe_down(pe, 1)
                with pe.Fori(2, NT) as i:
                    pe_x1(pe, i - 1)
                    pe_down(pe, i)
                pe_x1(pe, NT - 1)

            @block.scalar
            def _(act):
                act_down(act, 0)
                with act.Fori(1, NT) as i:
                    act_x1(act, i - 1)
                    act_down(act, i)
                act_x1(act, NT - 1)

            @block.vector
            def _(dve):
                global_scale(nc, Link(dve, sem("d_scale")), K["gall"][:, :], K["hg"][:, :],
                             K["hrg"][:, 0:1], K["hmax"][:, :, :].rearrange("p t b -> p (t b)"),
                             hrs[:, :, :].rearrange("p t b -> p (t b)"), tmp[:, :])
                dve_quantise(dve, 0, first=True)
                dve_quantise(dve, 1)
                dve_x1(dve, 0, first=True)
                with dve.Fori(2, NT) as i:
                    dve_quantise(dve, i)
                    dve_x1(dve, i - 1)
                dve_x1(dve, NT - 1)


TWO_PI = 6.283185307179586
C1 = 6.28125
C2 = 0.0019350051879882812
C3 = TWO_PI - C1 - C2


def project(nc, K, I, sem):
    NQ = HQ * D // H
    NK = HK * D // H
    NGR = NQ + 2 * NK
    HEADS = HQ + HK
    HPG = H // D
    with ExitStack() as ctx:
        sb = lambda n, s, d=F32: ctx.enter_context(nc.sbuf_tensor(n, s, d))
        ps = lambda n, s: ctx.enter_context(nc.psum_tensor(n, s, F32))
        w = sb("p_w", [P, KH, NGR * H])
        raw = sb("p_raw", [P, 2, HEADS * D])
        val = sb("p_val", [P, HK * D])
        sq = sb("p_sq", [P, 2, H])
        xs = sb("p_xs", [P, 2, H])
        rot = sb("p_rot", [P, 16 * D])
        cos, sin = sb("p_cos", [P, NT, D // 2]), sb("p_sin", [P, NT, D // 2])
        tab = sb("p_tab", [P, 4, D])
        nw = sb("p_nw", [P, 2, D])
        nws = sb("p_nws", [P, 2, D])
        ss, sd, y, t = (sb("p_" + n, [P, HEADS]) for n in ("ss", "sd", "y", "t"))
        pos = sb("p_pos", [P, NT])
        in_req = sb("p_in_req", [P, 1])
        invf = sb("p_invf", [P, D // 2])
        g_ps = ps("p_ps", [P, 4, H])

        def pe_tile(pe, i, slot, first=False):
            pe.wait_ge(sem("p_xs"), i + 1)
            for n in range(NGR):
                if not (first and n < 4):
                    pe.wait_ge(sem("p_read"), NGR * i + n - 3)
                for k in range(KH):
                    last = nc.tensor.matmul(g_ps[:, n % 4, :], xs[:, slot, k * P:(k + 1) * P],
                                            w[:, k, n * H:(n + 1) * H], start=(k == 0), stop=(k == KH - 1))
                last.then_inc(sem("p_mm"), 1)

        def act_tile(act, i, slot, turn):
            static = isinstance(turn, int)
            for n in range(NGR):
                act.wait_ge(sem("p_mm"), NGR * i + n + 1)
                src = g_ps[:, n % 4, :]
                if n < NQ + NK:
                    if not (static and i == 0 and n < 2):
                        act.wait_ge(sem("p_ss"), (NQ + NK) * i + n - 1)
                    nc.scalar.activation(sq[:, n % 2, :], src, ACT.Square).then_inc(sem("p_sq"), 1)
                    if n == 0 and not static:
                        act.wait_ge(sem(f"p_store{slot}"), 32 * turn)
                    nc.scalar.copy(raw[:, slot, n * H:(n + 1) * H], src).then_inc(sem("p_read"), 1)
                else:
                    if n == NQ + NK and not (static and i == 0):
                        act.wait_ge(sem("p_vstore"), 16 * i)
                    j = n - NQ - NK
                    nc.scalar.copy(val[:, j * H:(j + 1) * H], src).then_inc(sem("p_read"), 1)
            act.wait_ge(sem("p_ms"), i + 1)
            nc.scalar.activation(sd[:, :], ss[:, :], ACT.Sqrt).then_inc(sem("p_sd"), 1)

        def dve_tile(dve, i, slot, links):
            link = Link(dve, sem("p_link"), links * i)
            for q in range(2):
                for a, (base, wt) in enumerate(((cos, nw), (sin, nws))):
                    link(nc.vector.tensor_tensor(
                        tab[:, 2 * q + a, :].rearrange("p (h f) -> p h f", h=2),
                        wt[:, q, :].rearrange("p (h f) -> p h f", h=2),
                        base[:, bass.ds(i, 1), :].to_broadcast([P, 2, D // 2]), ALU.mult))
            for n in range(NQ + NK):
                dve.wait_ge(sem("p_sq"), (NQ + NK) * i + n + 1)
                nc.vector.tensor_reduce(ss[:, n * HPG:(n + 1) * HPG],
                                        sq[:, n % 2, :].rearrange("p (h d) -> p h d", d=D), AX_X,
                                        ALU.add).then_inc(sem("p_ss"), 1)
            dve.wait_ge(sem("p_ss"), (NQ + NK) * (i + 1))
            nc.vector.tensor_scalar(ss[:, :], ss[:, :], 1.0 / D, EPS, ALU.mult, ALU.add).then_inc(
                sem("p_ms"), 1)
            dve.wait_ge(sem("p_sd"), i + 1)
            link(nc.vector.reciprocal(y[:, :], sd[:, :]))
            link(nc.vector.tensor_tensor(t[:, :], y[:, :], y[:, :], ALU.mult))
            link(nc.vector.tensor_tensor(t[:, :], t[:, :], ss[:, :], ALU.mult))
            link(nc.vector.tensor_scalar(t[:, :], t[:, :], -0.5, 1.5, ALU.mult, ALU.add))
            link(nc.vector.tensor_tensor(y[:, :], y[:, :], t[:, :], ALU.mult))
            link(nc.vector.tensor_scalar(y[:, 0:HQ], y[:, 0:HQ], -SCALE, None, ALU.mult))
            dve.wait_ge(sem("p_read"), NGR * i + NQ + NK)
            for h0, nh, q in ((0, 16, 0), (16, 16, 0), (HQ, HK, 1)):
                x = raw[:, slot, h0 * D:(h0 + nh) * D].rearrange("p (h d) -> p h d", d=D)
                o = rot[:, 0:nh * D].rearrange("p (h d) -> p h d", d=D)
                over = lambda a, n: a.unsqueeze(1).to_broadcast([P, nh, n])
                half = D // 2
                c_, s_ = tab[:, 2 * q, :], tab[:, 2 * q + 1, :]
                nc.vector.tensor_tensor(o[:, :, 0:half], x[:, :, half:D], over(s_[:, 0:half], half), ALU.mult
                                        ).then_inc(sem("p_link"), 1)
                link.n += 1
                link(nc.vector.tensor_tensor(o[:, :, half:D], x[:, :, 0:half], over(s_[:, half:D], half),
                                             ALU.mult))
                link(nc.vector.tensor_tensor(x, x, over(c_, D), ALU.mult))
                link(nc.vector.tensor_tensor(x, x, o, ALU.add))
                last = nc.vector.tensor_tensor(
                    x, x, y[:, h0:h0 + nh].unsqueeze(2).to_broadcast([P, nh, D]), ALU.mult)
                last.then_inc(sem("p_out"), 1)
            return link.n

        PROJ_LINKS = 4 + 6 + 3 * 4

        with nc.Block() as block:
            @block.sync
            def _(sp):
                sp.dma_start(w[:, :, :], I["wqkvT"].rearrange("(c p) n -> p c n", p=P)).then_inc(
                    sem("p_w"), 16)
                for n, (dst, src) in enumerate((
                        (K["lens_i"][:, :], I["lens"].partition_broadcast(P)),
                        (in_req[:, :], I["in_req"]),
                        (invf[:, :], I["invf"].partition_broadcast(P)),
                        (nw[:, 0, :], I["qw"].partition_broadcast(P)),
                        (nw[:, 1, :], I["kw"].partition_broadcast(P)))):
                    sp.dma_start(dst, src).then_inc(sem("p_const"), 16)
                with sp.Fori(0, NT // 2) as j:
                    for slot in range(2):
                        i = 2 * j + slot
                        rows = bass.ds(i * P, P)
                        sp.wait_ge(sem("p_read"), NGR * (i + 1))
                        sp.dma_start(I["v_scratch"][rows, :], val[:, :]).then_inc(sem("p_vstore"), 16)
                        sp.wait_ge(sem("p_out"), 3 * (i + 1))
                        sp.dma_start(I["q_scratch"][rows, :], raw[:, slot, 0:HQ * D]).then_inc(
                            sem(f"p_store{slot}"), 16)
                        sp.dma_start(I["k_scratch"][rows, :], raw[:, slot, HQ * D:]).then_inc(
                            sem(f"p_store{slot}"), 16)
                sp.wait_ge(sem("p_vstore"), 16 * NT)
                sp.wait_ge(sem("p_store0"), 16 * NT)
                sp.wait_ge(sem("p_store1"), 16 * NT)

            @block.tensor
            def _(pe):
                pe.wait_ge(sem("p_w"), 16)
                pe_tile(pe, 0, 0, first=True)
                pe_tile(pe, 1, 1)
                with pe.Fori(1, NT // 2) as j:
                    pe_tile(pe, 2 * j, 0)
                    pe_tile(pe, 2 * j + 1, 1)

            @block.scalar
            def _(act):
                act.wait_ge(sem("p_angle"), 1)
                nc.scalar.activation(sin[:, :, :], sin[:, :, :], ACT.Sin).then_inc(sem("p_trig"), 1)
                nc.scalar.activation(cos[:, :, :], cos[:, :, :], ACT.Sin).then_inc(sem("p_trig"), 1)
                act_tile(act, 0, 0, 0)
                act_tile(act, 1, 1, 0)
                with act.Fori(1, NT // 2) as j:
                    for slot in range(2):
                        act_tile(act, 2 * j + slot, slot, j)

            @block.vector
            def _(dve):
                link = Link(dve, sem("p_link0"))
                lens = K["lens"]
                dve.wait_ge(sem("p_const"), 80)
                link(nc.vector.tensor_copy(lens[:, :], K["lens_i"][:, :]))
                for q in range(BT):
                    rows = slice(q * S, (q + 1) * S)
                    nc.vector.tensor_copy(
                        pos[rows, :], lens[rows, :].rearrange("p (t q) -> p t q", q=BT)[:, :, q]
                    ).then_inc(sem("p_pos"), 1)
                dve.wait_ge(sem("p_pos"), BT)
                link(nc.vector.tensor_scalar(pos[:, :], pos[:, :], in_req[:, 0:1], None, ALU.add))
                for q in range(2):
                    link(nc.vector.tensor_scalar(nws[:, q, 0:D // 2], nw[:, q, D // 2:D], -1.0, None,
                                                 ALU.mult))
                    link(nc.vector.tensor_copy(nws[:, q, D // 2:D], nw[:, q, 0:D // 2]))
                f = raw[:, 0, 0:NT * D // 2].rearrange("p (t f) -> p t f", f=D // 2)
                k_ = raw[:, 0, NT * D // 2:NT * D].rearrange("p (t f) -> p t f", f=D // 2)
                link(nc.vector.tensor_tensor(
                    f, pos[:, :].unsqueeze(2).to_broadcast([P, NT, D // 2]),
                    invf[:, :].unsqueeze(1).to_broadcast([P, NT, D // 2]), ALU.mult))
                link(nc.vector.tensor_scalar(k_, f, 1.0 / TWO_PI, MAGIC_INT, ALU.mult, ALU.add))
                link(nc.vector.tensor_scalar(k_, k_, MAGIC_INT, None, ALU.subtract))
                for part in (C1, C2, C3):
                    link(nc.vector.scalar_tensor_tensor(f, k_, -part, f, ALU.mult, ALU.add))
                link(nc.vector.tensor_scalar(sin[:, :, :], f, 3.1415925, -3.1415925, ALU.min, ALU.max))
                link(nc.vector.tensor_scalar(cos[:, :, :].bitcast(I32), sin[:, :, :].bitcast(I32), 0x7FFFFFFF,
                                             None, ALU.bitwise_and))
                nc.vector.tensor_scalar(cos[:, :, :], cos[:, :, :], -1.0, TWO_PI / 4, ALU.mult, ALU.add
                                        ).then_inc(sem("p_angle"), 1)
                dve.wait_ge(sem("p_trig"), 2)
                def stage_x(i, slot):
                    nc.vector.tensor_copy(xs[:, slot, :].rearrange("p (c t) -> p c t", t=P),
                                          K["x1T"][:, :, bass.ds(i * P, P)]).then_inc(sem("p_xs"), 1)

                def tile(i, slot, first=False, more=True):
                    if more:
                        if not first:
                            dve.wait_ge(sem("p_mm"), NGR * i)
                        stage_x(i + 1, 1 - slot)
                    n = dve_tile(dve, i, slot, PROJ_LINKS)
                    assert n == PROJ_LINKS, n

                stage_x(0, 0)
                tile(0, 0, first=True)
                tile(1, 1)
                with dve.Fori(1, NT // 2 - 1) as j:
                    tile(2 * j, 0)
                    tile(2 * j + 1, 1)
                tile(NT - 2, 0)
                tile(NT - 1, 1, more=False)


def attention(nc, K, I, sem):
    PAIRS = BT * HK
    UG = HK // 2
    UNITS = PAIRS // UG
    UW = UG * D
    W1 = LC + S
    with ExitStack() as ctx:
        sb = lambda n, s, d=F32: ctx.enter_context(nc.sbuf_tensor(n, s, d))
        ps = lambda n, s: ctx.enter_context(nc.psum_tensor(n, s, F32))
        kT = [sb(f"kT{n}", [P, NPP, HK * PSIZE]) for n in range(2)]
        vc = [sb(f"vc{n}", [P, KC, HK * D]) for n in range(2)]
        kn = [sb(f"kn{n}", [S, UW]) for n in range(2)]
        vn = [sb(f"vn{n}", [S, UW]) for n in range(2)]
        qu = [sb(f"qu{n}", [P, UW]) for n in range(2)]
        woT = sb("woT", [P, HQ, H])
        oT = sb("oT", [P, HQ, P])
        qT = sb("qT", [P, 2, P + S])
        sc = sb("sc", [P, 2, W1])
        pr = sb("pr", [P, 2, W1])
        pT = sb("pT", [P, 2, (KC + 1) * P])
        mask = sb("mask", [P, S + LC + S])
        key = sb("key", [P, LC])
        mneg, rsum, rinv = sb("mneg", [P, 2]), sb("rsum", [P, 2]), sb("rinv", [P, 2])
        bt_i = sc[:, :, :].rearrange("p a b -> p (a b)")[:, 0:B * NPP].bitcast(I32)
        bt_f = pr[:, :, :].rearrange("p a b -> p (a b)")[:, 0:B * NPP]
        k_rows, v_rows = sb("k_rows", [P, B * NPP], U32), sb("v_rows", [P, B * KC], U32)
        k_idx, v_idx = sb("k_idx", [P, BT * NPP], U32), sb("v_idx", [P, BT * KC], U32)
        in_page, part = sb("in_page", [P, 1]), sb("part", [P, 1])
        lin = sb("lin", [P, KH, H])
        ag = sb("ag", [P, KH, LMAX + NROUTE])
        bl = sb("bl", [LMAX, H])
        bias = sb("bias", [P, H])
        gb = sb("gb", [P, LMAX + NROUTE])
        yt, yT, x1t, res = sb("yt", [P, H]), sb("yT", [P, H]), sb("x1t", [P, H]), sb("res", [P, H])
        u, um, uT = sb("u", [P, LMAX + NROUTE]), sb("um", [P, LMAX]), sb("uT", [LMAX, P])
        rmax, low = sb("rmax", [P, 1]), sb("low", [P, NROUTE])
        s_ps = ps("s_ps", [P, 3 * H])
        cached = (s_ps[:, 0:LC], s_ps[:, 2 * H:2 * H + LC])
        new = (s_ps[:, H:H + S], s_ps[:, 2 * H - S:2 * H])
        scores = (s_ps[:, 0:W1], s_ps[:, 2 * H - S:2 * H + LC])
        masks = (mask[:, S:S + W1], mask[:, 0:W1])
        at_cached, at_new = (0, S), (LC, 0)
        q_ps = ps("q_ps", [P, H])
        pn_ps = q_ps[0:S, 256:256 + P]
        pT_ps = ps("pT_ps", [P, H])
        o_ps = ps("o_ps", [P, P])
        wo_ps = ps("wo_ps", [P, H])
        z_ps = ps("z_ps", [P, H])
        ident = K["ident"]

        def stages(k, first, last):
            pairs = [k - d for d in range(5)]
            return [p if (p < 0 or not last) and (p >= 0 or not first) else None for p in pairs]

        def base(i, first):
            def wait(eng, name, value):
                if first and value <= 0:
                    return
                eng.wait_ge(sem(name), i * PAIRS + value)
            return wait

        def place(pair):
            pair %= PAIRS
            return pair % HK, (pair // UG) % 2, (pair // HK) % 2, pair // HK

        def loads(i, pair):
            tile = i if pair >= 0 else i - 1
            pair %= PAIRS
            return (tile * (UNITS // 2) + pair // UG // 2 + 1, tile * (BT // 2) + pair // HK // 2 + 1)

        def pe_step(pe, i, k, first, last):
            wait = base(i, first)
            t, s, _, pt, pv = stages(k, first, last)
            if t is not None:
                g, un, _, _ = place(t)
                cols = slice(g % UG * D, (g % UG + 1) * D)
                if g % UG == 0:
                    pe.wait_ge(sem(f"a_q{un}"), 16 * (REP + 1) * loads(i, t)[0])
                wait(pe, "a_qTs", t)
                wait(pe, "a_pns", t - 3)
                nc.tensor.transpose(q_ps[:, 0:P], qu[un][:, cols], ident[:, :])
                nc.tensor.transpose(q_ps[:, P:P + S], kn[un][:, cols], ident[0:S, 0:S]).then_inc(
                    sem("a_qT"), 1)
            if pt is not None:
                wait(pe, "a_pr", pt + 1)
                if t is None:
                    wait(pe, "a_qTs", 0)
                    wait(pe, "a_pns", pt)
                o = at_new[pt % 2]
                nc.tensor.transpose(pn_ps, pr[:, pt % 2, o:o + S], ident[:, :]).then_inc(sem("a_pn"), 1)
                wait(pe, "a_pTs", pt)
                o = at_cached[pt % 2]
                for c in range(KC):
                    done = nc.tensor.transpose(pT_ps[:, c * P:(c + 1) * P],
                                               pr[:, pt % 2, o + c * P:o + (c + 1) * P], ident[:, :])
                done.then_inc(sem("a_pT"), 1)
            if s is not None:
                g, _, rq, _ = place(s)
                if g == 0:
                    pe.wait_ge(sem(f"a_k{rq}"), 16 * NPP * loads(i, s)[1])
                wait(pe, "a_qTs", s + 1)
                wait(pe, "a_max", s - 1)
                nc.tensor.matmul(cached[s % 2], qT[:, s % 2, 0:P],
                                 kT[rq][:, :, g * PSIZE:(g + 1) * PSIZE], start=True, stop=True)
                wait(pe, "a_max", s)
                nc.tensor.matmul(new[s % 2], qT[:, s % 2, 0:P], qT[:, s % 2, P:P + S],
                                 start=True, stop=True).then_inc(sem("a_s"), 1)
            if pv is not None:
                g, un, rq, _ = place(pv)
                if g == 0:
                    pe.wait_ge(sem(f"a_v{rq}"), 16 * KC * loads(i, pv)[1])
                if g % UG == 0:
                    pe.wait_ge(sem(f"a_vn{un}"), 16 * loads(i, pv)[0])
                wait(pe, "a_pTs", pv + 1)
                wait(pe, "a_pns", pv + 1)
                wait(pe, "a_oTs", pv)
                for c in range(KC):
                    nc.tensor.matmul(o_ps[:, :], vc[rq][:, c, g * D:(g + 1) * D],
                                     pT[:, pv % 2, c * P:(c + 1) * P], start=(c == 0), stop=False)
                nc.tensor.matmul(o_ps[:, :], vn[un][:, g % UG * D:(g % UG + 1) * D],
                                 pT[0:S, pv % 2, KC * P:(KC + 1) * P],
                                 start=False, stop=True).then_inc(sem("a_o"), 1)

        def pe_last_tile(pe, i, k, again):
            if k < HK:
                pe.wait_ge(sem("a_oTs"), i * PAIRS - HK + k + 1)
                for r in range(REP):
                    h = REP * k + r
                    done = nc.tensor.matmul(wo_ps[:, :], oT[:, h, :], woT[:, h, :],
                                            start=(h == 0), stop=(h == HQ - 1))
                done.then_inc(sem("a_wo"), 1)
            elif k == HK + 1:
                pe.wait_ge(sem("a_y"), i)
                for c in range(KH):
                    done = nc.tensor.transpose(wo_ps[:, c * P:(c + 1) * P], yt[:, c * P:(c + 1) * P],
                                               ident[:, :])
                done.then_inc(sem("a_yT"), 1)
            elif k == HK + 2:
                pe.wait_ge(sem("a_yTs"), i)
                for c in range(KH):
                    done = nc.tensor.matmul(wo_ps[:, 0:LMAX + NROUTE], yT[:, c * P:(c + 1) * P], ag[:, c, :],
                                            start=(c == 0), stop=(c == KH - 1))
                done.then_inc(sem("a_u"), 1)
                if again:
                    pe.wait_ge(sem("a_res"), 2 * (i - 1))
                for c in range(KH):
                    nc.tensor.matmul(z_ps[:, :], yT[:, c * P:(c + 1) * P], lin[:, c, :],
                                     start=(c == 0), stop=False)
            elif k == HK + 4:
                pe.wait_ge(sem("a_um"), i)
                hold(pe, sem("a_passed"))
                nc.tensor.transpose(wo_ps[0:LMAX, 0:P], um[:, :], ident[:, :]).then_inc(sem("a_uT"), 1)
            elif k == HK + 5:
                pe.wait_ge(sem("a_uTs"), i)
                nc.tensor.matmul(z_ps[:, :], uT[:, :], bl[:, :], start=False, stop=True).then_inc(
                    sem("a_z"), 1)

        def act_step(act, i, k, first, last):
            wait = base(i, first)
            t, s, _, pt, pv = stages(k, first, last)
            if pt is not None:
                wait(act, "a_pn", pt + 1)
            if t is not None:
                wait(act, "a_qT", t + 1)
                wait(act, "a_s", t - 1)
                nc.scalar.copy(qT[:, t % 2, :], q_ps[:, 0:P + S]).then_inc(sem("a_qTs"), 1)
            if pt is not None:
                wait(act, "a_o", pt - 1)
                nc.scalar.copy(pT[0:S, pt % 2, KC * P:(KC + 1) * P], pn_ps).then_inc(sem("a_pns"), 1)
            if s is not None:
                wait(act, "a_max", s + 1)
                wait(act, "a_pT", s - 1)
                nc.scalar.activation(pr[:, s % 2, :], sc[:, s % 2, :], ACT.Exp, scale=-1.0,
                                     bias=mneg[:, s % 2:s % 2 + 1],
                                     accum_out=rsum[:, s % 2:s % 2 + 1]).then_inc(sem("a_exp"), 1)
            if pv is not None:
                g, _, _, b = place(pv)
                wait(act, "a_o", pv + 1)
                if b == 0 and not first:
                    act.wait_ge(sem("a_wo"), i * HK - HK + g + 1)
                nc.scalar.copy(oT[:, REP * g:REP * (g + 1), b * S:(b + 1) * S],
                               o_ps[:, :].rearrange("p (r t) -> p r t", t=S)).then_inc(sem("a_oTs"), 1)

        def act_last_tile(act, i, k):
            if k == HK:
                act.wait_ge(sem("a_wo"), i * HK)
                nc.scalar.copy(yt[:, :], wo_ps[:, :]).then_inc(sem("a_y"), 1)
            elif k == HK + 1:
                act.wait_ge(sem("a_yT"), i)
                nc.scalar.copy(yT[:, :], wo_ps[:, :]).then_inc(sem("a_yTs"), 1)
            elif k == HK + 4:
                act.wait_ge(sem("a_uT"), i)
                nc.scalar.copy(uT[:, :], wo_ps[0:LMAX, 0:P]).then_inc(sem("a_uTs"), 1)

        ROUTE_LINKS = 8

        def dve_step(dve, i, k, first, last):
            wait = base(i, first)
            _, s, e, pt, pv = stages(k, first, last)
            if pt is not None:
                wait(dve, "a_pT", pt + 1)
                wait(dve, "a_o", pt - 1)
                nc.vector.tensor_copy(pT[:, pt % 2, 0:KC * P], pT_ps[:, :]).then_inc(sem("a_pTs"), 1)
            if e is not None:
                wait(dve, "a_exp", e + 1)
                nc.vector.reciprocal(rinv[:, e % 2:e % 2 + 1], rsum[:, e % 2:e % 2 + 1]).then_inc(
                    sem("a_rinv"), 1)
                wait(dve, "a_rinv", e + 1)
                nc.vector.tensor_scalar(pr[:, e % 2, :], pr[:, e % 2, :], rinv[:, e % 2:e % 2 + 1], None,
                                        ALU.mult).then_inc(sem("a_pr"), 1)
            if s is not None:
                if s % HK == 0:
                    if s > 0 or not first:
                        wait(dve, "a_max", s)
                    nc.vector.tensor_scalar(mask[:, S:S + LC], key[:, :],
                                            K["lens"][:, bass.ds(BT * i + s // HK, 1)], 1e30,
                                            ALU.is_ge, ALU.mult).then_inc(sem("a_mask"), 1)
                    dve.wait_ge(sem("a_mask"), BT * i + s // HK + 1)
                wait(dve, "a_s", s + 1)
                wait(dve, "a_exp", s - 1)
                hold(dve, sem("a_passed"))
                nc.vector.tensor_tensor_reduce(
                    out=sc[:, s % 2, :], in0=scores[s % 2], in1=masks[s % 2], scale=1.0,
                    scalar=3e38, op0=ALU.add, op1=ALU.min,
                    accum_out=mneg[:, s % 2:s % 2 + 1]).then_inc(sem("a_max"), 1)

        def dve_last_tile(dve, i, k, again):
            if k == HK + 2:
                link = Link(dve, sem("a_link"), (i - 1) * ROUTE_LINKS)
                dve.wait_ge(sem("a_u"), i)
                link(nc.vector.tensor_tensor(u[:, :], wo_ps[:, 0:LMAX + NROUTE], gb[:, :], ALU.add))
                link(nc.vector.tensor_reduce(rmax[:, :], u[:, LMAX:], AX_X, ALU.max))
                link(nc.vector.tensor_scalar(low[:, :], u[:, LMAX:], rmax[:, 0:1], None, ALU.is_lt))
                for r in range(1, NROUTE - 1):
                    link(nc.vector.tensor_tensor(low[:, r:r + 1], low[:, r:r + 1], low[:, r - 1:r],
                                                 ALU.mult))
                link(nc.vector.tensor_copy(um[:, 0:RANKS[0]], u[:, 0:RANKS[0]]))
                for r in range(NROUTE - 1):
                    done = nc.vector.tensor_scalar(um[:, RANKS[r]:RANKS[r + 1]],
                                                   u[:, RANKS[r]:RANKS[r + 1]], low[:, r:r + 1], None,
                                                   ALU.mult)
                    if r < NROUTE - 2:
                        link(done)
                done.then_inc(sem("a_um"), 1)
                assert link.n == ROUTE_LINKS
            elif k == HK + 5:
                dve.wait_ge(sem("a_x1"), 16 * i)
                if again:
                    dve.wait_ge(sem("a_out"), 16 * (i - 1))
                nc.vector.tensor_tensor(res[:, :], x1t[:, :], bias[:, :], ALU.add).then_inc(sem("a_res"), 1)
                dve.wait_ge(sem("a_res"), 2 * i - 1)
                dve.wait_ge(sem("a_z"), i)
                nc.vector.tensor_tensor(res[:, :], res[:, :], z_ps[:, :], ALU.add).then_inc(
                    sem("a_res"), 1)

        def pool_tile(pool, i, first=False):
            if not first:
                for n in range(2):
                    pool.wait_ge(sem(f"a_k{n}"), i * (BT // 2) * 16 * NPP)
                    pool.wait_ge(sem(f"a_v{n}"), i * (BT // 2) * 16 * KC)
            nc.gpsimd.tensor_copy(k_idx[:, :], k_rows[:, bass.ds(i * BT * NPP, BT * NPP)]).then_inc(
                sem("a_idx"), 1)
            nc.gpsimd.tensor_copy(v_idx[:, :], v_rows[:, bass.ds(i * BT * KC, BT * KC)]).then_inc(
                sem("a_idx"), 1)
            pool.wait_ge(sem("a_idx"), 2 * (i + 1))
            for b in range(BT):
                free = None if first and b < 2 else i * PAIRS + (b - 1) * HK
                for name, used, n, dst, idx, src in (
                        ("a_k", "a_s", NPP, kT[b % 2], k_idx, "kcacheT"),
                        ("a_v", "a_o", KC, vc[b % 2], v_idx, "vcache")):
                    if free is not None:
                        pool.wait_ge(sem(used), free)
                    hold(pool, sem("a_passed"))
                    for c in range(n):
                        nc.gpsimd.indirect_dma_start(
                            dst[:, c, :], None, I[src],
                            bass.IndirectOffsetOnAxis(ap=idx[:, b * n + c:b * n + c + 1], axis=0)
                        ).then_inc(sem(f"{name}{b % 2}"), 16)

        def sync_tile(sp, i, first=False, again=True):
            for un in range(UNITS):
                b, half, sl = un // 2, un % 2, un % 2
                tok = bass.ds(i * P + b * S, S)
                free = None if first and un < 2 else i * PAIRS + (un - 1) * UG
                if free is not None:
                    sp.wait_ge(sem("a_qT"), free)
                for r in range(REP):
                    src = I["q_scratch"][tok, :].rearrange("t (g r d) -> t g r d", r=REP, d=D)[
                        :, half * UG:(half + 1) * UG, r, :]
                    sp.dma_start(qu[sl][r * S:(r + 1) * S, :].rearrange("t (g d) -> t g d", d=D), src
                                 ).then_inc(sem(f"a_q{sl}"), 16)
                sp.dma_start(kn[sl][:, :], I["k_scratch"][tok, half * UW:(half + 1) * UW]).then_inc(
                    sem(f"a_q{sl}"), 16)
                if free is not None:
                    sp.wait_ge(sem("a_o"), free)
                sp.dma_start(vn[sl][:, :], I["v_scratch"][tok, half * UW:(half + 1) * UW]).then_inc(
                    sem(f"a_vn{sl}"), 16)
                if un == 1 and not first:
                    sync_x1(sp, i, again)
                if un == 5 and not first:
                    sync_out(sp, i)

        def sync_x1(sp, i, again):
            if again:
                sp.wait_ge(sem("a_res"), 2 * (i - 1))
            sp.dma_start(x1t[:, :], I["x1_scratch"][bass.ds(i * P - P, P), :]).then_inc(sem("a_x1"), 16)

        def sync_out(sp, i):
            sp.wait_ge(sem("a_res"), 2 * i)
            sp.dma_start(I["out"][bass.ds(i * P - P, P), :], res[:, :]).then_inc(sem("a_out"), 16)

        with nc.Block() as block:
            @block.sync
            def _(sp):
                for dst, src in ((bt_i, I["bt"].partition_broadcast(P)), (in_page[:, :], I["in_req"]),
                                 (part[:, :], I["part"])):
                    sp.dma_start(dst, src).then_inc(sem("a_pages"), 16)
                for dst, src in ((key[:, :], I["key"].partition_broadcast(P)),
                                 (bias[:, :], I["lb"].partition_broadcast(P)),
                                 (gb[:, LMAX:], I["gate_b"].partition_broadcast(P)),
                                 (bl[:, :], I["BlT"])):
                    sp.dma_start(dst, src).then_inc(sem("a_const"), 16)
                sync_tile(sp, 0, first=True)
                for dst, src in ((woT[:, :, :], I["woT"].rearrange("(h d) n -> d h n", d=P)),
                                 (lin[:, :, :], I["linT"].rearrange("(c p) n -> p c n", p=P)),
                                 (ag[:, :, 0:LMAX], I["AlT"].rearrange("(c p) n -> p c n", p=P)),
                                 (ag[:, :, LMAX:], I["gateT"].rearrange("(c p) n -> p c n", p=P))):
                    sp.dma_start(dst, src).then_inc(sem("a_weights"), 16)
                sync_tile(sp, 1, again=False)
                with sp.Fori(2, NT) as i:
                    sync_tile(sp, i)
                sync_x1(sp, NT, True)
                sync_out(sp, NT)
                sp.wait_ge(sem("a_out"), 16 * NT)

            @block.gpsimd
            def _(pool):
                pool.wait_ge(sem("a_rows"), 2)
                pool_tile(pool, 0, first=True)
                with pool.Fori(1, NT) as i:
                    pool_tile(pool, i)

            @block.tensor
            def _(pe):
                for k in range(PAIRS):
                    pe_step(pe, 0, k, True, False)
                pe.wait_ge(sem("a_weights"), 16 * 4)
                for k in range(PAIRS):
                    pe_step(pe, 1, k, False, False)
                    pe_last_tile(pe, 1, k, False)
                with pe.Fori(2, NT) as i:
                    for k in range(PAIRS):
                        pe_step(pe, i, k, False, False)
                        pe_last_tile(pe, i, k, True)
                for k in range(HK + 6):
                    pe_step(pe, NT, k, False, True)
                    pe_last_tile(pe, NT, k, True)

            @block.scalar
            def _(act):
                for k in range(PAIRS):
                    act_step(act, 0, k, True, False)
                with act.Fori(1, NT) as i:
                    for k in range(PAIRS):
                        act_step(act, i, k, False, False)
                        act_last_tile(act, i, k)
                for k in range(HK + 6):
                    act_step(act, NT, k, False, True)
                    act_last_tile(act, NT, k)

            @block.vector
            def _(dve):
                link = Link(dve, sem("a_link0"))
                link(nc.vector.memset(mask[:, :], 0.0))
                link(nc.vector.memset(gb[:, 0:LMAX], 0.0))
                dve.wait_ge(sem("a_pages"), 48)
                link(nc.vector.tensor_copy(bt_f, bt_i))
                nc.vector.tensor_scalar(k_rows[:, :], bt_f, float(D), part[:, 0:1], ALU.mult,
                                        ALU.add).then_inc(sem("a_rows"), 1)
                for q in range(P // PSIZE):
                    rows = slice(q * PSIZE, (q + 1) * PSIZE)
                    done = nc.vector.tensor_scalar(
                        v_rows[rows, :], bt_f[rows, :].rearrange("p (n q) -> p n q", q=P // PSIZE)[:, :, q],
                        float(PSIZE), in_page[rows, 0:1], ALU.mult, ALU.add)
                    if q < P // PSIZE - 1:
                        done.then_inc(sem("a_vrows"), 1)
                        dve.wait_ge(sem("a_vrows"), q + 1)
                done.then_inc(sem("a_rows"), 1)
                dve.wait_ge(sem("a_rows"), 2)
                dve.wait_ge(sem("a_const"), 16 * 4)
                for k in range(PAIRS):
                    dve_step(dve, 0, k, True, False)
                for k in range(PAIRS):
                    dve_step(dve, 1, k, False, False)
                    dve_last_tile(dve, 1, k, False)
                with dve.Fori(2, NT) as i:
                    for k in range(PAIRS):
                        dve_step(dve, i, k, False, False)
                        dve_last_tile(dve, i, k, True)
                for k in range(HK + 6):
                    dve_step(dve, NT, k, False, True)
                    dve_last_tile(dve, NT, k, True)


def build(nc, I):
    sems = {}
    with ExitStack() as ctx:
        def sem(name):
            if name not in sems:
                sems[name] = ctx.enter_context(nc.semaphore(name))
            return sems[name]

        keep = lambda c, n, s, d=F32: c.enter_context(nc.sbuf_tensor(n, s, d))
        K = {
            "ident": keep(ctx, "ident", [P, P]),
            "lens_i": keep(ctx, "lens_i", [P, B], I32),
            "lens": keep(ctx, "lens", [P, B]),
            "xg": keep(ctx, "xg", [P, 1]),
            "xrg": keep(ctx, "xrg", [P, 1]),
            "half_g": keep(ctx, "half_g", [P, 1]),
            "half_gg": keep(ctx, "half_gg", [P, 1]),
            "hg": keep(ctx, "hg", [P, 1]),
            "hrg": keep(ctx, "hrg", [P, 1]),
            "gpart": keep(ctx, "gpart", [P, 1]),
            "gall": keep(ctx, "gall", [P, 1]),
        }
        with ExitStack() as middle:
            K["x2"] = keep(middle, "x2", [P, NT, H])
            K["x1T"] = K["x2"][:, :, :].rearrange("p t n -> p (t n)").rearrange("p (c t) -> p c t", t=TOK)
            with ExitStack() as layer0:
                K["xmax"] = keep(layer0, "xmax", [P, NT, H // BLK])
                K["xrs"] = keep(layer0, "xrs", [P, NT, H // BLK])
                condition(nc, K, I, sem)
                K["wdT"] = keep(layer0, "wdT", [P, KI, H])
                K["h"] = keep(layer0, "h", [P, NT, I_DIM])
                K["hmax"] = keep(layer0, "hmax", [P, NT, I_DIM // BLK])
                with ExitStack() as gu:
                    K["wguT"] = keep(gu, "wguT", [P, 2, KH, I_DIM])
                    weights(nc, K, I, sem)
                    gate_up(nc, K, I, sem)
                down(nc, K, I, sem)
            project(nc, K, I, sem)
        attention(nc, K, I, sem)


def layout(x, itok_B_4_50, itok_Bx16_0_63, itok_B_207_1644, L0_cond_A, L0_cond_B, L0_ffn_w_gate,
           L0_ffn_w_up, L0_ffn_w_down, L0_ffn_ri_in, L0_ffn_ri_mid, L1_cond_Wq, L1_cond_Wk, L1_cond_Wv,
           L1_cond_Wo, L1_cond_q_norm_w, L1_cond_k_norm_w, L1_cond_k_cache, L1_cond_v_cache, L1_ffn_W,
           L1_ffn_b, L1_ffn_A, L1_ffn_B, L1_ffn_gate_w, L1_ffn_gate_b):
    import numpy as np

    c = np.ascontiguousarray
    x = np.asarray(x).reshape(TOK, H)
    p = np.arange(P)
    return {
        "x": c(x), "xT": c(x.T),
        "ids": c(itok_B_4_50), "bt": c(itok_Bx16_0_63).reshape(-1), "lens": c(itok_B_207_1644),
        "A_o": c(np.asarray(L0_cond_A).transpose(1, 0, 2).reshape(H, IDS * RANK)),
        "B_r": c(L0_cond_B).reshape(IDS * RANK, H),
        "wgT": c(np.asarray(L0_ffn_w_gate).T), "wuT": c(np.asarray(L0_ffn_w_up).T),
        "wdT": c(np.asarray(L0_ffn_w_down).T),
        "ri_in": c(np.asarray(L0_ffn_ri_in).reshape(KH, P).T),
        "ri_mid": c(np.asarray(L0_ffn_ri_mid)[:I_DIM // P * P].reshape(-1, P).T),
        "ri_tail": c(np.asarray(L0_ffn_ri_mid)[I_DIM // P * P:].reshape(-1, 1)),
        "wqkvT": c(np.concatenate([np.asarray(L1_cond_Wq), np.asarray(L1_cond_Wk),
                                   np.asarray(L1_cond_Wv)]).T),
        "woT": c(np.asarray(L1_cond_Wo).T),
        "qw": c(L1_cond_q_norm_w), "kw": c(L1_cond_k_norm_w),
        "kcacheT": c(np.asarray(L1_cond_k_cache).transpose(0, 3, 2, 1).reshape(PAGES * D, HK * PSIZE)),
        "vcache": c(L1_cond_v_cache).reshape(PAGES * PSIZE, HK * D),
        "linT": c(np.asarray(L1_ffn_W).T), "lb": c(L1_ffn_b), "AlT": c(np.asarray(L1_ffn_A).T),
        "BlT": c(np.asarray(L1_ffn_B).T), "gateT": c(np.asarray(L1_ffn_gate_w).T),
        "gate_b": c(L1_ffn_gate_b),
        "ident": np.eye(P, dtype=np.float32),
        "mine": (p[:, None] // RANK == np.arange(2 * P)[None, :] // S).astype(np.float32),
        "eight": (p[:, None] // RANK == np.arange(8)[None, :]).astype(np.float32),
        "rank_of": (p[:, None] % RANK).astype(np.float32),
        "part": p[:, None].astype(np.float32),
        "in_req": (p[:, None] % S).astype(np.float32),
        "key": np.arange(LC, dtype=np.float32),
        "invf": (1.0 / np.float32(10000.0) ** (np.arange(0, D, 2, dtype=np.float32) / np.float32(D))
                 ).astype(np.float32),
    }


def kernel(**inputs):
    import concourse.bacc as _bacc
    from concourse import mybir as _mybir
    from concourse.bass_utils import run_bass_kernel_spmd as _run

    nc = _bacc.Bacc("TRN2", target_bir_lowering=False, num_devices=1)
    arrays = layout(**inputs)
    I = {n: nc.dram_tensor(n + "_in", a.shape, _mybir.dt.from_np(a.dtype), kind="ExternalInput").ap()
         for n, a in arrays.items()}
    for n, shape in (("a_scratch", (IDS * RANK, H)), ("w_scratch", (2 * I_DIM, H)),
                     ("x1_scratch", (TOK, H)), ("q_scratch", (TOK, HQ * D)),
                     ("k_scratch", (TOK, HK * D)), ("v_scratch", (TOK, HK * D))):
        I[n] = nc.dram_tensor(n, shape, F32).ap()
    I["out"] = nc.dram_tensor("out", (TOK, H), F32, kind="ExternalOutput").ap()
    build(nc, I)
    r = _run(nc, [{n + "_in": a for n, a in arrays.items()}], core_ids=[0])
    return r.results[0]["out"].reshape(B, S, H)
```

```python
from contextlib import ExitStack

import concourse.bass as bass
from concourse import mybir

F32 = mybir.dt.float32
I32 = mybir.dt.int32
U32 = mybir.dt.uint32
ALU = mybir.AluOpType
ACT = mybir.ActivationFunctionType
AX_X = mybir.AxisListType.X
F32R = mybir.dt.float32r
RMAX = bass.bass_isa.ReduceOp.max

P = 128
B, S, H = 64, 32, 512
TOK = B * S
NT = TOK // P
BT = P // S
RANK = 16
IDS = 64
I_DIM = 1376
KH = H // P
CHUNKS_OF_X = (2, 0, 1, 3)
KI = (I_DIM + P - 1) // P
BLK = 16
SELECT = 128
HQ, HK, D = 32, 8, 128
REP = HQ // HK
PAGES, PSIZE, NPP = 64, 32, 16
LC = NPP * PSIZE
KC = LC // P
NKEY = LC + S
EPS = 1e-6
SCALE = D ** -0.5
FP8_MAX = 448.0
GDIV = 448.0 * 6.0
MAGIC_INT = 1.5 * 2.0 ** 23
FP8_TO_C = 1.5 * 2.0 ** 20
FP8_MIN_NORMAL = 2.0 ** -6
EXPONENT = 0x7F800000
LMAX = 64
NROUTE = 4
RANKS = (8, 16, 32, 64)
PIECES = [(0, 352), (352, 352), (704, 352), (1056, 320)]


def width(k):
    return min(P, I_DIM - k * P)


class Link:

    def __init__(self, eng, sem, base=0):
        self.eng, self.sem, self.base, self.n = eng, sem, base, 0

    def __call__(self, ins):
        self.n += 1
        ins.then_inc(self.sem, 1)
        self.eng.wait_ge(self.sem, self.base + self.n)


def hold(eng, passed):
    eng.sem_inc(passed, 1)


def blocks(ap):
    return ap.rearrange("p (b e) -> p b e", e=BLK)


def per_block(ap, nb):
    return ap.unsqueeze(2).to_broadcast([P, nb, BLK])


def seventh(nc, link, out, a, q, t):
    link(nc.vector.tensor_scalar(q, a, 1.0 / 7.0, None, ALU.mult))
    link(nc.vector.scalar_tensor_tensor(t, q, -8.0, a, ALU.mult, ALU.add))
    link(nc.vector.tensor_tensor(t, t, q, ALU.add))
    link(nc.vector.scalar_tensor_tensor(out, t, 1.0 / 7.0, q, ALU.mult, ALU.add))


def fp8_scales(nc, link, s, rs, t):
    seventh(nc, link, s, s, rs, t)
    link(nc.vector.tensor_scalar(s, s, 7.0 / FP8_MAX, 1e-8, ALU.mult, ALU.max))
    link(nc.vector.reciprocal(rs, s))


def fp8_round(nc, link, v, c):
    link(nc.vector.tensor_scalar(c.bitcast(I32), v.bitcast(I32), EXPONENT, None, ALU.bitwise_and))
    link(nc.vector.tensor_scalar(c, c, FP8_MIN_NORMAL, FP8_TO_C, ALU.max, ALU.mult))
    link(nc.vector.tensor_tensor(v, v, c, ALU.add))
    link(nc.vector.tensor_tensor(v, v, c, ALU.subtract))


def fp8_quantise(nc, link, x, rg, s, rs, out, v, c, s2, rs2, t2, r, n, out_gate, between=None):
    nb = n // BLK
    link(nc.vector.scalar_tensor_tensor(blocks(v), blocks(x), rg, per_block(rs, nb), ALU.mult, ALU.mult))
    fp8_round(nc, link, v, c)
    if out_gate is not None:
        out_gate()
    link(nc.vector.tensor_tensor(blocks(out), blocks(v), per_block(s, nb), ALU.mult))
    if between is not None:
        between()
    here = slice(n - SELECT, n)
    return fp8_residual(nc, link, x[:, here], rg, out[:, here], v[:, 0:SELECT], c[:, 0:SELECT], s2, rs2, t2, r)


def fp8_residual(nc, link, x, rg, tail, v, c, s2, rs2, t2, r):
    no = SELECT // BLK
    link(nc.vector.scalar_tensor_tensor(r, x, rg, tail, ALU.mult, ALU.subtract))
    link(nc.vector.tensor_reduce(s2, blocks(r), AX_X, ALU.max, apply_absolute_value=True))
    fp8_scales(nc, link, s2, rs2, t2)
    link(nc.vector.tensor_tensor(blocks(v), blocks(r), per_block(rs2, no), ALU.mult))
    fp8_round(nc, link, v, c)
    link(nc.vector.tensor_tensor(blocks(r), blocks(v), per_block(s2, no), ALU.mult))
    return nc.vector.tensor_tensor(tail, tail, r, ALU.add)


RESIDUAL_LINKS = (2 + 6) + (1 + 4 + 1)
FP8_LINKS = (1 + 4 + 1) + RESIDUAL_LINKS


def int4_quantise(nc, link, w, v, am, s, rs, out, nb):
    link(nc.vector.tensor_reduce(am, blocks(w), AX_X, ALU.max, apply_absolute_value=True))
    seventh(nc, link, am, am, rs, s)
    link(nc.vector.tensor_scalar(s, am, 1e-8, None, ALU.max))
    link(nc.vector.reciprocal(rs, s))
    m = w.shape[0]
    wide = lambda a: a.unsqueeze(2).to_broadcast([m, nb, BLK])
    link(nc.vector.tensor_tensor(blocks(v), blocks(w), wide(rs), ALU.mult))
    link(nc.vector.tensor_scalar(v, v, MAGIC_INT, MAGIC_INT, ALU.add, ALU.subtract))
    return nc.vector.tensor_tensor(blocks(out), blocks(v), wide(s), ALU.mult)


def condition(nc, K, I, sem):
    GB = 8
    NG = B // GB
    SEL = 4
    with ExitStack() as ctx:
        sb = lambda n, s, d=F32: ctx.enter_context(nc.sbuf_tensor(n, s, d))
        ps = lambda n, s: ctx.enter_context(nc.psum_tensor(n, s, F32))
        xT = sb("xT", [P, KH, TOK])
        a_gath = sb("a_gath", [P, KH, IDS * RANK])
        a_rows = sb("a_rows", [P, 2, H])
        ids = sb("ids", [P, NG, GB], I32)
        idf = sb("idf", [P, NG, GB])
        rowf = sb("rowf", [P, NG])
        row = sb("row", [P, NG], U32)
        ri = sb("ri", [P, KH], I32)
        tmp = sb("c_tmp", [P, NT * H // BLK])
        a_sel = sb("a_sel", [P, SEL, H])
        b_sel = sb("b_sel", [P, SEL, H])
        bT = sb("bT", [P, 2, KH * P])
        bx = sb("bx", [P, 2, 2 * P])
        mine = sb("mine", [P, 2 * P])
        rank_of = sb("rank_of", [P, 1])
        eight = sb("eight", [P, GB])
        t_ps = ps("t_ps", [P, 2, H])
        bT_ps = ps("bT_ps", [P, 2, H])
        bx_ps = ps("bx_ps", [P, 2, H])
        x2_ps = ps("x2_ps", [P, 2, H])

        def amax(dve, g):
            for n in (2 * g, 2 * g + 1):
                dve.wait_ge(sem("c_x2s"), n + 1)
                nc.vector.tensor_reduce(K["xmax"][:, n, :], blocks(K["x2"][:, n, :]), AX_X, ALU.max,
                                    apply_absolute_value=True).then_inc(sem("c_amax"), 1)

        def transpose_b(pe, g):
            pe.wait_ge(sem(f"c_bsel{g % SEL}"), 16 * (g // SEL + 1))
            if g >= 2:
                pe.wait_ge(sem("c_bTs"), g - 1)
            for c in range(KH):
                last = nc.tensor.transpose(
                    bT_ps[:, g % 2, c * P:(c + 1) * P],
                    b_sel[:, g % SEL, :].rearrange("p (i c) -> p c i", c=KH)[:, c, :], K["ident"][:, :])
            last.then_inc(sem("c_bT"), 1)

        def product_a(pe, g):
            pe.wait_ge(sem("c_bxs"), g + 1)
            pe.wait_ge(sem(f"c_asel{g % SEL}"), 16 * (g // SEL + 1))
            for h in range(2):
                n = 2 * g + h
                if n >= 2:
                    pe.wait_ge(sem("c_x2s"), n - 1)
                nc.tensor.matmul(x2_ps[:, h, :], bx[:, g % 2, h * P:(h + 1) * P],
                                 a_sel[:, g % SEL, :], start=True, stop=True).then_inc(sem("c_x2"), 1)

        with nc.Block() as block:
            @block.sync
            def _(sp):
                sp.dma_start(K["ident"][:, :], I["ident"]).then_inc(sem("c_const"), 16)
                sp.dma_start(mine[:, :], I["mine"]).then_inc(sem("c_const"), 16)
                sp.dma_start(rank_of[:, :], I["rank_of"]).then_inc(sem("c_const"), 16)
                sp.dma_start(eight[:, :], I["eight"]).then_inc(sem("c_const"), 16)
                sp.dma_start(ids[:, :, :], I["ids"].partition_broadcast(P).rearrange(
                    "p (g b) -> p g b", b=GB)).then_inc(sem("c_const"), 16)
                sp.dma_start(ri[:, :], I["ri_in"]).then_inc(sem("c_ri"), 16)
                sp.dma_start(xT[:, :, :], I["xT"].rearrange("(p c) t -> p c t", p=P)).then_inc(sem("c_x"), 16)
                for j in range(8):
                    sp.wait_ge(sem("c_arow"), j + 1)
                    sp.dma_start(I["a_scratch"][j * P:(j + 1) * P, :], a_rows[:, j % 2, :]).then_inc(
                        sem(f"c_astore{j % 2}"), 16)

            @block.gpsimd
            def _(pool):
                pool.wait_ge(sem("c_ri"), 16)
                for c in range(KH):
                    nc.gpsimd.indirect_dma_start(
                        a_gath[:, c, :], None, I["A_o"],
                        bass.IndirectOffsetOnAxis(ap=ri[:, c:c + 1], axis=0)).then_inc(sem("c_agath"), 16)
                pool.wait_ge(sem("c_row"), 1)
                pool.wait_ge(sem("c_astore0"), 64)
                pool.wait_ge(sem("c_astore1"), 64)
                for g in range(NG):
                    off = bass.IndirectOffsetOnAxis(ap=row[:, g:g + 1], axis=0)
                    if g >= SEL:
                        pool.wait_ge(sem("c_bT"), g - SEL + 1)
                    nc.gpsimd.indirect_dma_start(b_sel[:, g % SEL, :], None, I["B_r"], off).then_inc(
                        sem(f"c_bsel{g % SEL}"), 16)
                    if g >= SEL:
                        pool.wait_ge(sem("c_x2"), 2 * (g - SEL + 1))
                    nc.gpsimd.indirect_dma_start(a_sel[:, g % SEL, :], None, I["a_scratch"], off).then_inc(
                        sem(f"c_asel{g % SEL}"), 16)
                pool.wait_ge(sem("c_gmax"), 1)
                nc.gpsimd.partition_all_reduce(K["gall"][:, :], K["gpart"][:, :], P, RMAX).then_inc(
                    sem("c_gall"), 1)

            @block.tensor
            def _(pe):
                pe.wait_ge(sem("c_const"), 80)
                pe.wait_ge(sem("c_agath"), 64)
                for j in range(8):
                    if j >= 2:
                        pe.wait_ge(sem("c_arow"), j - 1)
                    for c in range(KH):
                        last = nc.tensor.transpose(t_ps[:, j % 2, c * P:(c + 1) * P],
                                                   a_gath[:, c, j * P:(j + 1) * P], K["ident"][:, :])
                    last.then_inc(sem("c_aT"), 1)
                pe.wait_ge(sem("c_x"), 16)
                transpose_b(pe, 0)
                for g in range(NG):
                    if g + 1 < NG:
                        transpose_b(pe, g + 1)
                    pe.wait_ge(sem("c_bTs"), g + 1)
                    for c in CHUNKS_OF_X:
                        last = nc.tensor.matmul(bx_ps[:, g % 2, 0:2 * P], bT[:, g % 2, c * P:(c + 1) * P],
                                                xT[:, c, g * 2 * P:(g + 1) * 2 * P],
                                                start=(c == CHUNKS_OF_X[0]), stop=(c == CHUNKS_OF_X[-1]))
                    last.then_inc(sem("c_bx"), 1)
                    if g:
                        product_a(pe, g - 1)
                product_a(pe, NG - 1)

            @block.scalar
            def _(act):
                for j in range(8):
                    act.wait_ge(sem("c_aT"), j + 1)
                    if j >= 2:
                        act.wait_ge(sem(f"c_astore{j % 2}"), 16 * (j // 2))
                    nc.scalar.copy(a_rows[:, j % 2, :], t_ps[:, j % 2, :]).then_inc(sem("c_arow"), 1)
                for step in range(NG + 2):
                    g = step
                    if g < NG:
                        act.wait_ge(sem("c_bT"), g + 1)
                        if g >= 2:
                            act.wait_ge(sem("c_bx"), g - 1)
                        nc.scalar.copy(bT[:, g % 2, :], bT_ps[:, g % 2, :]).then_inc(sem("c_bTs"), 1)
                    g = step - 2
                    if g < 0:
                        continue
                    for h in range(2):
                        n = 2 * g + h
                        act.wait_ge(sem("c_x2"), n + 1)
                        nc.scalar.copy(K["x2"][:, n, :], x2_ps[:, h, :]).then_inc(sem("c_x2s"), 1)

            @block.vector
            def _(dve):
                link = Link(dve, sem("c_link"))
                dve.wait_ge(sem("c_const"), 80)
                link(nc.vector.tensor_copy(idf[:, :, :], ids[:, :, :]))
                link(nc.vector.tensor_tensor(idf[:, :, :], idf[:, :, :],
                                             eight[:, :].unsqueeze(1).to_broadcast([P, NG, GB]), ALU.mult))
                link(nc.vector.tensor_reduce(rowf[:, :], idf[:, :, :], AX_X, ALU.add))
                link(nc.vector.tensor_scalar(rowf[:, :], rowf[:, :], float(RANK), rank_of[:, 0:1],
                                             ALU.mult, ALU.add))
                nc.vector.tensor_copy(row[:, :], rowf[:, :]).then_inc(sem("c_row"), 1)
                for g in range(NG):
                    dve.wait_ge(sem("c_bx"), g + 1)
                    if g >= 2:
                        dve.wait_ge(sem("c_x2"), 2 * (g - 1))
                    nc.vector.tensor_tensor(bx[:, g % 2, :], bx_ps[:, g % 2, 0:2 * P], mine[:, :],
                                            ALU.mult).then_inc(sem("c_bxs"), 1)
                    if g:
                        amax(dve, g - 1)
                amax(dve, NG - 1)
                dve.wait_ge(sem("c_amax"), NT)
                link(nc.vector.tensor_reduce(K["gpart"][:, :],
                                             K["xmax"][:, :, :].rearrange("p t b -> p (t b)"), AX_X, ALU.max))
                nc.vector.tensor_copy(K["gall"][:, :], K["gpart"][:, :]).then_inc(sem("c_gmax"), 1)
                dve.wait_ge(sem("c_gall"), 1)
                global_scale(nc, link, K["gall"][:, :], K["xg"][:, :], K["xrg"][:, 0:1])
                block_scales(nc, link, K["xrg"][:, 0:1],
                             K["xmax"][:, :, :].rearrange("p t b -> p (t b)"),
                             K["xrs"][:, :, :].rearrange("p t b -> p (t b)"), tmp[:, :])
                link(nc.vector.tensor_scalar(K["half_g"][:, :], K["xg"][:, :], 0.5, None, ALU.mult))
                link(nc.vector.tensor_tensor(K["half_gg"][:, :], K["half_g"][:, :], K["xg"][:, :], ALU.mult))



def global_scale(nc, link, gall, g, rg):
    link(nc.vector.tensor_scalar(g, gall, 1.0 / GDIV, 1e-8, ALU.mult, ALU.max))
    link(nc.vector.reciprocal(rg, g))


def block_scales(nc, link, rg, amax, rs, t):
    link(nc.vector.tensor_scalar(amax, amax, rg, None, ALU.mult))
    fp8_scales(nc, link, amax, rs, t)


def weights(nc, K, I, sem):
    with ExitStack() as ctx:
        sb = lambda n, s, d=F32: ctx.enter_context(nc.sbuf_tensor(n, s, d))
        ps = lambda n, s: ctx.enter_context(nc.psum_tensor(n, s, F32))
        taken = [0]

        def spare(*shape):
            n, a = 1, taken[0]
            for d in shape:
                n *= d
            taken[0] += n
            flat = K["h"][:, :, :].rearrange("p t n -> p (t n)")[:, a:a + n]
            names = "abc"[:len(shape)]
            sizes = dict(zip(names[1:], shape[1:]))
            return flat.rearrange(f"p ({' '.join(names)}) -> p {' '.join(names)}", **sizes)

        WI = 3
        guT = spare(2, KH, I_DIM)
        dT = spare(KI, H)
        ri = sb("w_ri", [P, KH], I32)
        rm = sb("w_rm", [P, KI], I32)
        nat = spare(2, H)
        wi = spare(WI, H)
        wq = spare(2, H)
        v = spare(1, I_DIM)[:, 0, :]
        am = sb("w_am", [P, I_DIM // BLK])
        s_ = sb("w_s", [P, I_DIM // BLK])
        rs = sb("w_rs", [P, I_DIM // BLK])
        dn = sb("dn", [P, I_DIM])
        dq = sb("dq", [P, I_DIM])
        a_ps = ps("a_ps", [P, 2, H])
        b_ps = ps("b_ps", [P, 2, H])
        d_ps = ps("d_ps", [P, 3 * H])
        tiles = [(m, k) for m in range(2) for k in range(KI)]
        per = (len(tiles) + KH - 1) // KH
        shares = [range(n * per, min((n + 1) * per, len(tiles))) for n in range(KH)]

        with nc.Block() as block:
            @block.sync
            def _(sp):
                sp.dma_start(ri[:, :], I["ri_in"]).then_inc(sem("w_idx"), 16)
                sp.dma_start(rm[:, 0:KI - 1], I["ri_mid"]).then_inc(sem("w_idx"), 16)
                sp.dma_start(rm[0:width(KI - 1), KI - 1:KI],
                             I["ri_tail"]).then_inc(sem("w_idx"), 16)
                for j, (m, k) in enumerate(tiles):
                    w = width(k)
                    sp.wait_ge(sem("w_nat"), j + 1)
                    sp.dma_start(I["w_scratch"][m * I_DIM + k * P:m * I_DIM + k * P + w, :],
                                 nat[0:w, j % 2, :]).then_inc(sem(f"w_store{j % 2}"), 16)

            @block.gpsimd
            def _(pool):
                pool.wait_ge(sem("w_idx"), 48)
                for k in range(KI):
                    w = width(k)
                    nc.gpsimd.indirect_dma_start(
                        dT[0:w, k, :], None, I["wdT"],
                        bass.IndirectOffsetOnAxis(ap=rm[0:w, k:k + 1], axis=0)).then_inc(sem("w_d"), 16)
                for m, name in enumerate(("wgT", "wuT")):
                    for c in range(KH):
                        nc.gpsimd.indirect_dma_start(
                            guT[:, m, c, :], None, I[name],
                            bass.IndirectOffsetOnAxis(ap=ri[:, c:c + 1], axis=0)).then_inc(sem("w_gu"), 16)
                pool.wait_ge(sem("w_store0"), 16 * KI)
                pool.wait_ge(sem("w_store1"), 16 * KI)
                for j, (m, k) in enumerate(tiles):
                    w = width(k)
                    if j >= WI:
                        pool.wait_ge(sem("w_q"), j - WI + 1)
                    nc.gpsimd.indirect_dma_start(
                        wi[0:w, j % WI, :], None, I["w_scratch"],
                        bass.IndirectOffsetOnAxis(ap=rm[0:w, k:k + 1], axis=0),
                        element_offset=m * I_DIM * H).then_inc(sem(f"w_wi{j % WI}"), 16)

            @block.tensor
            def _(pe):
                ident = K["ident"]
                pe.wait_ge(sem("w_d"), 16 * KI)
                for n in range(KH):
                    if n:
                        pe.wait_ge(sem("w_dts"), n)
                    for k in range(KI):
                        w = width(k)
                        last = nc.tensor.transpose(d_ps[:, k * P:k * P + w],
                                                   dT[0:w, k, n * P:(n + 1) * P], ident[0:w, 0:w])
                    last.then_inc(sem("w_dps"), 1)
                    if n == 0:
                        pe.wait_ge(sem("w_gu"), 16 * 2 * KH)
                    for j in shares[n]:
                        m, k = tiles[j]
                        w = width(k)
                        if j >= 2:
                            pe.wait_ge(sem("w_nat"), j - 1)
                        for c in range(KH):
                            last = nc.tensor.transpose(a_ps[0:w, j % 2, c * P:(c + 1) * P],
                                                       guT[:, m, c, k * P:k * P + w], ident[:, :])
                        last.then_inc(sem("w_aps"), 1)
                    pe.wait_ge(sem("w_dq"), n + 1)
                    pe.wait_ge(sem("w_dn"), n + 1)
                    for k in range(KI):
                        w = width(k)
                        last = nc.tensor.transpose(d_ps[0:w, k * P:(k + 1) * P],
                                                   dq[:, k * P:k * P + w], ident[:, :])
                    last.then_inc(sem("w_dtp"), 1)
                for j, (m, k) in enumerate(tiles):
                    w = width(k)
                    pe.wait_ge(sem("w_q"), j + 1)
                    if j >= 2:
                        pe.wait_ge(sem("w_bs"), j - 1)
                    for c in range(KH):
                        last = nc.tensor.transpose(b_ps[:, j % 2, c * P:c * P + w],
                                                   wq[0:w, j % 2, c * P:(c + 1) * P], ident[0:w, 0:w])
                    last.then_inc(sem("w_bps"), 1)

            @block.scalar
            def _(act):
                for n in range(KH):
                    act.wait_ge(sem("w_dps"), n + 1)
                    if n:
                        act.wait_ge(sem("w_dq"), n)
                    nc.scalar.copy(dn[:, :], d_ps[:, 0:I_DIM]).then_inc(sem("w_dn"), 1)
                    for j in shares[n]:
                        w = width(tiles[j][1])
                        act.wait_ge(sem("w_aps"), j + 1)
                        if j >= 2:
                            act.wait_ge(sem(f"w_store{j % 2}"), 16 * (j // 2))
                        nc.scalar.copy(nat[0:w, j % 2, :], a_ps[0:w, j % 2, :]).then_inc(sem("w_nat"), 1)
                    act.wait_ge(sem("w_dtp"), n + 1)
                    nc.scalar.copy(K["wdT"][:, 0:KI - 1, n * P:(n + 1) * P],
                                   d_ps[:, 0:(KI - 1) * P].rearrange("p (k o) -> p k o", o=P))
                    w = width(KI - 1)
                    nc.scalar.copy(K["wdT"][0:w, KI - 1, n * P:(n + 1) * P],
                                   d_ps[0:w, (KI - 1) * P:KI * P]).then_inc(sem("w_dts"), 1)
                for j, (m, k) in enumerate(tiles):
                    w = width(k)
                    act.wait_ge(sem("w_bps"), j + 1)
                    nc.scalar.copy(K["wguT"][:, m, :, k * P:k * P + w],
                                   b_ps[:, j % 2, :].rearrange("p (c i) -> p c i", i=P)[:, :, 0:w]
                                   ).then_inc(sem("w_bs"), 1)

            @block.vector
            def _(dve):
                link = Link(dve, sem("w_link"))
                for n in range(KH):
                    dve.wait_ge(sem("w_dn"), n + 1)
                    if n:
                        dve.wait_ge(sem("w_dtp"), n)
                    nb = I_DIM // BLK
                    int4_quantise(nc, link, dn[:, :], v[:, :], am[:, :], s_[:, :], rs[:, :], dq[:, :],
                                  nb).then_inc(sem("w_dq"), 1)
                for j, (m, k) in enumerate(tiles):
                    w = width(k)
                    nb = H // BLK
                    dve.wait_ge(sem(f"w_wi{j % WI}"), 16 * (j // WI + 1))
                    if j >= 2:
                        dve.wait_ge(sem("w_bps"), j - 1)
                    int4_quantise(nc, link, wi[0:w, j % WI, :], v[0:w, 0:H], am[0:w, 0:nb], s_[0:w, 0:nb],
                                  rs[0:w, 0:nb], wq[0:w, j % 2, :], nb).then_inc(sem("w_q"), 1)


def gate_up(nc, K, I, sem):
    NP_ = len(PIECES)
    with ExitStack() as ctx:
        sb = lambda n, s, d=F32: ctx.enter_context(nc.sbuf_tensor(n, s, d))
        ps = lambda n, s: ctx.enter_context(nc.psum_tensor(n, s, F32))
        v, c = sb("g_v", [P, H]), sb("g_c", [P, H])
        aq = sb("g_aq", [P, H])
        aT = sb("g_aT", [P, 2, H])
        s2, rs2, am2 = sb("g_s2", [P, 8]), sb("g_rs2", [P, 8]), sb("g_am2", [P, 8])
        r = sb("g_r", [P, SELECT])
        sg = sb("g_sg", [P, 2, 352])
        gate_ps, up_ps = ps("gate_ps", [P, 2, H]), ps("up_ps", [P, 2, H])
        aT_ps = ps("aT_ps", [P, H])

        def guarded(eng, name, value, first):
            if not first or value > 0:
                eng.wait_ge(sem(name), value)

        def pe_transpose(pe, i):
            pe.wait_ge(sem("g_aq"), i + 1)
            for k in range(KH):
                last = nc.tensor.transpose(aT_ps[:, k * P:(k + 1) * P], aq[:, k * P:(k + 1) * P],
                                           K["ident"][:, :])
            last.then_inc(sem("g_aT"), 1)

        def pe_tile(pe, i, slot, first=False, last_tile=False):
            for p, (o, w) in enumerate(PIECES):
                if p == NP_ - 1 and not last_tile:
                    pe_transpose(pe, i + 1)
                if p == 0:
                    pe.wait_ge(sem("g_aTs"), i + 1)
                guarded(pe, "g_h", NP_ * i + p - 1, first)
                for m, dst in enumerate((gate_ps, up_ps)):
                    for k in range(KH):
                        last = nc.tensor.matmul(dst[:, p % 2, 0:w], aT[:, slot, k * P:(k + 1) * P],
                                                K["wguT"][:, m, k, o:o + w],
                                                start=(k == 0), stop=(k == KH - 1))
                last.then_inc(sem("g_mm"), 1)

        def act_evac(act, i, slot, first=False):
            act.wait_ge(sem("g_aT"), i + 1)
            if not first:
                act.wait_ge(sem("g_mm"), NP_ * (i - 1))
            nc.scalar.copy(aT[:, slot, :], aT_ps[:, :]).then_inc(sem("g_aTs"), 1)

        def act_tile(act, i, slot, first=False, last_tile=False):
            for p, (o, w) in enumerate(PIECES):
                if p == NP_ - 1 and not last_tile:
                    act_evac(act, i + 1, 1 - slot, first)
                act.wait_ge(sem("g_mm"), NP_ * i + p + 1)
                guarded(act, "g_h", NP_ * i + p - 1, first)
                nc.scalar.activation(sg[:, p % 2, 0:w], gate_ps[:, p % 2, 0:w], ACT.Tanh,
                                     scale=K["half_g"][:, 0:1]).then_inc(
                    sem("g_tanh"), 1)

        def dve_quantise(dve, i, first=False, between=None):
            link = Link(dve, sem("g_link"), i * (FP8_LINKS))
            gate = None if first else (lambda: dve.wait_ge(sem("g_aT"), i))
            x = K["x2"][:, bass.ds(i, 1), :].squeeze(1)
            fp8_quantise(nc, link, x, K["xrg"][:, 0:1], K["xmax"][:, bass.ds(i, 1), :].squeeze(1),
                         K["xrs"][:, bass.ds(i, 1), :].squeeze(1), aq[:, :], v[:, :], c[:, :],
                         s2[:, :], rs2[:, :], am2[:, :], r[:, :], H, gate, between).then_inc(sem("g_aq"), 1)
            assert link.n == FP8_LINKS

        def dve_tile(dve, i, last_tile=False):
            if last_tile:
                dve_pieces(dve, i, 0, NP_)
            else:
                dve_quantise(dve, i + 1, between=lambda: dve_pieces(dve, i, 0, 1))
                dve_pieces(dve, i, 1, NP_)

        def dve_pieces(dve, i, lo, hi):
            for p, (o, w) in list(enumerate(PIECES))[lo:hi]:
                dve.wait_ge(sem("g_tanh"), NP_ * i + p + 1)
                h = K["h"][:, bass.ds(i, 1), o:o + w].squeeze(1)
                nc.vector.scalar_tensor_tensor(h, sg[:, p % 2, 0:w], 1.0, gate_ps[:, p % 2, 0:w],
                                               ALU.add, ALU.mult).then_inc(sem("g_silu"), 1)
                dve.wait_ge(sem("g_silu"), NP_ * i + p + 1)
                nc.vector.scalar_tensor_tensor(h, h, K["half_gg"][:, 0:1], up_ps[:, p % 2, 0:w], ALU.mult,
                                               ALU.mult).then_inc(sem("g_h"), 1)
                dve.wait_ge(sem("g_h"), NP_ * i + p + 1)
                nc.vector.tensor_reduce(
                    K["hmax"][:, bass.ds(i, 1), o // BLK:(o + w) // BLK].squeeze(1), blocks(h), AX_X,
                    ALU.max, apply_absolute_value=True).then_inc(sem("g_hmax"), 1)

        with nc.Block() as block:
            @block.tensor
            def _(pe):
                pe_transpose(pe, 0)
                pe_tile(pe, 0, 0, first=True)
                with pe.Fori(0, NT // 2 - 1) as j:
                    pe_tile(pe, 2 * j + 1, 1)
                    pe_tile(pe, 2 * j + 2, 0)
                pe_tile(pe, NT - 1, 1, last_tile=True)

            @block.scalar
            def _(act):
                act_evac(act, 0, 0, first=True)
                act_tile(act, 0, 0, first=True)
                with act.Fori(0, NT // 2 - 1) as j:
                    act_tile(act, 2 * j + 1, 1)
                    act_tile(act, 2 * j + 2, 0)
                act_tile(act, NT - 1, 1, last_tile=True)

            @block.vector
            def _(dve):
                dve_quantise(dve, 0, first=True)
                with dve.Fori(0, NT - 1) as i:
                    dve_tile(dve, i)
                dve_tile(dve, NT - 1, last_tile=True)
                link = Link(dve, sem("g_link2"))
                dve.wait_ge(sem("g_hmax"), NT * NP_)
                link(nc.vector.tensor_reduce(K["gpart"][:, :],
                                             K["hmax"][:, :, :].rearrange("p t b -> p (t b)"), AX_X, ALU.max))
                nc.vector.tensor_copy(K["gall"][:, :], K["gpart"][:, :]).then_inc(sem("g_gmax"), 1)
                dve.wait_ge(sem("g_gall"), 1)

            @block.gpsimd
            def _(pool):
                pool.wait_ge(sem("g_gmax"), 1)
                nc.gpsimd.partition_all_reduce(K["gall"][:, :], K["gpart"][:, :], P, RMAX).then_inc(
                    sem("g_gall"), 1)


def down(nc, K, I, sem):
    with ExitStack() as ctx:
        sb = lambda n, s, d=F32: ctx.enter_context(nc.sbuf_tensor(n, s, d))
        ps = lambda n, s: ctx.enter_context(nc.psum_tensor(n, s, F32))
        v, c, hq = sb("d_v", [P, 2, I_DIM]), sb("d_c", [P, I_DIM]), sb("d_hq", [P, I_DIM])
        v2, c2 = sb("d_v2", [P, SELECT]), sb("d_c2", [P, SELECT])
        hT = sb("d_hT", [P, 2, KI * P])
        NB = I_DIM // BLK
        hrs, tmp = sb("d_hrs", [P, NT, NB]), sb("d_tmp", [P, NT * NB])
        s2, rs2, am2 = sb("d_s2", [P, 8]), sb("d_rs2", [P, 8]), sb("d_am2", [P, 8])
        r = sb("d_r", [P, SELECT])
        x1s = sb("x1s", [P, H])
        xt = sb("d_xt", [P, H])
        hT_ps = ps("hT_ps", [P, 3 * H])
        y_ps = ps("y_ps", [P, 2, H])
        xT_ps = ps("xT_ps", [P, H])
        WL = width(KI - 1)

        def pe_transpose(pe, i, first=False):
            pe.wait_ge(sem("d_hq"), i + 1)
            pe.wait_ge(sem("d_body"), i + 1)
            if not first:
                pe.wait_ge(sem("d_hTs"), 2 * i)
            for k in range(KI):
                w = width(k)
                last = nc.tensor.transpose(hT_ps[0:w, k * P:(k + 1) * P], hq[:, k * P:k * P + w],
                                           K["ident"][:, :])
            last.then_inc(sem("d_hT"), 1)

        def pe_product(pe, i, slot, first=False):
            pe.wait_ge(sem("d_hTs"), 2 * (i + 1))
            if not first:
                pe.wait_ge(sem("d_x1"), i - 1)
            for k in range(KI):
                w = width(k)
                last = nc.tensor.matmul(y_ps[:, slot, :], hT[0:w, slot, k * P:(k + 1) * P],
                                        K["wdT"][0:w, k, :], start=(k == 0), stop=(k == KI - 1))
            last.then_inc(sem("d_y"), 1)

        def pe_x1(pe, i, first=False):
            pe.wait_ge(sem("d_x1"), i + 1)
            if not first:
                pe.wait_ge(sem("d_xTs"), i)
            for k in range(KH):
                last = nc.tensor.transpose(xT_ps[:, k * P:(k + 1) * P], x1s[:, k * P:(k + 1) * P],
                                           K["ident"][:, :])
            last.then_inc(sem("d_xT"), 1)

        def act_hT(act, i, slot, first=False):
            act.wait_ge(sem("d_hT"), i + 1)
            if not first:
                act.wait_ge(sem("d_y"), i - 1)
            nc.scalar.copy(hT[:, slot, 0:(KI - 1) * P], hT_ps[:, 0:(KI - 1) * P]).then_inc(
                sem("d_hTs"), 1)
            nc.scalar.copy(hT[0:WL, slot, (KI - 1) * P:KI * P], hT_ps[0:WL, (KI - 1) * P:KI * P]).then_inc(
                sem("d_hTs"), 1)

        def act_scale(act, i, slot, first=False):
            if not first:
                act.wait_ge(sem("d_body"), i - 1)
                act.wait_ge(sem("d_tail"), i - 1)
            nc.scalar.activation(v[:, slot, :], K["h"][:, bass.ds(i, 1), :].squeeze(1), ACT.Copy,
                                 scale=K["hrg"][:, 0:1]).then_inc(sem("d_xg"), 1)

        def act_x1(act, i):
            act.wait_ge(sem("d_xT"), i + 1)
            nc.scalar.copy(K["x1T"][:, :, bass.ds(i * P, P)],
                           xT_ps[:, :].rearrange("p (c t) -> p c t", t=P)).then_inc(sem("d_xTs"), 1)

        BODY = I_DIM - SELECT

        def row(a, i, lo, hi):
            return a[:, bass.ds(i, 1), lo:hi].squeeze(1)

        def pool_divide(pool, i, slot):
            pool.wait_ge(sem("d_xg"), i + 1)
            nc.gpsimd.tensor_tensor(blocks(v[:, slot, :]), blocks(v[:, slot, :]),
                                    per_block(row(hrs, i, 0, NB), NB), ALU.mult).then_inc(sem("d_v"), 1)

        def pool_body(pool, i, slot, first=False):
            pool.wait_ge(sem("d_round"), i + 1)
            if not first:
                pool.wait_ge(sem("d_hT"), i)
            nb = BODY // BLK
            nc.gpsimd.tensor_tensor(blocks(hq[:, 0:BODY]), blocks(v[:, slot, 0:BODY]),
                                    per_block(row(K["hmax"], i, 0, nb), nb), ALU.mult).then_inc(
                                        sem("d_body"), 1)

        def pool_tile(pool, i, slot, first=False, ahead=True):
            pool_body(pool, i, slot, first)
            if ahead:
                pool_divide(pool, i + 2, slot)

        DOWN_LINKS = 3 + RESIDUAL_LINKS

        def dve_quantise(dve, i, slot, first=False):
            link = Link(dve, sem("d_link"), i * DOWN_LINKS)
            dve.wait_ge(sem("d_v"), i + 1)
            a = v[:, slot, :]
            link(nc.vector.tensor_scalar(c[:, :].bitcast(I32), a.bitcast(I32), EXPONENT, None,
                                         ALU.bitwise_and))
            link(nc.vector.tensor_scalar(c[:, :], c[:, :], FP8_MIN_NORMAL, FP8_TO_C, ALU.max, ALU.mult))
            link(nc.vector.tensor_tensor(a, a, c[:, :], ALU.add))
            nc.vector.tensor_tensor(a, a, c[:, :], ALU.subtract).then_inc(sem("d_round"), 1)
            dve.wait_ge(sem("d_round"), i + 1)
            if not first:
                dve.wait_ge(sem("d_hT"), i)
            nb = SELECT // BLK
            tail = hq[:, BODY:]
            nc.vector.tensor_tensor(blocks(tail), blocks(a[:, BODY:]),
                                    per_block(row(K["hmax"], i, BODY // BLK, NB), nb), ALU.mult).then_inc(
                                        sem("d_tail"), 1)
            dve.wait_ge(sem("d_tail"), i + 1)
            fp8_residual(nc, link, row(K["h"], i, BODY, I_DIM), K["hrg"][:, 0:1], tail, v2[:, :], c2[:, :],
                         s2[:, :], rs2[:, :], am2[:, :], r[:, :]).then_inc(sem("d_hq"), 1)
            assert link.n == DOWN_LINKS

        def dve_x1(dve, i, slot, first=False):
            dve.wait_ge(sem("d_y"), i + 1)
            if not first:
                dve.wait_ge(sem("d_xT"), i)
                dve.wait_ge(sem("d_store"), 16 * i)
            dve.wait_ge(sem("d_x"), 16 * (i + 1))
            nc.vector.scalar_tensor_tensor(x1s[:, :], y_ps[:, slot, :], K["hg"][:, 0:1], xt[:, :], ALU.mult,
                                           ALU.add).then_inc(sem("d_x1"), 1)

        with nc.Block() as block:
            @block.sync
            def _(sp):
                with sp.Fori(0, NT) as i:
                    sp.dma_start(xt[:, :], I["x"][bass.ds(i * P, P), :]).then_inc(sem("d_x"), 16)
                    sp.wait_ge(sem("d_x1"), i + 1)
                    sp.dma_start(I["x1_scratch"][bass.ds(i * P, P), :], x1s[:, :]).then_inc(
                        sem("d_store"), 16)
                sp.wait_ge(sem("d_store"), 16 * NT)

            @block.gpsimd
            def _(pool):
                pool.wait_ge(sem("d_scales"), 1)
                pool_divide(pool, 0, 0)
                pool_divide(pool, 1, 1)
                pool.wait_ge(sem("d_scales"), 2)
                pool_tile(pool, 0, 0, first=True)
                pool_tile(pool, 1, 1)
                with pool.Fori(1, NT // 2 - 1) as j:
                    pool_tile(pool, 2 * j, 0)
                    pool_tile(pool, 2 * j + 1, 1)
                pool_tile(pool, NT - 2, 0, ahead=False)
                pool_tile(pool, NT - 1, 1, ahead=False)

            @block.tensor
            def _(pe):
                pe_transpose(pe, 0, first=True)
                pe_transpose(pe, 1)
                pe_product(pe, 0, 0, first=True)
                pe_transpose(pe, 2)
                pe_product(pe, 1, 1, first=True)
                pe_x1(pe, 0, first=True)
                with pe.Fori(1, NT // 2 - 1) as j:
                    for slot in range(2):
                        pe_transpose(pe, 2 * j + slot + 1)
                        pe_product(pe, 2 * j + slot, slot)
                        pe_x1(pe, 2 * j + slot - 1)
                pe_transpose(pe, NT - 1)
                pe_product(pe, NT - 2, 0)
                pe_x1(pe, NT - 3)
                pe_product(pe, NT - 1, 1)
                pe_x1(pe, NT - 2)
                pe_x1(pe, NT - 1)

            @block.scalar
            def _(act):
                act.wait_ge(sem("d_g"), 1)
                act_scale(act, 0, 0, first=True)
                act_scale(act, 1, 1, first=True)
                act_hT(act, 0, 0, first=True)
                act_scale(act, 2, 0)
                act_hT(act, 1, 1, first=True)
                act_scale(act, 3, 1)
                with act.Fori(1, NT // 2 - 1) as j:
                    for slot in range(2):
                        act_hT(act, 2 * j + slot, slot)
                        act_scale(act, 2 * j + slot + 2, slot)
                        act_x1(act, 2 * j + slot - 2)
                for slot in range(2):
                    act_hT(act, NT - 2 + slot, slot)
                    act_x1(act, NT - 4 + slot)
                act_x1(act, NT - 2)
                act_x1(act, NT - 1)

            @block.vector
            def _(dve):
                link = Link(dve, sem("d_scale"))
                global_scale(nc, link, K["gall"][:, :], K["hg"][:, :], K["hrg"][:, 0:1])
                dve.sem_inc(sem("d_g"), 1)
                for lo, hi in ((0, 2), (2, NT)):
                    flat = lambda a: a[:, lo:hi, :].rearrange("p t b -> p (t b)")
                    block_scales(nc, link, K["hrg"][:, 0:1], flat(K["hmax"]), flat(hrs),
                                 tmp[:, 0:(hi - lo) * NB])
                    dve.sem_inc(sem("d_scales"), 1)
                dve_quantise(dve, 0, 0, first=True)
                dve_quantise(dve, 1, 1)
                dve_quantise(dve, 2, 0)
                dve_x1(dve, 0, 0, first=True)
                dve_quantise(dve, 3, 1)
                dve_x1(dve, 1, 1)
                with dve.Fori(2, NT // 2) as j:
                    for slot in range(2):
                        dve_quantise(dve, 2 * j + slot, slot)
                        dve_x1(dve, 2 * j + slot - 2, slot)
                dve_x1(dve, NT - 2, 0)
                dve_x1(dve, NT - 1, 1)


TWO_PI = 6.283185307179586
C1 = 6.28125
C2 = 0.0019350051879882812
C3 = TWO_PI - C1 - C2


def project(nc, K, I, sem):
    G = 4
    CW = G * H
    PASSES = (HQ + 2 * HK) * D // CW
    HG = H // D
    half = D // 2
    with ExitStack() as ctx:
        sb = lambda n, s, d=F32: ctx.enter_context(nc.sbuf_tensor(n, s, d))
        ps = lambda n, s: ctx.enter_context(nc.psum_tensor(n, s, F32))
        w = sb("p_w", [P, KH, CW])
        wh, wl = sb("p_wh", [P, KH, CW], F32R), sb("p_wl", [P, KH, CW], F32R)
        xh, xl = sb("p_xh", [P, 2, H], F32R), sb("p_xl", [P, 2, H], F32R)
        raw = sb("p_raw", [P, 2, CW])
        rot = sb("p_rot", [P, 2, CW // 2])
        junk = sb("p_junk", [P, D])
        cos, sin = sb("p_cos", [P, NT, half]), sb("p_sin", [P, NT, half])
        tab = sb("p_tab", [P, 2, 2, D])
        nw = sb("p_nw", [P, 2, D])
        nws = sb("p_nws", [P, 2, D])
        ss, sd = sb("p_ss", [P, 2, G * HG]), sb("p_sd", [P, 2, G * HG])
        y, t, ms = (sb("p_" + n, [P, G * HG]) for n in ("y", "t", "ms"))
        pos = sb("p_pos", [P, NT])
        eps = sb("p_eps", [P, 1])
        in_req, part = sb("p_in_req", [P, 1]), sb("p_part", [P, 1])
        bt_i, bt_f = rot[:, 0, :].bitcast(I32), rot[:, 1, :]
        k_rows, v_rows = sb("p_k_rows", [P, B * NPP], U32), sb("p_v_rows", [P, B * KC], U32)
        invf = sb("p_invf", [P, half])
        g_ps = ps("p_ps", [P, G, H])

        def heads(p):
            return G * HG if p < PASSES - 1 else HK

        def pe_item(pe, p, i, slot, first=False, cold=False):
            n = NT * p + i
            pe.wait_ge(sem("p_xs"), n + 1)
            for g in range(G):
                if cold:
                    pe.wait_ge(sem("p_ws"), G * p + g + 1)
                if not first:
                    pe.wait_ge(sem("p_read"), G * (n - 1) + g + 1)
                parts = ((xh, wh), (xh, wl), (xl, wh))
                for m, (a, b) in enumerate(parts):
                    for k in range(KH):
                        last = nc.tensor.matmul(
                            g_ps[:, g, :], a[:, slot, k * P:(k + 1) * P], b[:, k, g * H:(g + 1) * H],
                            start=(m == 0 and k == 0), stop=(m == len(parts) - 1 and k == KH - 1))
                last.then_inc(sem("p_mm"), 1)

        def act_split(act, p):
            for g in range(G):
                act.wait_ge(sem(f"p_w{g}"), 16 * (p + 1))
                if p:
                    act.wait_ge(sem("p_mm"), G * (NT * p - 1) + g + 1)
                nc.scalar.copy(wh[:, :, g * H:(g + 1) * H], w[:, :, g * H:(g + 1) * H]).then_inc(
                    sem("p_wh"), 1)

        def dve_split(dve, p):
            for g in range(G):
                dve.wait_ge(sem("p_wh"), G * p + g + 1)
                cols = slice(g * H, (g + 1) * H)
                nc.vector.tensor_tensor(wl[:, :, cols], w[:, :, cols], wh[:, :, cols].bitcast(F32),
                                        ALU.subtract).then_inc(sem("p_ws"), 1)

        def act_stage(act, n, i, slot, first=False):
            if not first and not (isinstance(n, int) and n < 2):
                act.wait_ge(sem("p_mm"), G * (n - 1))
            nc.scalar.copy(xh[:, slot, :].rearrange("p (c t) -> p c t", t=P),
                           K["x1T"][:, :, bass.ds(i * P, P)]).then_inc(sem("p_xh"), 1)

        def low_part(eng, engine, n, i, slot):
            eng.wait_ge(sem("p_xh"), n + 1)
            part = lambda a: a[:, slot, :].rearrange("p (c t) -> p c t", t=P)
            engine.tensor_tensor(part(xl), K["x1T"][:, :, bass.ds(i * P, P)], part(xh).bitcast(F32),
                                 ALU.subtract).then_inc(sem("p_xs"), 1)

        def act_item(act, p, i, slot, j, first=False, stage=None):
            n = NT * p + i
            for g in range(G):
                act.wait_ge(sem("p_mm"), G * n + g + 1)
                src = g_ps[:, g, :]
                if g % 2 == 0 and not first:
                    act.wait_ge(sem(f"p_store{g // 2}{slot}"), 16 * stored(p, g // 2, j))
                if g == 0 and not first:
                    act.wait_ge(sem("p_y"), n - 1)
                normed = g * HG < heads(p)
                copied = nc.scalar.copy(raw[:, slot, g * H:(g + 1) * H], src)
                if not normed:
                    copied.then_inc(sem("p_read"), 1)
                else:
                    for h in range(HG):
                        last = nc.scalar.activation(junk[:, :], src[:, h * D:(h + 1) * D], ACT.Square,
                                                    accum_out=ss[:, slot, g * HG + h:g * HG + h + 1])
                        last.then_inc(sem("p_sq"), 1)
                        act.wait_ge(sem("p_sq"), squares(p, i) + g * HG + h + 1)
                    nc.scalar.activation(sd[:, slot, g * HG:(g + 1) * HG], ss[:, slot, g * HG:(g + 1) * HG],
                                         ACT.Sqrt, bias=eps[:, 0:1], scale=1.0 / D).then_inc(
                                             sem("p_read"), 1)
                if g == 0 and stage is not None:
                    act_stage(act, n + 1, stage, 1 - slot)

        def squares(p, i):
            return p * NT * G * HG + i * heads(p)

        def shapes(p, slot, a):
            mh = heads(p) // 2
            x = raw[:, slot, a * mh * D:(a + 1) * mh * D].rearrange("p (h d) -> p h d", d=D)
            o = rot[:, a, 0:mh * D].rearrange("p (h d) -> p h d", d=D)
            return mh, x, o, lambda v, m: v.unsqueeze(1).to_broadcast([P, mh, m])

        def dve_item(dve, p, i, slot, first=False):
            n = NT * p + i
            nh = heads(p)
            link = Link(dve, sem("p_link"), LINKS * n)
            dve.wait_ge(sem("p_read"), G * (n + 1))
            link(nc.vector.tensor_scalar(ms[:, 0:nh], ss[:, slot, 0:nh], 1.0 / D, EPS, ALU.mult, ALU.add))
            link(nc.vector.reciprocal(y[:, 0:nh], sd[:, slot, 0:nh]))
            link(nc.vector.tensor_tensor(t[:, 0:nh], y[:, 0:nh], y[:, 0:nh], ALU.mult))
            link(nc.vector.tensor_tensor(t[:, 0:nh], t[:, 0:nh], ms[:, 0:nh], ALU.mult))
            link(nc.vector.tensor_scalar(t[:, 0:nh], t[:, 0:nh], -0.5, 1.5, ALU.mult, ALU.add))
            nc.vector.tensor_tensor(y[:, 0:nh], y[:, 0:nh], t[:, 0:nh], ALU.mult).then_inc(sem("p_y"), 1)
            dve.wait_ge(sem("p_y"), n + 1)
            for a in range(2):
                mh, x, _, _ = shapes(p, slot, a)
                nc.vector.tensor_tensor(x, x, y[:, a * mh:(a + 1) * mh].unsqueeze(2).to_broadcast(
                    [P, mh, D]), ALU.mult).then_inc(sem("p_scaled"), 1)
            dve.wait_ge(sem("p_scaled"), 2 * (n + 1))
            dve.wait_ge(sem("p_tab"), 2 * (n + 1))
            for a in range(2):
                mh, x, o, over = shapes(p, slot, a)
                cos_w, sin_w = tab[:, slot, 0, :], tab[:, slot, 1, :]
                if not first:
                    dve.wait_ge(sem("p_out"), 2 * n - 1 + a)
                done = nc.vector.tensor_tensor(o[:, :, 0:half], x[:, :, half:D], over(sin_w[:, 0:half], half),
                                               ALU.mult)
                if a == 0:
                    link(done)
                    dve.wait_ge(sem("p_rot"), n + 1)
                else:
                    link(nc.vector.tensor_tensor(o[:, :, half:D], x[:, :, 0:half],
                                                 over(sin_w[:, half:D], half), ALU.mult))
                nc.vector.tensor_tensor(x, x, over(cos_w, D), ALU.mult).then_inc(sem("p_cos"), 1)
            assert link.n == LINKS, link.n

        LINKS = 5 + 2

        def pool_tables(pool, p, i, slot):
            q = int(p == PASSES - 1)
            for a, (base, wt) in enumerate(((cos, nw), (sin, nws))):
                nc.gpsimd.tensor_tensor(
                    tab[:, slot, a, :].rearrange("p (h f) -> p h f", h=2),
                    wt[:, q, :].rearrange("p (h f) -> p h f", h=2),
                    base[:, bass.ds(i, 1), :].to_broadcast([P, 2, half]), ALU.mult).then_inc(
                        sem("p_tab"), 1)

        def pool_item(pool, p, i, slot, tables, stage):
            n = NT * p + i
            mh, x, o, over = shapes(p, slot, 0)
            pool.wait_ge(sem("p_tab"), 2 * (n + 1))
            pool.wait_ge(sem("p_scaled"), 2 * n + 1)
            nc.gpsimd.tensor_tensor(o[:, :, half:D], x[:, :, 0:half], over(tab[:, slot, 1, half:D], half),
                                    ALU.mult).then_inc(sem("p_rot"), 1)
            if stage is not None:
                low_part(pool, nc.gpsimd, n + 2, stage, slot)
            for a in range(2):
                _, x, o, _ = shapes(p, slot, a)
                pool.wait_ge(sem("p_cos"), 2 * n + a + 1)
                nc.gpsimd.tensor_tensor(x, x, o, ALU.add).then_inc(sem("p_out"), 1)
            if tables is not None:
                pool_tables(pool, *tables, 1 - slot)

        def stored(p, side, j):
            return p * NT // 2 + (2 * j if p == PASSES - 1 and side == 0 else j)

        with nc.Block() as block:
            @block.sync
            def _(sp):
                def load(p):
                    for g in range(G):
                        if p:
                            sp.wait_ge(sem("p_ws"), G * (p - 1) + g + 1)
                        sp.dma_start(w[:, :, g * H:(g + 1) * H],
                                     I["wqkvT"].rearrange("(c p) n -> p c n", p=P)[
                                         :, :, p * CW + g * H:p * CW + (g + 1) * H]).then_inc(
                                             sem(f"p_w{g}"), 16)

                def store(p, i, slot):
                    rows = bass.ds(i * P, P)
                    n = NT * p + i
                    if p == PASSES - 1:
                        sp.wait_ge(sem("p_read"), G * (n + 1))
                        sp.dma_start(I["v_scratch"][rows, :], raw[:, slot, HK * D:]).then_inc(
                            sem(f"p_store1{slot}"), 16)
                    for a in range(2):
                        sp.wait_ge(sem("p_out"), 2 * n + a + 1)
                        m = heads(p) // 2 * D
                        here = slice(a * m, (a + 1) * m)
                        if p < PASSES - 1:
                            sp.dma_start(I["q_scratch"][rows, p * CW + a * m:p * CW + (a + 1) * m],
                                         raw[:, slot, here]).then_inc(sem(f"p_store{a}{slot}"), 16)
                        else:
                            sp.dma_start(I["k_scratch"][rows, here], raw[:, slot, here]).then_inc(
                                sem(f"p_store0{slot}"), 16)

                load(0)
                for dst, src in ((K["lens_i"][:, :], I["lens"].partition_broadcast(P)),
                                 (in_req[:, :], I["in_req"]),
                                 (invf[:, :], I["invf"].partition_broadcast(P)),
                                 (nw[:, 0, :], I["qw"].partition_broadcast(P)),
                                 (nw[:, 1, :], I["kw"].partition_broadcast(P)),
                                 (part[:, :], I["part"]), (bt_i, I["bt"].partition_broadcast(P))):
                    sp.dma_start(dst, src).then_inc(sem("p_const"), 16)
                for p in range(PASSES):
                    if p < PASSES - 1:
                        load(p + 1)
                    with sp.Fori(0, NT // 2) as j:
                        store(p, 2 * j, 0)
                        store(p, 2 * j + 1, 1)
                sp.wait_ge(sem("p_rows"), 2)
                for dst, src in ((I["k_rows"], k_rows), (I["v_rows"], v_rows)):
                    sp.dma_start(dst, src[:, :]).then_inc(sem("p_rstore"), 16)
                sp.wait_ge(sem("p_rstore"), 32)
                for slot in range(2):
                    for side in range(2):
                        sp.wait_ge(sem(f"p_store{side}{slot}"), 16 * stored(PASSES - 1, side, NT // 2))

            @block.tensor
            def _(pe):
                for p in range(PASSES):
                    pe_item(pe, p, 0, 0, first=(p == 0), cold=True)
                    pe_item(pe, p, 1, 1)
                    with pe.Fori(1, NT // 2) as j:
                        pe_item(pe, p, 2 * j, 0)
                        pe_item(pe, p, 2 * j + 1, 1)

            @block.scalar
            def _(act):
                act.wait_ge(sem("p_eps"), 1)
                act_stage(act, 0, 0, 0, first=True)
                act_split(act, 0)
                for p in range(PASSES):
                    if p:
                        act_split(act, p)
                    act_item(act, p, 0, 0, 0, first=(p == 0), stage=1)
                    if p == 0:
                        act.wait_ge(sem("p_angle"), 1)
                        nc.scalar.activation(sin[:, :, :], sin[:, :, :], ACT.Sin).then_inc(sem("p_trig"), 1)
                        nc.scalar.activation(cos[:, :, :], cos[:, :, :], ACT.Sin).then_inc(sem("p_trig"), 1)
                    act_item(act, p, 1, 1, 0, first=(p == 0), stage=2)
                    with act.Fori(1, NT // 2 - 1) as j:
                        act_item(act, p, 2 * j, 0, j, stage=2 * j + 1)
                        act_item(act, p, 2 * j + 1, 1, j, stage=2 * j + 2)
                    j = NT // 2 - 1
                    act_item(act, p, 2 * j, 0, j, stage=2 * j + 1)
                    act_item(act, p, 2 * j + 1, 1, j, stage=0 if p < PASSES - 1 else None)

            @block.gpsimd
            def _(pool):
                def first_pages(lo, hi):
                    for c in range(lo, hi):
                        nc.gpsimd.indirect_dma_start(
                            K["kT"][0][:, c, :], None, I["kcacheT"],
                            bass.IndirectOffsetOnAxis(ap=k_rows[:, c:c + 1], axis=0)
                        ).then_inc(sem("a_k0"), 16)

                low_part(pool, nc.gpsimd, 1, 1, 1)
                pool.wait_ge(sem("p_trig"), 2)
                pool_tables(pool, 0, 0, 0)
                for p in range(PASSES):
                    more = p < PASSES - 1
                    with pool.Fori(0, NT // 2 - 1) as j:
                        pool_item(pool, p, 2 * j, 0, (p, 2 * j + 1), 2 * j + 2)
                        pool_item(pool, p, 2 * j + 1, 1, (p, 2 * j + 2), 2 * j + 3)
                    pool_item(pool, p, NT - 2, 0, (p, NT - 1), 0 if more else None)
                    if not more:
                        pool.wait_ge(sem("p_xs"), PASSES * NT)
                        first_pages(0, 5)
                    pool_item(pool, p, NT - 1, 1, (p + 1, 0) if more else None, 1 if more else None)
                first_pages(5, NPP)

            @block.vector
            def _(dve):
                link = Link(dve, sem("p_link0"))
                nc.vector.memset(eps[:, :], EPS).then_inc(sem("p_eps"), 1)
                low_part(dve, nc.vector, 0, 0, 0)
                dve_split(dve, 0)
                lens = K["lens"]
                dve.wait_ge(sem("p_const"), 16 * 7)
                link(nc.vector.tensor_copy(bt_f, bt_i))
                nc.vector.tensor_scalar(k_rows[:, :], bt_f, float(D), part[:, 0:1], ALU.mult,
                                        ALU.add).then_inc(sem("p_rows"), 1)
                for q in range(P // PSIZE):
                    rows = slice(q * PSIZE, (q + 1) * PSIZE)
                    done = nc.vector.tensor_scalar(
                        v_rows[rows, :], bt_f[rows, :].rearrange("p (n q) -> p n q", q=P // PSIZE)[:, :, q],
                        float(PSIZE), in_req[rows, 0:1], ALU.mult, ALU.add)
                    if q < P // PSIZE - 1:
                        done.then_inc(sem("p_vrows"), 1)
                        dve.wait_ge(sem("p_vrows"), q + 1)
                done.then_inc(sem("p_rows"), 1)
                dve.wait_ge(sem("p_rows"), 2)
                link(nc.vector.tensor_copy(lens[:, :], K["lens_i"][:, :]))
                for q in range(BT):
                    rows = slice(q * S, (q + 1) * S)
                    nc.vector.tensor_copy(
                        pos[rows, :], lens[rows, :].rearrange("p (t q) -> p t q", q=BT)[:, :, q]
                    ).then_inc(sem("p_pos"), 1)
                dve.wait_ge(sem("p_pos"), BT)
                link(nc.vector.tensor_scalar(pos[:, :], pos[:, :], in_req[:, 0:1], None, ALU.add))
                link(nc.vector.tensor_scalar(nw[:, 0, :], nw[:, 0, :], -SCALE, None, ALU.mult))
                for q in range(2):
                    link(nc.vector.tensor_scalar(nws[:, q, 0:half], nw[:, q, half:D], -1.0, None,
                                                 ALU.mult))
                    link(nc.vector.tensor_copy(nws[:, q, half:D], nw[:, q, 0:half]))
                f = rot[:, 0, 0:NT * half].rearrange("p (t f) -> p t f", f=half)
                k_ = rot[:, 1, 0:NT * half].rearrange("p (t f) -> p t f", f=half)
                link(nc.vector.tensor_tensor(
                    f, pos[:, :].unsqueeze(2).to_broadcast([P, NT, half]),
                    invf[:, :].unsqueeze(1).to_broadcast([P, NT, half]), ALU.mult))
                link(nc.vector.tensor_scalar(k_, f, 1.0 / TWO_PI, MAGIC_INT, ALU.mult, ALU.add))
                link(nc.vector.tensor_scalar(k_, k_, MAGIC_INT, None, ALU.subtract))
                for c_ in (C1, C2, C3):
                    link(nc.vector.scalar_tensor_tensor(f, k_, -c_, f, ALU.mult, ALU.add))
                link(nc.vector.tensor_scalar(sin[:, :, :], f, 3.1415925, -3.1415925, ALU.min, ALU.max))
                link(nc.vector.tensor_scalar(cos[:, :, :].bitcast(I32), sin[:, :, :].bitcast(I32), 0x7FFFFFFF,
                                             None, ALU.bitwise_and))
                nc.vector.tensor_scalar(cos[:, :, :], cos[:, :, :], -1.0, TWO_PI / 4, ALU.mult, ALU.add
                                        ).then_inc(sem("p_angle"), 1)
                dve.wait_ge(sem("p_trig"), 2)
                for p in range(PASSES):
                    dve_item(dve, p, 0, 0, first=(p == 0))
                    with dve.Fori(1, NT // 2) as j:
                        dve_item(dve, p, 2 * j - 1, 1)
                        dve_item(dve, p, 2 * j, 0)
                    if p < PASSES - 1:
                        dve_split(dve, p + 1)
                    dve_item(dve, p, NT - 1, 1)


def attention(nc, K, I, sem):
    PAIRS = BT * HK
    UG = HK // 2
    UNITS = PAIRS // UG
    UW = UG * D
    W1 = LC + S
    with ExitStack() as ctx:
        sb = lambda n, s, d=F32: ctx.enter_context(nc.sbuf_tensor(n, s, d))
        ps = lambda n, s: ctx.enter_context(nc.psum_tensor(n, s, F32))
        kT = K["kT"]
        vc = [sb(f"vc{n}", [P, KC, HK * D]) for n in range(2)]
        kn = [sb(f"kn{n}", [S, UW]) for n in range(2)]
        vn = [sb(f"vn{n}", [S, UW]) for n in range(2)]
        qu = [sb(f"qu{n}", [P, UW]) for n in range(2)]
        woT = sb("woT", [P, HQ, H])
        oT = sb("oT", [P, HQ, P])
        qT = sb("qT", [P, 2, P + S])
        sc = sb("sc", [P, 2, W1])
        pr = sb("pr", [P, 2, W1])
        pT = sb("pT", [P, 2, (KC + 1) * P])
        mask = sb("mask", [P, S + LC + S])
        key = sb("key", [P, LC])
        mneg, rsum, rinv = sb("mneg", [P, 2]), sb("rsum", [P, 2]), sb("rinv", [P, 2])
        k_rows, v_rows = sb("k_rows", [P, B * NPP], U32), sb("v_rows", [P, B * KC], U32)
        k_idx, v_idx = sb("k_idx", [P, BT * NPP], U32), sb("v_idx", [P, BT * KC], U32)
        lin = sb("lin", [P, KH, H])
        ag = sb("ag", [P, KH, LMAX + NROUTE])
        bl = sb("bl", [LMAX, H])
        bias = sb("bias", [P, H])
        gb = sb("gb", [P, LMAX + NROUTE])
        yt, yT, x1t, res = sb("yt", [P, H]), sb("yT", [P, H]), sb("x1t", [P, H]), sb("res", [P, H])
        u, um, uT = sb("u", [P, LMAX + NROUTE]), sb("um", [P, LMAX]), sb("uT", [LMAX, P])
        rmax, low = sb("rmax", [P, 1]), sb("low", [P, NROUTE])
        s_ps = ps("s_ps", [P, 3 * H])
        cached = (s_ps[:, 0:LC], s_ps[:, 2 * H:2 * H + LC])
        new = (s_ps[:, H:H + S], s_ps[:, 2 * H - S:2 * H])
        scores = (s_ps[:, 0:W1], s_ps[:, 2 * H - S:2 * H + LC])
        masks = (mask[:, S:S + W1], mask[:, 0:W1])
        at_cached, at_new = (0, S), (LC, 0)
        q_ps = ps("q_ps", [P, H])
        pn_ps = q_ps[0:S, 256:256 + P]
        pT_ps = ps("pT_ps", [P, H])
        o_ps = ps("o_ps", [P, P])
        wo_ps = ps("wo_ps", [P, H])
        z_ps = ps("z_ps", [P, H])
        ident = K["ident"]

        def stages(k, first, last):
            pairs = [k - d for d in range(5)]
            return [p if (p < 0 or not last) and (p >= 0 or not first) else None for p in pairs]

        def base(i, first):
            def wait(eng, name, value):
                if first and value <= 0:
                    return
                eng.wait_ge(sem(name), i * PAIRS + value)
            return wait

        def place(pair):
            pair %= PAIRS
            return pair % HK, (pair // UG) % 2, (pair // HK) % 2, pair // HK

        def loads(i, pair):
            tile = i if pair >= 0 else i - 1
            pair %= PAIRS
            return (tile * (UNITS // 2) + pair // UG // 2 + 1, tile * (BT // 2) + pair // HK // 2 + 1)

        def pe_step(pe, i, k, first, last):
            wait = base(i, first)
            t, s, _, pt, pv = stages(k, first, last)
            if t is not None:
                g, un, _, _ = place(t)
                cols = slice(g % UG * D, (g % UG + 1) * D)
                if g % UG == 0:
                    pe.wait_ge(sem(f"a_q{un}"), 16 * (REP + 1) * loads(i, t)[0])
                wait(pe, "a_qTs", t)
                wait(pe, "a_pns", t - 3)
                nc.tensor.transpose(q_ps[:, 0:P], qu[un][:, cols], ident[:, :])
                nc.tensor.transpose(q_ps[:, P:P + S], kn[un][:, cols], ident[0:S, 0:S]).then_inc(
                    sem("a_qT"), 1)
            if pt is not None:
                wait(pe, "a_pr", pt + 1)
                if t is None:
                    wait(pe, "a_qTs", 0)
                    wait(pe, "a_pns", pt)
                o = at_new[pt % 2]
                nc.tensor.transpose(pn_ps, pr[:, pt % 2, o:o + S], ident[:, :]).then_inc(sem("a_pn"), 1)
                wait(pe, "a_pTs", pt)
                o = at_cached[pt % 2]
                for c in range(KC):
                    done = nc.tensor.transpose(pT_ps[:, c * P:(c + 1) * P],
                                               pr[:, pt % 2, o + c * P:o + (c + 1) * P], ident[:, :])
                done.then_inc(sem("a_pT"), 1)
            if s is not None:
                g, _, rq, _ = place(s)
                if g == 0:
                    pe.wait_ge(sem(f"a_k{rq}"), 16 * NPP * loads(i, s)[1])
                wait(pe, "a_qTs", s + 1)
                wait(pe, "a_max", s - 1)
                nc.tensor.matmul(cached[s % 2], qT[:, s % 2, 0:P],
                                 kT[rq][:, :, g * PSIZE:(g + 1) * PSIZE], start=True, stop=True)
                wait(pe, "a_max", s)
                nc.tensor.matmul(new[s % 2], qT[:, s % 2, 0:P], qT[:, s % 2, P:P + S],
                                 start=True, stop=True).then_inc(sem("a_s"), 1)
            if pv is not None:
                g, un, rq, _ = place(pv)
                if g == 0:
                    pe.wait_ge(sem(f"a_v{rq}"), 16 * KC * loads(i, pv)[1])
                if g % UG == 0:
                    pe.wait_ge(sem(f"a_vn{un}"), 16 * loads(i, pv)[0])
                wait(pe, "a_pTs", pv + 1)
                wait(pe, "a_pns", pv + 1)
                wait(pe, "a_oTs", pv)
                for c in range(KC):
                    nc.tensor.matmul(o_ps[:, :], vc[rq][:, c, g * D:(g + 1) * D],
                                     pT[:, pv % 2, c * P:(c + 1) * P], start=(c == 0), stop=False)
                nc.tensor.matmul(o_ps[:, :], vn[un][:, g % UG * D:(g % UG + 1) * D],
                                 pT[0:S, pv % 2, KC * P:(KC + 1) * P],
                                 start=False, stop=True).then_inc(sem("a_o"), 1)

        def pe_last_tile(pe, i, k, again):
            if k < HK:
                pe.wait_ge(sem("a_oTs"), i * PAIRS - HK + k + 1)
                for r in range(REP):
                    h = REP * k + r
                    done = nc.tensor.matmul(wo_ps[:, :], oT[:, h, :], woT[:, h, :],
                                            start=(h == 0), stop=(h == HQ - 1))
                done.then_inc(sem("a_wo"), 1)
            elif k == HK + 1:
                pe.wait_ge(sem("a_y"), i)
                for c in range(KH):
                    done = nc.tensor.transpose(wo_ps[:, c * P:(c + 1) * P], yt[:, c * P:(c + 1) * P],
                                               ident[:, :])
                done.then_inc(sem("a_yT"), 1)
            elif k == HK + 2:
                pe.wait_ge(sem("a_yTs"), i)
                for c in range(KH):
                    done = nc.tensor.matmul(wo_ps[:, 0:LMAX + NROUTE], yT[:, c * P:(c + 1) * P], ag[:, c, :],
                                            start=(c == 0), stop=(c == KH - 1))
                done.then_inc(sem("a_u"), 1)
                if again:
                    pe.wait_ge(sem("a_res"), 2 * (i - 1))
                for c in range(KH):
                    nc.tensor.matmul(z_ps[:, :], yT[:, c * P:(c + 1) * P], lin[:, c, :],
                                     start=(c == 0), stop=False)
            elif k == HK + 4:
                pe.wait_ge(sem("a_um"), i)
                hold(pe, sem("a_passed"))
                nc.tensor.transpose(wo_ps[0:LMAX, 0:P], um[:, :], ident[:, :]).then_inc(sem("a_uT"), 1)
            elif k == HK + 5:
                pe.wait_ge(sem("a_uTs"), i)
                nc.tensor.matmul(z_ps[:, :], uT[:, :], bl[:, :], start=False, stop=True).then_inc(
                    sem("a_z"), 1)

        def act_step(act, i, k, first, last):
            wait = base(i, first)
            t, s, _, pt, pv = stages(k, first, last)
            if pt is not None:
                wait(act, "a_pn", pt + 1)
            if t is not None:
                wait(act, "a_qT", t + 1)
                wait(act, "a_s", t - 1)
                nc.scalar.copy(qT[:, t % 2, :], q_ps[:, 0:P + S]).then_inc(sem("a_qTs"), 1)
            if pt is not None:
                wait(act, "a_o", pt - 1)
                nc.scalar.copy(pT[0:S, pt % 2, KC * P:(KC + 1) * P], pn_ps).then_inc(sem("a_pns"), 1)
            if s is not None:
                wait(act, "a_max", s + 1)
                wait(act, "a_pT", s - 1)
                nc.scalar.activation(pr[:, s % 2, :], sc[:, s % 2, :], ACT.Exp, scale=-1.0,
                                     bias=mneg[:, s % 2:s % 2 + 1],
                                     accum_out=rsum[:, s % 2:s % 2 + 1]).then_inc(sem("a_exp"), 1)
            if pv is not None:
                g, _, _, b = place(pv)
                wait(act, "a_o", pv + 1)
                if b == 0 and not first:
                    act.wait_ge(sem("a_wo"), i * HK - HK + g + 1)
                nc.scalar.copy(oT[:, REP * g:REP * (g + 1), b * S:(b + 1) * S],
                               o_ps[:, :].rearrange("p (r t) -> p r t", t=S)).then_inc(sem("a_oTs"), 1)

        def act_last_tile(act, i, k):
            if k == HK:
                act.wait_ge(sem("a_wo"), i * HK)
                nc.scalar.copy(yt[:, :], wo_ps[:, :]).then_inc(sem("a_y"), 1)
            elif k == HK + 1:
                act.wait_ge(sem("a_yT"), i)
                nc.scalar.copy(yT[:, :], wo_ps[:, :]).then_inc(sem("a_yTs"), 1)
            elif k == HK + 4:
                act.wait_ge(sem("a_uT"), i)
                nc.scalar.copy(uT[:, :], wo_ps[0:LMAX, 0:P]).then_inc(sem("a_uTs"), 1)

        ROUTE_LINKS = 8

        def dve_step(dve, i, k, first, last):
            wait = base(i, first)
            _, s, e, pt, pv = stages(k, first, last)
            if pt is not None:
                wait(dve, "a_pT", pt + 1)
                wait(dve, "a_o", pt - 1)
                nc.vector.tensor_copy(pT[:, pt % 2, 0:KC * P], pT_ps[:, :]).then_inc(sem("a_pTs"), 1)
            if e is not None:
                wait(dve, "a_exp", e + 1)
                nc.vector.reciprocal(rinv[:, e % 2:e % 2 + 1], rsum[:, e % 2:e % 2 + 1]).then_inc(
                    sem("a_rinv"), 1)
                wait(dve, "a_rinv", e + 1)
                nc.vector.tensor_scalar(pr[:, e % 2, :], pr[:, e % 2, :], rinv[:, e % 2:e % 2 + 1], None,
                                        ALU.mult).then_inc(sem("a_pr"), 1)
            if s is not None:
                if s % HK == 0:
                    if s > 0 or not first:
                        wait(dve, "a_max", s)
                    nc.vector.tensor_scalar(mask[:, S:S + LC], key[:, :],
                                            K["lens"][:, bass.ds(BT * i + s // HK, 1)], 1e30,
                                            ALU.is_ge, ALU.mult).then_inc(sem("a_mask"), 1)
                    dve.wait_ge(sem("a_mask"), BT * i + s // HK + 1)
                wait(dve, "a_s", s + 1)
                wait(dve, "a_exp", s - 1)
                hold(dve, sem("a_passed"))
                nc.vector.tensor_tensor_reduce(
                    out=sc[:, s % 2, :], in0=scores[s % 2], in1=masks[s % 2], scale=1.0,
                    scalar=3e38, op0=ALU.add, op1=ALU.min,
                    accum_out=mneg[:, s % 2:s % 2 + 1]).then_inc(sem("a_max"), 1)

        def dve_last_tile(dve, i, k, again):
            if k == HK + 2:
                link = Link(dve, sem("a_link"), (i - 1) * ROUTE_LINKS)
                dve.wait_ge(sem("a_u"), i)
                link(nc.vector.tensor_tensor(u[:, :], wo_ps[:, 0:LMAX + NROUTE], gb[:, :], ALU.add))
                link(nc.vector.tensor_reduce(rmax[:, :], u[:, LMAX:], AX_X, ALU.max))
                link(nc.vector.tensor_scalar(low[:, :], u[:, LMAX:], rmax[:, 0:1], None, ALU.is_lt))
                for r in range(1, NROUTE - 1):
                    link(nc.vector.tensor_tensor(low[:, r:r + 1], low[:, r:r + 1], low[:, r - 1:r],
                                                 ALU.mult))
                link(nc.vector.tensor_copy(um[:, 0:RANKS[0]], u[:, 0:RANKS[0]]))
                for r in range(NROUTE - 1):
                    done = nc.vector.tensor_scalar(um[:, RANKS[r]:RANKS[r + 1]],
                                                   u[:, RANKS[r]:RANKS[r + 1]], low[:, r:r + 1], None,
                                                   ALU.mult)
                    if r < NROUTE - 2:
                        link(done)
                done.then_inc(sem("a_um"), 1)
                assert link.n == ROUTE_LINKS
            elif k == HK + 5:
                dve.wait_ge(sem("a_x1"), 16 * i)
                if again:
                    dve.wait_ge(sem("a_out"), 16 * (i - 1))
                nc.vector.tensor_tensor(res[:, :], x1t[:, :], bias[:, :], ALU.add).then_inc(sem("a_res"), 1)
                dve.wait_ge(sem("a_res"), 2 * i - 1)
                dve.wait_ge(sem("a_z"), i)
                nc.vector.tensor_tensor(res[:, :], res[:, :], z_ps[:, :], ALU.add).then_inc(
                    sem("a_res"), 1)

        def pool_tile(pool, i, first=False):
            if not first:
                for n in range(2):
                    pool.wait_ge(sem(f"a_k{n}"), i * (BT // 2) * 16 * NPP)
                    pool.wait_ge(sem(f"a_v{n}"), i * (BT // 2) * 16 * KC)
            nc.gpsimd.tensor_copy(k_idx[:, :], k_rows[:, bass.ds(i * BT * NPP, BT * NPP)]).then_inc(
                sem("a_idx"), 1)
            nc.gpsimd.tensor_copy(v_idx[:, :], v_rows[:, bass.ds(i * BT * KC, BT * KC)]).then_inc(
                sem("a_idx"), 1)
            pool.wait_ge(sem("a_idx"), 2 * (i + 1))
            for b in range(BT):
                free = None if first and b < 2 else i * PAIRS + (b - 1) * HK
                for name, used, n, dst, idx, src in (
                        ("a_k", "a_s", NPP, kT[b % 2], k_idx, "kcacheT"),
                        ("a_v", "a_o", KC, vc[b % 2], v_idx, "vcache")):
                    if first and b == 0 and name == "a_k":
                        continue
                    if free is not None:
                        pool.wait_ge(sem(used), free)
                    hold(pool, sem("a_passed"))
                    for c in range(n):
                        nc.gpsimd.indirect_dma_start(
                            dst[:, c, :], None, I[src],
                            bass.IndirectOffsetOnAxis(ap=idx[:, b * n + c:b * n + c + 1], axis=0)
                        ).then_inc(sem(f"{name}{b % 2}"), 16)

        def sync_tile(sp, i, first=False, again=True):
            for un in range(UNITS):
                b, half, sl = un // 2, un % 2, un % 2
                tok = bass.ds(i * P + b * S, S)
                free = None if first and un < 2 else i * PAIRS + (un - 1) * UG
                if free is not None:
                    sp.wait_ge(sem("a_qT"), free)
                for r in range(REP):
                    src = I["q_scratch"][tok, :].rearrange("t (g r d) -> t g r d", r=REP, d=D)[
                        :, half * UG:(half + 1) * UG, r, :]
                    sp.dma_start(qu[sl][r * S:(r + 1) * S, :].rearrange("t (g d) -> t g d", d=D), src
                                 ).then_inc(sem(f"a_q{sl}"), 16)
                sp.dma_start(kn[sl][:, :], I["k_scratch"][tok, half * UW:(half + 1) * UW]).then_inc(
                    sem(f"a_q{sl}"), 16)
                if free is not None:
                    sp.wait_ge(sem("a_o"), free)
                sp.dma_start(vn[sl][:, :], I["v_scratch"][tok, half * UW:(half + 1) * UW]).then_inc(
                    sem(f"a_vn{sl}"), 16)
                if un == 1 and not first:
                    sync_x1(sp, i, again)
                if un == 5 and not first:
                    sync_out(sp, i)

        def sync_x1(sp, i, again):
            if again:
                sp.wait_ge(sem("a_res"), 2 * (i - 1))
            sp.dma_start(x1t[:, :], I["x1_scratch"][bass.ds(i * P - P, P), :]).then_inc(sem("a_x1"), 16)

        def sync_out(sp, i):
            sp.wait_ge(sem("a_res"), 2 * i)
            sp.dma_start(I["out"][bass.ds(i * P - P, P), :], res[:, :]).then_inc(sem("a_out"), 16)

        with nc.Block() as block:
            @block.sync
            def _(sp):
                for dst, src in ((k_rows, I["k_rows"]), (v_rows, I["v_rows"])):
                    sp.dma_start(dst[:, :], src).then_inc(sem("a_rows"), 16)
                for dst, src in ((key[:, :], I["key"].partition_broadcast(P)),
                                 (bias[:, :], I["lb"].partition_broadcast(P)),
                                 (gb[:, LMAX:], I["gate_b"].partition_broadcast(P)),
                                 (bl[:, :], I["BlT"])):
                    sp.dma_start(dst, src).then_inc(sem("a_const"), 16)
                sync_tile(sp, 0, first=True)
                for dst, src in ((woT[:, :, :], I["woT"].rearrange("(h d) n -> d h n", d=P)),
                                 (lin[:, :, :], I["linT"].rearrange("(c p) n -> p c n", p=P)),
                                 (ag[:, :, 0:LMAX], I["AlT"].rearrange("(c p) n -> p c n", p=P)),
                                 (ag[:, :, LMAX:], I["gateT"].rearrange("(c p) n -> p c n", p=P))):
                    sp.dma_start(dst, src).then_inc(sem("a_weights"), 16)
                sync_tile(sp, 1, again=False)
                with sp.Fori(2, NT) as i:
                    sync_tile(sp, i)
                sync_x1(sp, NT, True)
                sync_out(sp, NT)
                sp.wait_ge(sem("a_out"), 16 * NT)

            @block.gpsimd
            def _(pool):
                pool.wait_ge(sem("a_rows"), 32)
                pool_tile(pool, 0, first=True)
                with pool.Fori(1, NT) as i:
                    pool_tile(pool, i)

            @block.tensor
            def _(pe):
                for k in range(PAIRS):
                    pe_step(pe, 0, k, True, False)
                pe.wait_ge(sem("a_weights"), 16 * 4)
                for k in range(PAIRS):
                    pe_step(pe, 1, k, False, False)
                    pe_last_tile(pe, 1, k, False)
                with pe.Fori(2, NT) as i:
                    for k in range(PAIRS):
                        pe_step(pe, i, k, False, False)
                        pe_last_tile(pe, i, k, True)
                for k in range(HK + 6):
                    pe_step(pe, NT, k, False, True)
                    pe_last_tile(pe, NT, k, True)

            @block.scalar
            def _(act):
                for k in range(PAIRS):
                    act_step(act, 0, k, True, False)
                with act.Fori(1, NT) as i:
                    for k in range(PAIRS):
                        act_step(act, i, k, False, False)
                        act_last_tile(act, i, k)
                for k in range(HK + 6):
                    act_step(act, NT, k, False, True)
                    act_last_tile(act, NT, k)

            @block.vector
            def _(dve):
                link = Link(dve, sem("a_link0"))
                link(nc.vector.memset(mask[:, :], 0.0))
                link(nc.vector.memset(gb[:, 0:LMAX], 0.0))
                dve.wait_ge(sem("a_const"), 16 * 4)
                for k in range(PAIRS):
                    dve_step(dve, 0, k, True, False)
                for k in range(PAIRS):
                    dve_step(dve, 1, k, False, False)
                    dve_last_tile(dve, 1, k, False)
                with dve.Fori(2, NT) as i:
                    for k in range(PAIRS):
                        dve_step(dve, i, k, False, False)
                        dve_last_tile(dve, i, k, True)
                for k in range(HK + 6):
                    dve_step(dve, NT, k, False, True)
                    dve_last_tile(dve, NT, k, True)


def build(nc, I):
    sems = {}
    with ExitStack() as ctx:
        def sem(name):
            if name not in sems:
                sems[name] = ctx.enter_context(nc.semaphore(name))
            return sems[name]

        keep = lambda c, n, s, d=F32: c.enter_context(nc.sbuf_tensor(n, s, d))
        K = {
            "ident": keep(ctx, "ident", [P, P]),
            "lens_i": keep(ctx, "lens_i", [P, B], I32),
            "lens": keep(ctx, "lens", [P, B]),
            "xg": keep(ctx, "xg", [P, 1]),
            "xrg": keep(ctx, "xrg", [P, 1]),
            "half_g": keep(ctx, "half_g", [P, 1]),
            "half_gg": keep(ctx, "half_gg", [P, 1]),
            "hg": keep(ctx, "hg", [P, 1]),
            "hrg": keep(ctx, "hrg", [P, 1]),
            "gpart": keep(ctx, "gpart", [P, 1]),
            "gall": keep(ctx, "gall", [P, 1]),
        }
        with ExitStack() as middle:
            K["x2"] = keep(middle, "x2", [P, NT, H])
            slots = K["x2"][:, :, :].rearrange("p t n -> p (t n)").rearrange("p (s w) -> p s w", s=2)
            K["kT"] = [slots[:, n, :].rearrange("p (j c) -> p j c", j=NPP) for n in range(2)]
            K["x1T"] = K["x2"][:, :, :].rearrange("p t n -> p (t n)").rearrange("p (c t) -> p c t", t=TOK)
            with ExitStack() as layer0:
                K["xmax"] = keep(layer0, "xmax", [P, NT, H // BLK])
                K["xrs"] = keep(layer0, "xrs", [P, NT, H // BLK])
                condition(nc, K, I, sem)
                K["wdT"] = keep(layer0, "wdT", [P, KI, H])
                K["h"] = keep(layer0, "h", [P, NT, I_DIM])
                K["hmax"] = keep(layer0, "hmax", [P, NT, I_DIM // BLK])
                with ExitStack() as gu:
                    K["wguT"] = keep(gu, "wguT", [P, 2, KH, I_DIM])
                    weights(nc, K, I, sem)
                    gate_up(nc, K, I, sem)
                down(nc, K, I, sem)
            project(nc, K, I, sem)
            attention(nc, K, I, sem)


def layout(x, itok_B_4_50, itok_Bx16_0_63, itok_B_207_1644, L0_cond_A, L0_cond_B, L0_ffn_w_gate,
           L0_ffn_w_up, L0_ffn_w_down, L0_ffn_ri_in, L0_ffn_ri_mid, L1_cond_Wq, L1_cond_Wk, L1_cond_Wv,
           L1_cond_Wo, L1_cond_q_norm_w, L1_cond_k_norm_w, L1_cond_k_cache, L1_cond_v_cache, L1_ffn_W,
           L1_ffn_b, L1_ffn_A, L1_ffn_B, L1_ffn_gate_w, L1_ffn_gate_b):
    import numpy as np

    c = np.ascontiguousarray
    x = np.asarray(x).reshape(TOK, H)
    p = np.arange(P)
    return {
        "x": c(x), "xT": c(x.T),
        "ids": c(itok_B_4_50), "bt": c(itok_Bx16_0_63).reshape(-1), "lens": c(itok_B_207_1644),
        "A_o": c(np.asarray(L0_cond_A).transpose(1, 0, 2).reshape(H, IDS * RANK)),
        "B_r": c(L0_cond_B).reshape(IDS * RANK, H),
        "wgT": c(np.asarray(L0_ffn_w_gate).T), "wuT": c(np.asarray(L0_ffn_w_up).T),
        "wdT": c(np.asarray(L0_ffn_w_down).T),
        "ri_in": c(np.asarray(L0_ffn_ri_in).reshape(KH, P).T),
        "ri_mid": c(np.asarray(L0_ffn_ri_mid)[:I_DIM // P * P].reshape(-1, P).T),
        "ri_tail": c(np.asarray(L0_ffn_ri_mid)[I_DIM // P * P:].reshape(-1, 1)),
        "wqkvT": c(np.concatenate([np.asarray(L1_cond_Wq), np.asarray(L1_cond_Wk),
                                   np.asarray(L1_cond_Wv)]).T),
        "woT": c(np.asarray(L1_cond_Wo).T),
        "qw": c(L1_cond_q_norm_w), "kw": c(L1_cond_k_norm_w),
        "kcacheT": c(np.asarray(L1_cond_k_cache).transpose(0, 3, 2, 1).reshape(PAGES * D, HK * PSIZE)),
        "vcache": c(L1_cond_v_cache).reshape(PAGES * PSIZE, HK * D),
        "linT": c(np.asarray(L1_ffn_W).T), "lb": c(L1_ffn_b), "AlT": c(np.asarray(L1_ffn_A).T),
        "BlT": c(np.asarray(L1_ffn_B).T), "gateT": c(np.asarray(L1_ffn_gate_w).T),
        "gate_b": c(L1_ffn_gate_b),
        "ident": np.eye(P, dtype=np.float32),
        "mine": (p[:, None] // RANK == np.arange(2 * P)[None, :] // S).astype(np.float32),
        "eight": (p[:, None] // RANK == np.arange(8)[None, :]).astype(np.float32),
        "rank_of": (p[:, None] % RANK).astype(np.float32),
        "part": p[:, None].astype(np.float32),
        "in_req": (p[:, None] % S).astype(np.float32),
        "key": np.arange(LC, dtype=np.float32),
        "invf": (1.0 / np.float32(10000.0) ** (np.arange(0, D, 2, dtype=np.float32) / np.float32(D))
                 ).astype(np.float32),
    }


def kernel(**inputs):
    import concourse.bacc as _bacc
    from concourse import mybir as _mybir
    from concourse.bass_utils import run_bass_kernel_spmd as _run

    nc = _bacc.Bacc("TRN2", target_bir_lowering=False, num_devices=1)
    arrays = layout(**inputs)
    I = {n: nc.dram_tensor(n + "_in", a.shape, _mybir.dt.from_np(a.dtype), kind="ExternalInput").ap()
         for n, a in arrays.items()}
    for n, shape in (("a_scratch", (IDS * RANK, H)), ("w_scratch", (2 * I_DIM, H)),
                     ("x1_scratch", (TOK, H)), ("q_scratch", (TOK, HQ * D)),
                     ("k_scratch", (TOK, HK * D)), ("v_scratch", (TOK, HK * D))):
        I[n] = nc.dram_tensor(n, shape, F32).ap()
    I["k_rows"] = nc.dram_tensor("k_rows_scratch", (P, B * NPP), U32).ap()
    I["v_rows"] = nc.dram_tensor("v_rows_scratch", (P, B * KC), U32).ap()
    I["out"] = nc.dram_tensor("out", (TOK, H), F32, kind="ExternalOutput").ap()
    build(nc, I)
    r = _run(nc, [{n + "_in": a for n, a in arrays.items()}], core_ids=[0])
    return r.results[0]["out"].reshape(B, S, H)
```
